# Optimizing a Trainium2 kernel written in Bass

```python
import numpy as np
import jax
import jax.numpy as jnp

def _softmax(x, axis=-1):
    return jax.nn.softmax(x, axis=axis)

def _gelu(x):
    return jax.nn.gelu(x, approximate=True)

def _silu(x):
    return jax.nn.silu(x)

def _sigmoid(x):
    return jax.nn.sigmoid(x)

def _layernorm(x, axis=-1, eps=1e-05):
    m = jnp.mean(x, axis=axis, keepdims=True)
    v = jnp.var(x, axis=axis, keepdims=True)
    return (x - m) / jnp.sqrt(v + eps)

def _scatter_add(tgt, idx, src, axis=0):
    return tgt.at[idx].add(src)

def _segment_sum(src, seg, n):
    return jax.ops.segment_sum(src, seg, n)
kernel_name = 'mk_perceiver_d1_seqx_r8_a34401'

def setup_inputs(seed: int=0):
    np.random.seed(seed)
    _w = jnp.asarray

    def _rec_inputs():
        import jax
        import jax.numpy as jnp
        _rk = jax.random.key(seed)
        x = -0.0002928 + 1 * jax.random.normal(jax.random.fold_in(_rk, 1), (32, 64, 128), jnp.float32)
        _lenS = 64 - jax.random.randint(jax.random.fold_in(_rk, 7), (32,), 0, max(1, 64 // 4) + 1, jnp.int32)
        _lenS2 = 1601 - jax.random.randint(jax.random.fold_in(_rk, 8), (32,), 0, max(1, 1601 // 4) + 1, jnp.int32)
        _ctx_1024P = jax.random.normal(jax.random.fold_in(_rk, 11), (32, 16, 128), jnp.float32)
        _ctx_1024c = jax.random.dirichlet(jax.random.fold_in(_rk, 511), 0.3 * jnp.ones((16,), jnp.float32), (32, 1601))
        _ctx_1024t = jnp.einsum('bsk,bkd->bsd', _ctx_1024c, _ctx_1024P)
        _ctx_1024t = _ctx_1024t * jax.lax.rsqrt(jnp.mean(jnp.square(_ctx_1024t)) + 1e-12) * 0.953939
        ctx_1024 = -1.39393e-06 + 0.999914 * (_ctx_1024t + 0.3 * jax.random.normal(jax.random.fold_in(_rk, 611), (32, 1601, 128), jnp.float32))
        _validS = jnp.arange(64)[None, :] < _lenS[:, None]
        _validS2 = jnp.arange(1601)[None, :] < _lenS2[:, None]
        _causal = jnp.tril(jnp.ones((64, 64), dtype=bool))
        mask_BxSxS2_bf1 = jnp.ones((32, 64, 1601), dtype=bool)
        return (x, ctx_1024, mask_BxSxS2_bf1)
    x, ctx_1024, mask_BxSxS2_bf1 = _rec_inputs()

    def _L0_xattn_setup():
        import jax, jax.numpy as jnp
        import numpy as np
        import math
        B, S, D, H = (2, 256, 128, 16)
        DH = D // H

        def _split_heads(x):
            b, s, _ = x.shape
            return x.reshape(b, s, H, DH).transpose(0, 2, 1, 3)
        key = jax.random.key(seed)
        ks = jax.random.split(key, 8)
        scale = 0.02
        inp = {'query': jax.random.normal(ks[0], (B, S, D), dtype=jnp.float32), 'key': jax.random.normal(ks[1], (B, S, D), dtype=jnp.float32), 'value': jax.random.normal(ks[2], (B, S, D), dtype=jnp.float32), 'mask': jnp.ones((B, S, S), dtype=bool), 'Wq': jax.random.normal(ks[3], (D, D), dtype=jnp.float32) * scale, 'bq': jnp.zeros((D,), dtype=jnp.float32), 'Wk': jax.random.normal(ks[4], (D, D), dtype=jnp.float32) * scale, 'bk': jnp.zeros((D,), dtype=jnp.float32), 'Wv': jax.random.normal(ks[5], (D, D), dtype=jnp.float32) * scale, 'bv': jnp.zeros((D,), dtype=jnp.float32), 'Wo': jax.random.normal(ks[6], (D, D), dtype=jnp.float32) * scale, 'bo': jnp.zeros((D,), dtype=jnp.float32)}
        return inp
    _L0_xattn_all = _L0_xattn_setup()
    _L0_xattn_in = {k: v for k, v in _L0_xattn_all.items() if k in ('Wq', 'bq', 'Wk', 'bk', 'Wv', 'bv', 'Wo', 'bo')}
    del _L0_xattn_all

    def _L0_attn_setup():
        import jax, jax.numpy as jnp
        import numpy as np
        B, N, C, H, K = (4, 512, 128, 16, 2)
        D = C // H

        def _kernel(x):
            return jax.nn.silu(x) + 0.5
        key = jax.random.key(seed)
        ks = jax.random.split(key, 8)
        s = 0.02
        x = jax.random.normal(ks[0], (B, N, C), jnp.float32)
        Wq = jax.random.normal(ks[1], (C, C), jnp.float32) * s
        bq = jnp.zeros((C,), jnp.float32)
        Wk = jax.random.normal(ks[2], (K, C, C), jnp.float32) * s
        bk = jnp.zeros((K, C), jnp.float32)
        Wv = jax.random.normal(ks[3], (K, C, C), jnp.float32) * s
        bv = jnp.zeros((K, C), jnp.float32)
        Wo = jax.random.normal(ks[4], (C, C), jnp.float32) * s
        bo = jnp.zeros((C,), jnp.float32)
        ln_g = jnp.ones((C,), jnp.float32)
        ln_b = jnp.zeros((C,), jnp.float32)
        return dict(x=x, Wq=Wq, bq=bq, Wk=Wk, bk=bk, Wv=Wv, bv=bv, Wo=Wo, bo=bo, ln_g=ln_g, ln_b=ln_b)
    _L0_attn_all = _L0_attn_setup()
    _L0_attn_in = {k: v for k, v in _L0_attn_all.items() if k in ('Wq', 'bq', 'Wk', 'bk', 'Wv', 'bv', 'Wo', 'bo', 'ln_g', 'ln_b')}
    del _L0_attn_all

    def _L0_ffn_setup():
        import jax, jax.numpy as jnp
        import numpy as np
        B, S, H, E, K, I = (4, 256, 128, 8, 2, 512)
        GATE_EPS = 1e-06
        LN_EPS = 1e-05
        key = jax.random.key(seed)
        k0, k1, k2, k3 = jax.random.split(key, 4)
        x = jax.random.normal(k0, (B, S, H), jnp.float32)
        gate_w = jax.random.normal(k1, (E, H), jnp.float32) * np.float32(np.sqrt(2.0 / (H + E)))
        expert_bias = jnp.zeros((E,), jnp.float32)
        w_up = jax.random.normal(k2, (E, I, H), jnp.float32) * np.float32(np.sqrt(2.0 / (H + I)))
        w_down = jax.random.normal(k3, (E, H, I), jnp.float32) * np.float32(np.sqrt(2.0 / (H + I)))
        return {'x': x, 'gate_w': gate_w, 'expert_bias': expert_bias, 'w_up': w_up, 'w_down': w_down}
    _L0_ffn_all = _L0_ffn_setup()
    _L0_ffn_in = {k: v for k, v in _L0_ffn_all.items() if k in ('gate_w', 'expert_bias', 'w_up', 'w_down')}
    del _L0_ffn_all
    return {'x': x, 'ctx_1024': ctx_1024, 'mask_BxSxS2_bf1': mask_BxSxS2_bf1, 'L0_xattn_Wq': _L0_xattn_in['Wq'], 'L0_xattn_bq': _L0_xattn_in['bq'], 'L0_xattn_Wk': _L0_xattn_in['Wk'], 'L0_xattn_bk': _L0_xattn_in['bk'], 'L0_xattn_Wv': _L0_xattn_in['Wv'], 'L0_xattn_bv': _L0_xattn_in['bv'], 'L0_xattn_Wo': _L0_xattn_in['Wo'], 'L0_xattn_bo': _L0_xattn_in['bo'], 'L0_attn_Wq': _L0_attn_in['Wq'], 'L0_attn_bq': _L0_attn_in['bq'], 'L0_attn_Wk': _L0_attn_in['Wk'], 'L0_attn_bk': _L0_attn_in['bk'], 'L0_attn_Wv': _L0_attn_in['Wv'], 'L0_attn_bv': _L0_attn_in['bv'], 'L0_attn_Wo': _L0_attn_in['Wo'], 'L0_attn_bo': _L0_attn_in['bo'], 'L0_attn_ln_g': _L0_attn_in['ln_g'], 'L0_attn_ln_b': _L0_attn_in['ln_b'], 'L0_ffn_gate_w': _L0_ffn_in['gate_w'], 'L0_ffn_expert_bias': _L0_ffn_in['expert_bias'], 'L0_ffn_w_up': _L0_ffn_in['w_up'], 'L0_ffn_w_down': _L0_ffn_in['w_down']}

def reference(x, ctx_1024, mask_BxSxS2_bf1, L0_xattn_Wq, L0_xattn_bq, L0_xattn_Wk, L0_xattn_bk, L0_xattn_Wv, L0_xattn_bv, L0_xattn_Wo, L0_xattn_bo, L0_attn_Wq, L0_attn_bq, L0_attn_Wk, L0_attn_bk, L0_attn_Wv, L0_attn_bv, L0_attn_Wo, L0_attn_bo, L0_attn_ln_g, L0_attn_ln_b, L0_ffn_gate_w, L0_ffn_expert_bias, L0_ffn_w_up, L0_ffn_w_down):
    import jax
    import jax.numpy as jnp

    def _L0_xattn_ref(query, key, value, mask, Wq, bq, Wk, bk, Wv, bv, Wo, bo):
        import jax, jax.numpy as jnp
        import numpy as np
        import math
        B, S, D, H = (2, 256, 128, 16)
        DH = D // H

        def _split_heads(x):
            b, s, _ = x.shape
            return x.reshape(b, s, H, DH).transpose(0, 2, 1, 3)
        q = _split_heads(query @ Wq.T + bq)
        k = _split_heads(key @ Wk.T + bk)
        v = _split_heads(value @ Wv.T + bv)
        scores = jnp.einsum('bhqd,bhkd->bhqk', q, k) / math.sqrt(DH)
        scores = jnp.where(mask[:, None, :, :], scores, jnp.float32(1e-09))
        attn = jax.nn.softmax(scores, axis=-1)
        x = jnp.einsum('bhqk,bhkd->bhqd', attn, v)
        x = x.transpose(0, 2, 1, 3).reshape(query.shape[0], -1, H * DH)
        return x @ Wo.T + bo

    def _L0_attn_ref(x, Wq, bq, Wk, bk, Wv, bv, Wo, bo, ln_g, ln_b):
        import jax, jax.numpy as jnp
        import numpy as np
        B, N, C, H, K = (4, 512, 128, 16, 2)
        D = C // H

        def _kernel(x):
            return jax.nn.silu(x) + 0.5
        dtype = x.dtype
        Bn, Nn, Cn = x.shape
        q = x + x @ Wq.T + bq
        ks = x[None] + jnp.einsum('bnc,kdc->kbnd', x, Wk) + bk[:, None, None, :]
        vs = x[None] + jnp.einsum('bnc,kdc->kbnd', x, Wv) + bv[:, None, None, :]
        q = q.reshape(Bn, Nn, H, D).transpose(0, 2, 1, 3)
        ks = ks.reshape(K, Bn, Nn, H, D).transpose(0, 1, 3, 2, 4)
        vs = vs.reshape(K, Bn, Nn, H, D).transpose(0, 1, 3, 2, 4)
        q = _kernel(q)
        ks = _kernel(ks)
        q = q / (jnp.linalg.norm(q, axis=-1, keepdims=True) + 1e-06)
        ks = ks / (jnp.linalg.norm(ks, axis=-1, keepdims=True) + 1e-06)
        scale = Nn ** (-0.5)
        ks = ks.astype(jnp.float32) * scale
        vs = vs.astype(jnp.float32) * scale
        states = jnp.einsum('kbhnd,kbhne->kbhde', ks, vs)
        state = jnp.prod(states, axis=0)
        out = jnp.einsum('bhnd,bhde->bhne', q.astype(jnp.float32), state)
        out = out.astype(dtype)
        out = out.transpose(0, 2, 1, 3).reshape(Bn, Nn, Cn)
        mu = out.mean(axis=-1, keepdims=True)
        var = out.var(axis=-1, keepdims=True)
        out = (out - mu) * jax.lax.rsqrt(var + 1e-05) * ln_g + ln_b
        out = out @ Wo.T + bo
        return out

    def _L0_ffn_ref(x, gate_w, expert_bias, w_up, w_down):
        import jax, jax.numpy as jnp
        import numpy as np
        B, S, H, E, K, I = (4, 256, 128, 8, 2, 512)
        GATE_EPS = 1e-06
        LN_EPS = 1e-05
        logits = jnp.einsum('bsh,eh->bse', x, gate_w) + expert_bias
        weights = jax.nn.softmax(logits, axis=-1)
        top_w, top_i = jax.lax.top_k(weights, K)
        top_w = top_w / (jnp.sum(top_w, axis=-1, keepdims=True) + GATE_EPS)
        sparse_w = jnp.sum(jax.nn.one_hot(top_i, E, dtype=weights.dtype) * top_w[..., None], axis=-2)
        out = jnp.zeros_like(x)
        for e in range(E):
            h = jax.nn.gelu(jnp.einsum('bsh,ih->bsi', x, w_up[e]), approximate=False)
            y = jnp.einsum('bsi,hi->bsh', h, w_down[e])
            out = out + sparse_w[..., e:e + 1] * y
        mu = jnp.mean(out, axis=-1, keepdims=True)
        var = jnp.mean(jnp.square(out - mu), axis=-1, keepdims=True)
        out = (out - mu) * jax.lax.rsqrt(var + LN_EPS)
        return out + x
    x = x + _L0_xattn_ref(_layernorm(x, axis=-1), ctx_1024, ctx_1024, mask_BxSxS2_bf1, L0_xattn_Wq, L0_xattn_bq, L0_xattn_Wk, L0_xattn_bk, L0_xattn_Wv, L0_xattn_bv, L0_xattn_Wo, L0_xattn_bo)
    x = x + _L0_attn_ref(_layernorm(x, axis=-1), L0_attn_Wq, L0_attn_bq, L0_attn_Wk, L0_attn_bk, L0_attn_Wv, L0_attn_bv, L0_attn_Wo, L0_attn_bo, L0_attn_ln_g, L0_attn_ln_b)
    x = x + _L0_ffn_ref(_layernorm(x, axis=-1), L0_ffn_gate_w, L0_ffn_expert_bias, L0_ffn_w_up, L0_ffn_w_down)
    return x

_drawn_inputs = setup_inputs


def setup_inputs(seed=0):
    import zlib

    import numpy as np

    out = dict(_drawn_inputs(seed))
    spreads = {'L0_xattn_bq': (0.0, 0.8),
     'L0_xattn_bk': (0.0, 0.8),
     'L0_xattn_bv': (0.0, 0.1),
     'L0_xattn_bo': (0.0, 0.1),
     'L0_attn_bq': (0.0, 0.1),
     'L0_attn_bk': (0.0, 0.1),
     'L0_attn_bv': (0.0, 0.1),
     'L0_attn_bo': (0.0, 0.1),
     'L0_attn_ln_g': (1.0, 0.2),
     'L0_attn_ln_b': (0.0, 0.1),
     'L0_ffn_expert_bias': (0.0, 0.1)}
    factors = {'L0_xattn_Wq': 8.0, 'L0_xattn_Wk': 7.211}
    for name, (base, spread) in spreads.items():
        noise = np.random.default_rng([zlib.crc32(name.encode()), seed]).standard_normal(out[name].shape)
        drawn = base * np.exp(spread * noise) if base else spread * noise
        out[name] = jnp.asarray(drawn.astype(out[name].dtype))
    for name, factor in factors.items():
        out[name] = (out[name] * factor).astype(out[name].dtype)
    return out
```

```python
from contextlib import ExitStack

import concourse.bass as bass
from concourse import mybir

F32 = mybir.dt.float32
BF16 = mybir.dt.bfloat16
U8 = mybir.dt.uint8
U16 = mybir.dt.uint16
I32 = mybir.dt.int32
ALU = mybir.AluOpType
ACT = mybir.ActivationFunctionType
AX = mybir.AxisListType

P = 128
NB, SQ, SK, D = 32, 64, 1601, 128
NH = 16
DH = D // NH
NPAIR = NH // 2
TOK = NB * SQ
NT = TOK // P
KT = (SK + P - 1) // P
KLAST = SK - (KT - 1) * P
NSLOT = 6
AROWS = NSLOT * DH
ROWS = 2 * AROWS
MROWS = 3
CH = [(0, 401), (401, 801), (801, 1201), (1201, 1601)]
MW = 401
NCH = 4
VG = [(0, 4), (4, 8), (8, 12), (12, 13)]
E, I = 8, 512
IC = I // P
EPS = 1e-5
PV_W = 32
ONE_COL = 2 * DH

LATE_WEIGHTS = [
    ("x_bv", [P, 1], False), ("x_wo", [P, D], False), ("x_bo", [P, D], True),
    ("w5", [P, 5 * D], False), ("b5", [P, 5 * D], True), ("blocks", [P, D], False),
    ("ln_g", [P, 1], False), ("ln_b", [P, 1], False), ("a_wo", [P, D], False), ("a_bo", [P, D], True),
    ("gate", [P, E], False), ("ebias", [P, E], True), ("before", [P, E * E], True)]
LATE = 16 * len(LATE_WEIGHTS)


def keys_of(t):
    return P if t < KT - 1 else KLAST


def query_phase(nc, ctx_args, sb_keep):
    (x_d, mask_d, ident_d, wq_d, bq_d) = ctx_args
    (x_sb, q_scr, flag_i, ident, ident_b, ones_f) = sb_keep
    with ExitStack() as ctx:
        sb = lambda n, s, d: ctx.enter_context(nc.sbuf_tensor(n, s, d))
        sem = lambda n: ctx.enter_context(nc.semaphore(n))
        n16 = NB * SQ * SK // P // 2
        half = n16 // 2
        mask_sb = sb("mask_sb", [P, n16], U16)
        sink = sb("mask_sink", [P, n16 - half], BF16)
        wq = sb("wq", [P, D], F32)
        bq = sb("bq", [P, 1], F32)
        bqs = sb("bqs", [P, 1], F32)
        stats = sb("stats", [P, NT, 6], F32)
        mv = sb("mv", [P, NT, 2], F32)
        eps_t = sb("eps_t", [P, NT], F32)
        expo = sb("expo", [P, NT], F32)
        rstd = sb("rstd", [P, NT], F32)
        xn = sb("xn", [P, NT, D], F32)
        xnT = sb("xnT", [P, TOK], F32)
        qf = sb("qf", [P, TOK], F32)
        rest = sb("rest", [P, TOK], F32)
        q_parts = sb("q_parts", [P, 3, TOK], BF16)
        fmin = sb("fmin", [P, 1], F32)
        fsum = sb("fsum", [P, 1], F32)
        ok_a = sb("ok_a", [P, 1], F32)
        ok = sb("ok", [P, 1], F32)
        ps_t = [ctx.enter_context(nc.psum_tensor(f"ps_t{i}", [P, 512], F32)) for i in range(2)]
        ps_q = [ctx.enter_context(nc.psum_tensor(f"ps_q{i}", [P, 512], F32)) for i in range(2)]
        ps_f = ctx.enter_context(nc.psum_tensor("ps_f", [P, 512], F32))
        x_in, w_in, mask_in = sem("x_in"), sem("w_in"), sem("mask_in")
        stat_done, var_done, rstd_done, xn_done = sem("stat_done"), sem("var_done"), sem("rstd_done"), sem("xn_done")
        tr_done, tr_evac, q_done, q_evac, split = sem("tr_done"), sem("tr_evac"), sem("q_done"), sem("q_evac"), sem("split")
        fmin_done, fsum_done, ok_done, okm_done, flag_done, cst = (
            sem("fmin_done"), sem("fsum_done"), sem("ok_done"), sem("okm_done"), sem("flag_done"), sem("cst"))
        q_stored = sem("q_stored")
        bqs_done, identb_done = sem("bqs_done"), sem("identb_done")
        block = ctx.enter_context(nc.Block())

        @block.sync
        def _(sp):
            sp.dma_start(x_sb[:, :, :], x_d.rearrange("(t p) d -> p t d", p=P)).then_inc(x_in, 16)
            sp.dma_start(ident[:, :], ident_d).then_inc(w_in, 16)
            sp.dma_start(wq[:, :], wq_d).then_inc(w_in, 16)
            sp.dma_start(bq[:, :], bq_d.rearrange("(p a) -> p a", a=1)).then_inc(w_in, 16)
            sp.dma_start(mask_sb[:, :].bitcast(U8),
                         mask_d.rearrange("b q k -> (b q k)").rearrange("(p n) -> p n", p=P)).then_inc(mask_in, 16)
            sp.wait_ge(split, 16)
            for s, part in enumerate((0, 0, 0, 1, 1, 2)):
                for a in range(2):
                    sp.dma_start(q_scr[a, s].rearrange("r p n -> (r p) n"),
                                 q_parts[64 * a:64 * a + 64, part, :]).then_inc(q_stored, 16)
            sp.wait_ge(q_stored, 2 * NSLOT * 16)

        @block.gpsimd
        def _(pool):
            pool.memset(ones_f[:, :], 1.0).then_inc(cst, 1)
            pool.memset(eps_t[:, :], EPS).then_inc(cst, 1)
            pool.memset(expo[:, :], -0.5).then_inc(cst, 1)
            pool.wait_ge(cst, 3)
            pool.wait_ge(var_done, NT)
            nc.gpsimd.tensor_tensor(rstd[:, :], mv[:, :, 1], eps_t[:, :], ALU.add).then_inc(cst, 1)
            pool.wait_ge(cst, 4)
            nc.gpsimd.tensor_tensor(rstd[:, :], rstd[:, :], expo[:, :], ALU.pow).then_inc(rstd_done, 1)

        @block.vector
        def _(dve):
            dve.wait_ge(x_in, 16)
            for t in range(NT):
                nc.vector.bn_stats(stats[:, t, :], x_sb[:, t, :]).then_inc(stat_done, 1)
            for t in range(NT):
                dve.wait_ge(stat_done, t + 1)
                nc.vector.bn_aggr(mv[:, t, :], stats[:, t, :]).then_inc(var_done, 1)
            dve.wait_ge(w_in, 48)
            nc.vector.tensor_scalar(bqs[:, :], bq[:, :], DH ** -0.5, None, ALU.mult).then_inc(bqs_done, 1)
            nc.vector.tensor_copy(ident_b[:, :], ident[:, :]).then_inc(identb_done, 1)
            dve.wait_ge(rstd_done, 1)
            for t in range(NT):
                nc.vector.tensor_scalar(xn[:, t, :], x_sb[:, t, :], mv[:, t, 0:1], rstd[:, t:t + 1],
                                        ALU.subtract, ALU.mult).then_inc(xn_done, 1)
            dve.wait_ge(mask_in, 16)
            nc.vector.tensor_reduce(fmin[:, :], mask_sb[:, 0:half], AX.X, ALU.min).then_inc(fmin_done, 1)
            for g in range(4):
                s = slice(512 * g, 512 * g + 512)
                dve.wait_ge(q_evac, g + 1)
                nc.vector.tensor_copy(q_parts[:, 0, s], qf[:, s]).then_inc(split, 1)
                dve.wait_ge(split, 4 * g + 1)
                nc.vector.tensor_tensor(rest[:, s], qf[:, s], q_parts[:, 0, s], ALU.subtract).then_inc(split, 1)
                dve.wait_ge(split, 4 * g + 2)
                nc.vector.tensor_copy(q_parts[:, 1, s], rest[:, s]).then_inc(split, 1)
                dve.wait_ge(split, 4 * g + 3)
                nc.vector.tensor_tensor(q_parts[:, 2, s], rest[:, s], q_parts[:, 1, s], ALU.subtract).then_inc(split, 1)
            dve.wait_ge(fmin_done, 1)
            dve.wait_ge(fsum_done, 1)
            nc.vector.tensor_scalar(ok_a[:, :], fmin[:, :], 257.0, None, ALU.is_equal).then_inc(ok_done, 1)
            dve.wait_ge(ok_done, 1)
            nc.vector.scalar_tensor_tensor(out=ok[:, :], in0=fsum[:, :], scalar=257.0 * (n16 - half), in1=ok_a[:, :],
                                           op0=ALU.is_equal, op1=ALU.mult).then_inc(ok_done, 1)
            dve.wait_ge(okm_done, 1)
            nc.vector.tensor_scalar(flag_i[:, :], ps_f[0:1, 0:1], float(P), None, ALU.is_equal).then_inc(flag_done, 1)

        @block.scalar
        def _(act):
            for g in range(4):
                act.wait_ge(tr_done, g + 1)
                nc.scalar.activation(xnT[:, 512 * g:512 * g + 512], ps_t[g % 2][:, :], ACT.Copy).then_inc(tr_evac, 1)
            act.wait_ge(bqs_done, 1)
            for g in range(4):
                act.wait_ge(q_done, g + 1)
                nc.scalar.activation(qf[:, 512 * g:512 * g + 512], ps_q[g % 2][:, :], ACT.Identity,
                                     bias=bqs[:, 0:1], scale=DH ** -0.5).then_inc(q_evac, 1)
            act.wait_ge(mask_in, 16)
            nc.scalar.activation(sink[:, :], mask_sb[:, half:n16], ACT.Copy, accum_out=fsum[:, :]).then_inc(fsum_done, 1)

        @block.tensor
        def _(pe):
            pe.wait_ge(w_in, 48)
            for g in range(4):
                pe.wait_ge(xn_done, 4 * g + 4)
                if g >= 2:
                    pe.wait_ge(tr_evac, g - 1)
                for j in range(4):
                    last = nc.tensor.transpose(ps_t[g % 2][:, j * P:(j + 1) * P], xn[:, 4 * g + j, :], ident[:, :])
                last.then_inc(tr_done, 1)
            for g in range(4):
                pe.wait_ge(tr_evac, g + 1)
                if g >= 2:
                    pe.wait_ge(q_evac, g - 1)
                nc.tensor.matmul(ps_q[g % 2][:, :], wq[:, :], xnT[:, 512 * g:512 * g + 512],
                                 start=True, stop=True).then_inc(q_done, 1)
            pe.wait_ge(ok_done, 2)
            pe.wait_ge(cst, 1)
            nc.tensor.matmul(ps_f[0:1, 0:1], ok[:, :], ones_f[:, 0:1], start=True, stop=True).then_inc(okm_done, 1)


def cross_attention(nc, args, keep, drams, w, late_in):
    (ctx_d, mask_d, maskT_d, wk_d, bk_d, wv_d) = args
    (q_scr, k_scr, flag_i, ident, ident_b, ones_f, att) = keep
    with ExitStack() as ctx:
        sb = lambda n, s, d: ctx.enter_context(nc.sbuf_tensor(n, s, d))
        psb = lambda n: ctx.enter_context(nc.psum_tensor(n, [P, 512], F32))
        sem = lambda n: ctx.enter_context(nc.semaphore(n))
        wk, wv, bk = sb("wk", [P, D], F32), sb("wv", [P, D], F32), sb("bk", [P, 1], F32)
        ctxT = [sb(f"ctxT{i}", [P, SK], F32) for i in range(2)]
        kf = [sb(f"kf{i}", [P, MW], F32) for i in range(2)]
        krest = [sb(f"krest{i}", [P, MW], F32) for i in range(2)]
        kparts = sb("kparts", [P, 3, SK], BF16)
        kst = [sb(f"kst{i}", [P, NPAIR, SK], BF16) for i in range(2)]
        qmax = [sb(f"qmax{i}", [P, NPAIR * P], BF16) for i in range(2)]
        qsc = [sb(f"qsc{i}", [P, NPAIR * P], BF16) for i in range(2)]
        v = [sb(f"v{i}", [P, KT, NPAIR, PV_W], F32) for i in range(2)]
        probs = [sb(f"probs{i}", [P, NPAIR * P], F32) for i in range(2)]
        mx2 = sb("mx2", [P, 2, NPAIR], F32)
        mx = sb("mx", [P, NPAIR], F32)
        mrest = sb("mrest", [P, NPAIR], F32)
        mparts = sb("mparts", [P, NPAIR, MROWS], BF16)
        oT = sb("oT", [P, 2 * P], F32)
        rec = sb("rec", [P, NPAIR], F32)
        mask_q = sb("mask_q", [P, SK], U8)
        mask_k = sb("mask_k", [P, KT, SQ], U8)
        picked = sb("picked", [P, 2, MW], F32)
        fill = sb("fill", [P, NPAIR * P], F32)
        tiny, held = sb("tiny", [P, 1], F32), sb("held", [P, 1], F32)
        arg = sb("arg", [P, NPAIR * P], F32)
        score = [psb(f"score{i}") for i in range(2)]
        maxps = [ctx.enter_context(nc.psum_tensor(f"maxps{i}", [P, 2, 512], F32)) for i in range(2)]
        pvps, misc = psb("pvps"), psb("misc")

        w_in = sem("w_in1")
        ctx_in = [sem("ctx_in0"), sem("ctx_in1")]
        cst = sem("cst1")
        k_done, k_evac, k_split, k_chain = sem("k_done"), sem("k_evac"), sem("k_split"), sem("k_chain")
        v_done, v_evac = sem("v_done"), sem("v_evac")
        k_scr_in = [sem("k_scr_in0"), sem("k_scr_in1")]
        kst_in = [sem("kst_in0"), sem("kst_in1")]
        qmax_in, qsc_in = sem("qmax_in"), sem("qsc_in")
        max_ready, max_red, m_chain, m_parts = sem("max_ready"), sem("max_red"), sem("m_chain"), sem("m_parts")
        mrow_done, mrow_evac = sem("mrow_done"), sem("mrow_evac")
        score_ready, exp_done, pv_done = sem("score_ready"), sem("exp_done"), sem("pv_done")
        mask_in, mask_kin = sem("mask_in1"), sem("mask_kin")
        pick_fill, pick_done, fill_done, fill_evac, arg_fill, arg_done = (
            sem("pick_fill"), sem("pick_done"), sem("fill_done"), sem("fill_evac"), sem("arg_fill"), sem("arg_done"))
        oT_copied, oT_back, rec_done, att_done = sem("oT_copied"), sem("oT_back"), sem("rec_done"), sem("att_done")

        MAX_STEPS = {0: [0], 1: [1], 2: [2, 3], 3: [4], 4: [5, 6], 5: [7], 6: [8, 9], 7: [10, 11], 8: [12, 13],
                     9: [14, 15]}
        MISC = {0: ("v", 1, 2), 1: ("v", 1, 3), 2: ("o", -1, 0), 3: ("k", 2, 0), 4: ("k", 2, 1), 5: ("v", 2, 0),
                6: ("k", 2, 2), 7: ("k", 2, 3), 9: ("v", 2, 1), 11: ("m", 1, 0), 12: ("m", 1, 1)}

        def wanted(kind, stage, i_known):
            return i_known is None or 0 <= i_known + stage < NB

        def evacuated(eng, kind, b, n):
            if kind == "v":
                eng.wait_ge(v_evac, b * 4 + (n + 1))
            elif kind == "k":
                eng.wait_ge(k_evac, b * 4 + (n + 1))
            elif kind == "m":
                eng.wait_ge(mrow_evac, b * 2 + (n + 1))
            else:
                eng.wait_ge(att_done, b * 2 + 2)

        def previous_use(slot, i_known):
            for s in range(slot - 1, -1, -1):
                if s in MISC and wanted(MISC[s][0], MISC[s][1], i_known):
                    return MISC[s]
            return ("m", 0, 1)

        def iterations(eng, body):
            body(0, 0, 0, 0)
            body(1, 0, 1, 1)
            with eng.Fori(1, NB // 2 - 2) as r:
                body(r * 2, r, 0, None)
                body(r * 2 + 1, r, 1, None)
            for i in range(NB - 4, NB):
                body(i, i // 2, i % 2, i)

        def batches(eng, body):
            body(0, 0, 0, 0)
            body(1, 0, 1, 1)
            with eng.Fori(1, NB // 2) as r:
                body(r * 2, r, 0, None)
                body(r * 2 + 1, r, 1, None)

        def sync_program(sp, all_true):
            def load_ctx(b, half, p):
                sp.dma_start(ctxT[p][:, :], ctx_d[b, :, :]).then_inc(ctx_in[p], 16)

            def load_q(b, p):
                for a in range(2):
                    dst = qmax[p][a * AROWS:(a + 1) * AROWS, :].rearrange("r (p a n) -> r p a n", a=2, n=SQ)[:, :, a, :]
                    src = q_scr[a].rearrange("s r p n -> (s r) p n")[:, :, bass.ds(b * SQ, SQ)]
                    sp.dma_start(dst, src).then_inc(qmax_in, 16)

            def copy_q(p):
                sp.dma_start(qsc[p][0:ROWS, :], qmax[p][0:ROWS, :]).then_inc(qsc_in, 16)

            def stack_k(half, b, p, tiles_used):
                lo, hi = (0, CH[1][1]) if half == 0 else (CH[2][0], SK)
                sp.wait_ge(k_split, b * 4 + (2 * half + 2))
                for a in range(2):
                    if a == 1 and tiles_used is not None:
                        sp.wait_ge(score_ready, tiles_used)
                    sp.dma_start(k_scr[a, :, :, :, lo:hi].rearrange("s r p n -> (r p) s n"),
                                 kparts[64 * a:64 * a + 64, :, lo:hi]).then_inc(k_scr_in[half], 16)
                sp.wait_ge(k_scr_in[half], b * 32 + 32)
                for a in range(2):
                    for row, parts in ((0, 3), (3 * DH, 2), (5 * DH, 1)):
                        src = k_scr[a, 0:parts, :, :, lo:hi].rearrange("s r p n -> (s r) p n")
                        r0 = a * AROWS + row
                        sp.dma_start(kst[p][r0:r0 + parts * DH, :, lo:hi], src).then_inc(kst_in[half], 16)

            sp.dma_start(wk[:, :], wk_d).then_inc(w_in, 16)
            sp.dma_start(bk[:, :], bk_d.rearrange("(p a) -> p a", a=1)).then_inc(w_in, 16)
            sp.dma_start(wv[:, :], wv_d).then_inc(w_in, 16)
            load_ctx(0, 0, 0)
            for name, shape, to_all in LATE_WEIGHTS:
                src = drams[name].to_broadcast([P, shape[1]]) if to_all else drams[name]
                sp.dma_start(w[name][:, :], src).then_inc(late_in, 16)
            sp.wait_ge(cst, 1)
            with sp.If(all_true):
                load_ctx(1, 0, 1)
                load_q(0, 0)
                load_q(1, 1)
                stack_k(0, 0, 0, None)
                stack_k(1, 0, 0, None)
                sp.wait_ge(v_done, 4)
                load_ctx(2, 1, 0)
                sp.wait_ge(qmax_in, 2 * 32)
                copy_q(0)
                stack_k(0, 1, 1, None)
                stack_k(1, 1, 1, None)

                def body(i, r, p, known):
                    if known is None or known + 3 < NB:
                        sp.wait_ge(v_done, (i + 1) * 4 + 4)
                        load_ctx(i + 3, r, 1 - p)
                    if known is None or known + 1 < NB:
                        if known != 0:
                            sp.wait_ge(score_ready, i * (2 * KT))
                        sp.wait_ge(qmax_in, i * 32 + 64)
                        copy_q(1 - p)
                    if known is None or known + 2 < NB:
                        sp.wait_ge(max_ready, i * 16 + 16)
                        sp.wait_ge(qsc_in, i * 16 + 16)
                        load_q(i + 2, p)
                        stack_k(0, i + 2, p, i * (2 * KT) + 14)
                        stack_k(1, i + 2, p, i * (2 * KT) + 2 * KT)

                iterations(sp, body)
            with sp.Else():
                def body(b, r, half, known):
                    if known != 0:
                        sp.wait_ge(v_done, b * 4)
                        load_ctx(b, r, 0)
                        sp.wait_ge(max_red, b * 16)
                        sp.wait_ge(qsc_in, b * 16)
                    load_q(b, 0)
                    for a in range(2):
                        sp.dma_start(mask_q[64 * a:64 * a + 64, :], mask_d[b, :, :]).then_inc(mask_in, 16)
                    if known != 0:
                        sp.wait_ge(arg_done, b * (2 * KT))
                    sp.dma_start(mask_k[:, 0:KT - 1, :], maskT_d[b, 0:(KT - 1) * P, :].rearrange(
                        "(t p) q -> p t q", p=P)).then_inc(mask_kin, 16)
                    sp.dma_start(mask_k[0:KLAST, KT - 1, :], maskT_d[b, (KT - 1) * P:SK, :]).then_inc(mask_kin, 16)
                    if known != 0:
                        sp.wait_ge(score_ready, b * (2 * KT))
                    sp.wait_ge(qmax_in, b * 32 + 32)
                    copy_q(0)
                    stack_k(0, b, 0, None)
                    stack_k(1, b, 0, None)

                batches(sp, body)
            sp.wait_ge(att_done, 2 * NB)

        def split_k(pool, b, j):
            lo, hi = CH[j]
            w = hi - lo
            pool.wait_ge(k_evac, b * 4 + (j + 1))
            nc.gpsimd.tensor_tensor(krest[j % 2][:, 0:w], kf[j % 2][:, 0:w], kparts[:, 0, lo:hi], ALU.subtract)\
                .then_inc(k_chain, 1)
            nc.gpsimd.tensor_tensor(kparts[:, 1, lo:hi], kf[j % 2][:, 0:w], kparts[:, 0, lo:hi], ALU.subtract)\
                .then_inc(k_chain, 1)
            pool.wait_ge(k_chain, b * 8 + (2 * j + 2))
            nc.gpsimd.tensor_tensor(kparts[:, 2, lo:hi], krest[j % 2][:, 0:w], kparts[:, 1, lo:hi], ALU.subtract)\
                .then_inc(k_split, 1)

        def pool_program(pool, all_true):
            with pool.If(all_true):
                for b in (0, 1):
                    for j in range(NCH):
                        split_k(pool, b, j)

                def body(i, r, p, known):
                    if known is None or known + 2 < NB:
                        for j in range(NCH):
                            split_k(pool, i + 2, j)

                iterations(pool, body)
            with pool.Else():
                def body(b, r, half, known):
                    for j in range(NCH):
                        split_k(pool, b, j)

                batches(pool, body)

        def scalar_program(act, all_true):
            def evac_k(b, j, known):
                lo, hi = CH[j]
                w = hi - lo
                act.wait_ge(k_done, b * 4 + (j + 1))
                if not (known is not None and known == 0 and j < 2):
                    act.wait_ge(k_split, b * 4 + (j - 1))
                if j % 2 == 0 and known != 0:
                    act.wait_ge(kst_in[j // 2], b * 96)
                nc.scalar.activation(kf[j % 2][:, 0:w], misc[:, 0:w], ACT.Identity, bias=bk[:, 0:1])
                nc.scalar.activation(kparts[:, 0, lo:hi], misc[:, 0:w], ACT.Identity, bias=bk[:, 0:1])\
                    .then_inc(k_evac, 1)

            def evac_m(b, h, p, known):
                act.wait_ge(mrow_done, b * 2 + (h + 1))
                nc.scalar.activation(qsc[p][ROWS:ROWS + MROWS, h * 512:h * 512 + 512],
                                     misc[ROWS:ROWS + MROWS, :], ACT.Copy).then_inc(mrow_evac, 1)

            act.wait_ge(w_in, 48)
            act.wait_ge(cst, 3)
            with act.If(all_true):
                for j in range(NCH):
                    evac_k(0, j, 0)
                for j in range(NCH):
                    evac_k(1, j, 1)
                evac_m(0, 0, 0, 0)
                evac_m(0, 1, 0, 0)

                def body(i, r, p, known):
                    for t in range(KT):
                        n = keys_of(t)
                        for h in range(2):
                            act.wait_ge(score_ready, i * (2 * KT) + (2 * t + h + 1))
                            if not (known == 0 and t < 2):
                                act.wait_ge(pv_done, i * KT + (t - 1))
                            nc.scalar.activation(probs[(t + p) % 2][0:n, h * 512:h * 512 + 512], score[h][0:n, :],
                                                 ACT.Exp).then_inc(exp_done, 1)
                        if t in MISC and wanted(*MISC[t][0:2], known):
                            kind, stage, num = MISC[t]
                            if kind == "k":
                                evac_k(i + stage, num, None)
                            if kind == "m":
                                evac_m(i + stage, num, 1 - p, None)

                iterations(act, body)
            with act.Else():
                def body(b, r, half, known):
                    for j in range(NCH):
                        evac_k(b, j, known)
                    for h in range(2):
                        evac_m(b, h, 0, known)
                    for h in range(2):
                        act.wait_ge(fill_done, b * 2 + (h + 1))
                        nc.scalar.activation(fill[:, h * 512:h * 512 + 512], misc[:, :], ACT.Identity, bias=tiny[:, 0:1])\
                            .then_inc(fill_evac, 1)
                    for t in range(KT):
                        n = keys_of(t)
                        for h in range(2):
                            act.wait_ge(arg_done, b * (2 * KT) + (2 * t + h + 1))
                            if not (known == 0 and t == 0):
                                act.wait_ge(pv_done, b * KT + t)
                            nc.scalar.activation(probs[t % 2][0:n, h * 512:h * 512 + 512],
                                                 arg[0:n, h * 512:h * 512 + 512], ACT.Exp).then_inc(exp_done, 1)

                batches(act, body)

        def vector_program(dve, all_true):
            def reduce_step(b, s):
                dve.wait_ge(max_ready, b * 16 + (s + 1))
                nc.vector.tensor_reduce(mx2[:, s // 8, s % 8:s % 8 + 1], maxps[s % 2][:, :, 0:MW], AX.XY, ALU.max)\
                    .then_inc(max_red, 1)

            def split_m(b, known):
                dve.wait_ge(max_red, b * 16 + 16)
                nc.vector.tensor_tensor(mx[:, :], mx2[:, 0, :], mx2[:, 1, :], ALU.max).then_inc(m_chain, 1)
                if known != 0:
                    dve.wait_ge(mrow_done, b * 2)
                dve.wait_ge(m_chain, b * 4 + 1)
                nc.vector.tensor_scalar(mparts[:, :, 0], mx[:, :], -1.0, None, ALU.mult).then_inc(m_chain, 1)
                dve.wait_ge(m_chain, b * 4 + 2)
                nc.vector.scalar_tensor_tensor(out=mrest[:, :], in0=mx[:, :], scalar=-1.0, in1=mparts[:, :, 0],
                                               op0=ALU.mult, op1=ALU.subtract).then_inc(m_chain, 1)
                dve.wait_ge(m_chain, b * 4 + 3)
                nc.vector.tensor_copy(mparts[:, :, 1], mrest[:, :]).then_inc(m_chain, 1)
                dve.wait_ge(m_chain, b * 4 + 4)
                nc.vector.tensor_tensor(mparts[:, :, 2], mrest[:, :], mparts[:, :, 1], ALU.subtract)\
                    .then_inc(m_parts, 1)

            def evac_v(b, g, p, used):
                t0, t1 = VG[g]
                n = keys_of(t1 - 1)
                dve.wait_ge(v_done, b * 4 + (g + 1))
                if used is not None:
                    dve.wait_ge(pv_done, used)
                nc.vector.tensor_copy(
                    v[p][0:n, t0:t1, :, 0:2 * DH],
                    misc[0:n, 0:(t1 - t0) * P].rearrange("k (t p c) -> k t p c", p=NPAIR, c=2 * DH))\
                    .then_inc(v_evac, 1)

            def copy_o(b):
                dve.wait_ge(pv_done, b * KT + KT)
                nc.vector.tensor_copy(oT[:, :], pvps[:, 0:2 * P]).then_inc(oT_copied, 1)

            def norm_o(b, r, p):
                back = misc[:, 0:2 * P].rearrange("k (p c) -> k p c", c=PV_W)
                dve.wait_ge(oT_back, b + 1)
                nc.vector.reciprocal(rec[:, :], back[:, :, ONE_COL]).then_inc(rec_done, 1)
                dve.wait_ge(rec_done, b + 1)
                for a in range(2):
                    dst = att[64 * p:64 * p + 64, bass.ds(r * D, D)].rearrange("q (p a d) -> q p a d", a=2, d=DH)
                    nc.vector.tensor_tensor(
                        dst[:, :, a, :], back[64 * a:64 * a + 64, :, a * DH:(a + 1) * DH],
                        rec[64 * a:64 * a + 64, :].unsqueeze(2).to_broadcast([64, NPAIR, DH]),
                        ALU.mult).then_inc(att_done, 1)

            nc.vector.memset(tiny[:, :], 1e-9)
            for p in range(2):
                nc.vector.memset(qmax[p][:, :], 0.0)
            nc.vector.memset(qsc[0][:, :], 0.0).then_inc(cst, 1)
            for p in range(2):
                nc.vector.memset(v[p][:, :, :, :], 0.0)
            nc.vector.memset(kst[0][ROWS:P, :, :], 1.0)
            nc.vector.memset(kst[1][ROWS:P, :, :], 1.0).then_inc(cst, 1)
            dve.wait_ge(cst, 2)
            for p in range(2):
                last = nc.vector.memset(v[p][:, :, :, ONE_COL], 1.0)
            last.then_inc(cst, 1)
            with dve.If(all_true):
                for g in range(4):
                    evac_v(0, g, 0, None)
                for g in range(2):
                    evac_v(1, g, 1, None)
                for s in range(16):
                    reduce_step(0, s)
                split_m(0, 0)

                def body(i, r, p, known):
                    for t in range(KT):
                        if t == 0 and known != 0:
                            copy_o(i - 1)
                        if known is None or known + 1 < NB:
                            for s in MAX_STEPS.get(t, ()):
                                reduce_step(i + 1, s)
                            if t == 10:
                                split_m(i + 1, None)
                        if t in MISC and wanted(*MISC[t][0:2], known):
                            kind, stage, num = MISC[t]
                            if kind == "v":
                                used = None if known is not None and known + stage < 2 else \
                                    (i + (stage - 2)) * KT + VG[num][1]
                                evac_v(i + stage, num, (p + stage) % 2, used)
                            if kind == "o":
                                norm_o(i - 1, r if p == 1 else r - 1, 1 - p)

                iterations(dve, body)
                copy_o(NB - 1)
                norm_o(NB - 1, NB // 2 - 1, 1)
            with dve.Else():
                def body(b, r, half, known):
                    for g in range(4):
                        evac_v(b, g, 0, None if known == 0 else b * KT)
                    dve.wait_ge(mask_in, b * 32 + 32)
                    for s in range(16):
                        if not (known == 0 and s == 0):
                            dve.wait_ge(max_red, b * 16 + s)
                        nc.vector.memset(picked[:, :, :], 1e-9).then_inc(pick_fill, 1)
                        dve.wait_ge(pick_fill, b * 16 + (s + 1))
                        dve.wait_ge(max_ready, b * 16 + (s + 1))
                        nc.vector.tensor_copy(held[:, :], tiny[:, :])
                        for c in range(2):
                            lo = 400 * (2 * (s // 8) + c)
                            last = nc.vector.copy_predicated(picked[:, c, :], mask_q[:, lo:lo + MW],
                                                             maxps[s % 2][:, c, 0:MW])
                        last.then_inc(pick_done, 1)
                        dve.wait_ge(pick_done, b * 16 + (s + 1))
                        nc.vector.tensor_reduce(mx2[:, s // 8, s % 8:s % 8 + 1], picked[:, :, :], AX.XY, ALU.max)\
                            .then_inc(max_red, 1)
                    split_m(b, known)
                    dve.wait_ge(mask_kin, b * 32 + 32)
                    for t in range(KT):
                        n = keys_of(t)
                        for h in range(2):
                            at = lambda a: a[0:n, :].rearrange("k (h q) -> k h q", q=SQ)
                            hs = slice(h * 512, h * 512 + 512)
                            k = 2 * t + h
                            if not (known == 0 and t == 0):
                                dve.wait_ge(exp_done, b * (2 * KT) + (k - 1))
                            dve.wait_ge(fill_evac, b * 2 + (h + 1))
                            nc.vector.tensor_copy(arg[0:n, hs], fill[0:n, hs]).then_inc(arg_fill, 1)
                            dve.wait_ge(arg_fill, b * (2 * KT) + (k + 1))
                            dve.wait_ge(score_ready, b * (2 * KT) + (k + 1))
                            nc.vector.tensor_copy(held[:, :], tiny[:, :])
                            nc.vector.copy_predicated(
                                at(arg[:, hs]), mask_k[0:n, t, :].unsqueeze(1).to_broadcast([n, 8, SQ]),
                                at(score[h])).then_inc(arg_done, 1)
                    copy_o(b)
                    norm_o(b, r, half)

                batches(dve, body)

        def tensor_program(pe, all_true):
            def k_proj(b, rb, j, p):
                lo, hi = CH[j]
                if j == 0:
                    pe.wait_ge(ctx_in[p], rb * 16 + 16)
                nc.tensor.matmul(misc[:, 0:hi - lo], wk[:, :], ctxT[p][:, lo:hi], start=True, stop=True)\
                    .then_inc(k_done, 1)

            def v_proj(b, g, p):
                t0, t1 = VG[g]
                for t in range(t0, t1):
                    n = keys_of(t)
                    last = nc.tensor.matmul(misc[0:n, (t - t0) * P:(t - t0 + 1) * P],
                                            ctxT[p][:, t * P:t * P + n], wv[:, :], start=True, stop=True)
                last.then_inc(v_done, 1)

            def max_step(b, s, p, known):
                pair, half = s % 8, s // 8
                if s == 0:
                    pe.wait_ge(qmax_in, b * 32 + 32)
                if s % 8 == 0:
                    pe.wait_ge(kst_in[half], b * 96 + 96)
                if not (known == 0 and s < 2):
                    pe.wait_ge(max_red, b * 16 + (s - 1))
                for c in range(2):
                    lo = 400 * (2 * half + c)
                    last = nc.tensor.matmul(maxps[s % 2][:, c, 0:MW], qmax[p][0:ROWS, pair * P:(pair + 1) * P],
                                            kst[p][0:ROWS, pair, lo:lo + MW], start=True, stop=True)
                last.then_inc(max_ready, 1)

            def m_rows(b, h):
                pe.wait_ge(m_parts, b + 1)
                for j in range(4):
                    last = nc.tensor.matmul(misc[ROWS:ROWS + MROWS, j * P:(j + 1) * P], mparts[:, 4 * h + j, :],
                                            ident_b[:, :], start=True, stop=True)
                last.then_inc(mrow_done, 1)

            def scores(i, t, p, known):
                n = keys_of(t)
                for h in range(2):
                    if t == 0:
                        pe.wait_ge(mrow_evac, i * 2 + (h + 1))
                        pe.wait_ge(qsc_in, i * 16 + 16)
                    if not (known == 0 and t == 0):
                        pe.wait_ge(exp_done, i * (2 * KT) + (2 * t + h - 1))
                    for j in range(4):
                        pair = 4 * h + j
                        last = nc.tensor.matmul(score[h][0:n, j * P:(j + 1) * P],
                                                kst[p][0:ROWS + MROWS, pair, t * P:t * P + n],
                                                qsc[p][0:ROWS + MROWS, pair * P:(pair + 1) * P],
                                                start=True, stop=True)
                    last.then_inc(score_ready, 1)

            def p_v(i, t, p, known):
                n = keys_of(t)
                for g, (t0, _) in enumerate(VG):
                    if t == t0:
                        pe.wait_ge(v_evac, i * 4 + (g + 1))
                if t == 0 and known != 0:
                    pe.wait_ge(oT_copied, i)
                for pair in range(NPAIR):
                    g, r = pair % 4, pair // 4
                    if pair % 4 == 0:
                        pe.wait_ge(exp_done, i * (2 * KT) + (2 * t + r + 1))
                    last = nc.tensor.matmul(pvps[32 * g:32 * g + PV_W, r * P:(r + 1) * P], v[p][0:n, t, pair, :],
                                            probs[(t + p) % 2][0:n, pair * P:(pair + 1) * P],
                                            start=(t == 0 and r == 0), stop=(t == KT - 1), skip_group_check=True)
                last.then_inc(pv_done, 1)

            def o_back(b):
                pe.wait_ge(oT_copied, b + 1)
                for r in range(2):
                    last = nc.tensor.transpose(misc[:, r * P:(r + 1) * P], oT[:, r * P:(r + 1) * P], ident[:, :])
                last.then_inc(oT_back, 1)

            pe.wait_ge(w_in, 48)
            with pe.If(all_true):
                prev = None
                for b in range(2):
                    for j in range(NCH):
                        if prev:
                            evacuated(pe, *prev)
                        k_proj(b, 0, j, b)
                        prev = ("k", b, j)
                    for g in range(4 if b == 0 else 2):
                        evacuated(pe, *prev)
                        v_proj(b, g, b)
                        prev = ("v", b, g)
                pe.wait_ge(cst, 3)
                for s in range(16):
                    max_step(0, s, 0, 0)
                evacuated(pe, *prev)
                m_rows(0, 0)
                evacuated(pe, "m", 0, 0)
                m_rows(0, 1)

                def body(i, r, p, known):
                    for t in range(KT):
                        scores(i, t, p, known)
                        if t > 0:
                            p_v(i, t - 1, p, known)
                        elif known != 0:
                            p_v(i - 1, KT - 1, 1 - p, None)
                        if known is None or known + 1 < NB:
                            for s in MAX_STEPS.get(t, ()):
                                max_step(i + 1, s, 1 - p, None)
                        if t in MISC and wanted(*MISC[t][0:2], known):
                            kind, stage, num = MISC[t]
                            pk, pst, pn = previous_use(t, known)
                            evacuated(pe, pk, i + pst, pn)
                            if kind == "k":
                                k_proj(i + 2, r + 1, num, p)
                            elif kind == "v":
                                v_proj(i + stage, num, (p + stage) % 2)
                            elif kind == "o":
                                o_back(i - 1)
                            else:
                                m_rows(i + 1, num)

                iterations(pe, body)
                p_v(NB - 1, KT - 1, 1, None)
                o_back(NB - 1)
            with pe.Else():
                def body(b, r, half, known):
                    prev = None if known == 0 else ("o", b - 1, 0)
                    for kind, n in [("k", j) for j in range(NCH)] + [("v", g) for g in range(4)]:
                        if prev:
                            evacuated(pe, *prev)
                        if kind == "k":
                            k_proj(b, b, n, 0)
                        else:
                            v_proj(b, n, 0)
                        prev = (kind, b, n)
                    pe.wait_ge(cst, 3)
                    for s in range(16):
                        max_step(b, s, 0, known)
                    evacuated(pe, *prev)
                    m_rows(b, 0)
                    evacuated(pe, "m", b, 0)
                    m_rows(b, 1)
                    evacuated(pe, "m", b, 1)
                    for h in range(2):
                        if h:
                            pe.wait_ge(fill_evac, b * 2 + 1)
                        nc.tensor.matmul(misc[:, :], kst[0][ROWS:ROWS + MROWS, 0, 0:P],
                                         qsc[0][ROWS:ROWS + MROWS, h * 512:h * 512 + 512],
                                         start=True, stop=True).then_inc(fill_done, 1)
                    for t in range(KT):
                        scores(b, t, 0, known)
                        p_v(b, t, 0, known)
                    pe.wait_ge(fill_evac, b * 2 + 2)
                    o_back(b)

                batches(pe, body)

        block = ctx.enter_context(nc.Block())

        @block.sync
        def _(sp):
            sync_program(sp, sp.value_load(flag_i[0:1, 0:1]) == 1)

        @block.gpsimd
        def _(pool):
            pool_program(pool, pool.value_load(flag_i[0:1, 0:1]) == 1)

        @block.scalar
        def _(act):
            scalar_program(act, act.value_load(flag_i[0:1, 0:1]) == 1)

        @block.vector
        def _(dve):
            vector_program(dve, dve.value_load(flag_i[0:1, 0:1]) == 1)

        @block.tensor
        def _(pe):
            tensor_program(pe, pe.value_load(flag_i[0:1, 0:1]) == 1)


def self_attention(nc, w, keep):
    (x_sb, att, xn3T, ident, late_in) = keep
    NG, GT = 4, 4
    QK, VV = 3 * D, 2 * D
    G8 = QK // DH
    with ExitStack() as ctx:
        sb = lambda n, s: ctx.enter_context(nc.sbuf_tensor(n, s, F32))
        psb = lambda n: ctx.enter_context(nc.psum_tensor(n, [P, 512], F32))
        sem = lambda n: ctx.enter_context(nc.semaphore(n))
        attT, xn1, xnT = sb("attT", [P, TOK]), sb("xn1", [P, NT, D]), sb("xnT1", [P, TOK])
        y, vv = sb("y", [P, NT, QK]), sb("vv", [P, NT, VV])
        th, sq = sb("th", [P, NT, QK]), sb("sq", [P, GT, QK])
        ss, nrm = sb("ss", [P, NT, G8]), sb("nrm", [P, NT, G8])
        halfs = sb("halfs", [P, GT * G8])
        st = sb("st", [P, 2, 2, D])
        state = sb("state", [P, NT, 2, D])
        qT, on, onT = sb("qT", [P, TOK]), sb("on", [P, NT, D]), sb("onT", [P, TOK])
        stats, mv = sb("stats1", [P, 3, NT, 6]), sb("mv1", [P, 3, NT, 2])
        rstd, epsv, minus_half = sb("rstd1", [P, 3, NT]), sb("epsv", [P, GT]), sb("minus_half", [P, GT])
        wsum = sb("wsum", [P, 5 * D])
        psT = [psb(f"psT{i}") for i in range(2)]
        psM = [psb(f"psM{i}") for i in range(2)]
        psQ, psV = psb("psQ"), psb("psV")
        psG = [psb(f"psG{i}") for i in range(2)]
        t_done, t_evac = sem("t_done"), sem("t_evac")
        m_done, m_evac = sem("m_done"), sem("m_evac")
        p_done, y_done, v_done = sem("p_done"), sem("y_done"), sem("vv_done")
        stat_done, var_done, rstd_done = sem("stat1"), sem("var1"), sem("rstd1_done")
        eps_add = sem("eps_add")
        n_done, cst, xb_done, x1b_done, wsum_done = sem("n_done"), sem("cst2"), sem("xb_done"), sem("x1b_done"), sem("wsum_done")
        th_done, w_done, sq_done, ss_done, root_done, nrm_add, inv_done, k_ready = (
            sem("th_done"), sem("w_done"), sem("sq_done"), sem("ss_done"), sem("root_done"), sem("nrm_add"),
            sem("inv_done"), sem("k_ready"))
        g_done, st1, state_done, res_done = sem("g_done"), sem("st1"), sem("state_done"), sem("res_done")
        block = ctx.enter_context(nc.Block())
        g_of = lambda t, b: (psG if t % 2 == 0 else (psQ, psV))[b]
        cols = lambda t: slice(t * P, (t + 1) * P)
        tiles = lambda g: range(GT * g, GT * g + GT)
        grp = lambda g: slice(GT * g, GT * g + GT)

        @block.gpsimd
        def _(pool):
            pool.memset(epsv[:, :], EPS).then_inc(cst, 1)
            pool.memset(minus_half[:, :], -0.5).then_inc(cst, 1)
            pool.memset(halfs[:, :], 0.5).then_inc(cst, 1)
            pool.wait_ge(late_in, LATE)
            for t in range(NT):
                last = nc.gpsimd.tensor_tensor(x_sb[:, t, :], x_sb[:, t, :], w["x_bo"][:, :], ALU.add)
                if t % GT == GT - 1:
                    last.then_inc(xb_done, 1)
            pool.wait_ge(cst, 3)

            def rstds(rnd):
                for g in range(NG):
                    n = rnd * NG + g
                    pool.wait_ge(var_done, (n + 1) * GT)
                    nc.gpsimd.tensor_tensor(rstd[:, rnd, grp(g)], mv[:, rnd, grp(g), 1], epsv[:, :], ALU.add)\
                        .then_inc(eps_add, 1)
                    pool.wait_ge(eps_add, n + 1)
                    nc.gpsimd.tensor_tensor(rstd[:, rnd, grp(g)], rstd[:, rnd, grp(g)], minus_half[:, :], ALU.pow)\
                        .then_inc(rstd_done, 1)

            rstds(0)
            for g in range(NG):
                pool.wait_ge(n_done, g + 1)
                for t in tiles(g):
                    last = nc.gpsimd.tensor_tensor(x_sb[:, t, :], x_sb[:, t, :], w["a_bo"][:, :], ALU.add)
                last.then_inc(x1b_done, 1)
            for g in range(NG):
                pool.wait_ge(ss_done, g + 1)
                flat = nrm[:, grp(g), :].rearrange("p t h -> p (t h)")
                nc.gpsimd.tensor_tensor(flat, ss[:, grp(g), :].rearrange("p t h -> p (t h)"), halfs[:, :], ALU.pow)\
                    .then_inc(root_done, 1)
                pool.wait_ge(root_done, g + 1)
                nc.gpsimd.tensor_scalar(flat, flat, 2e-6, None, ALU.add).then_inc(nrm_add, 1)
            rstds(1)
            rstds(2)
            for g in range(NG):
                pool.wait_ge(n_done, 2 * NG + g + 1)
                nc.gpsimd.tensor_tensor(x_sb[:, grp(g), :], x_sb[:, grp(g), :], on[:, grp(g), :], ALU.add)\
                    .then_inc(res_done, 1)

        @block.scalar
        def _(act):
            act.wait_ge(late_in, LATE)

            def out_of_psT(n, dst, scale=None, bias=None):
                act.wait_ge(t_done, n + 1)
                if bias is None:
                    nc.scalar.activation(dst, psT[n % 2][:, :], ACT.Copy).then_inc(t_evac, 1)
                elif scale is None:
                    nc.scalar.activation(dst, psT[n % 2][:, :], ACT.Identity, bias=bias).then_inc(t_evac, 1)
                else:
                    nc.scalar.activation(dst, psT[n % 2][:, :], ACT.Identity, bias=bias, scale=scale).then_inc(t_evac, 1)

            part = lambda a, g: a[:, 512 * g:512 * g + 512]
            for g in range(NG):
                out_of_psT(g, part(attT, g), bias=w["x_bv"][:, 0:1])
            for g in range(NG):
                out_of_psT(NG + g, part(xnT, g))
            for g in range(NG):
                act.wait_ge(y_done, (g + 1) * GT)
                nc.scalar.activation(th[:, grp(g), :], y[:, grp(g), :], ACT.Tanh, scale=0.5).then_inc(th_done, 1)
            for g in range(NG):
                act.wait_ge(w_done, g + 1)
                if g >= 1:
                    act.wait_ge(ss_done, g)
                nc.scalar.activation(sq[:, :, :], y[:, grp(g), :], ACT.Square, bias=1.0).then_inc(sq_done, 1)
            for g in range(NG):
                out_of_psT(2 * NG + g, part(qT, g))
            for g in range(NG):
                out_of_psT(3 * NG + g, part(onT, g), scale=w["ln_g"][:, 0:1], bias=w["ln_b"][:, 0:1])
            for g in range(NG):
                out_of_psT(4 * NG + g, part(xn3T, g))

        @block.vector
        def _(dve):
            dve.wait_ge(late_in, LATE)
            for j in range(5):
                last = nc.vector.tensor_tensor(wsum[:, cols(j)], w["w5"][:, cols(j)], ident[:, :], ALU.add)
            last.then_inc(wsum_done, 1)

            def statistics(rnd, g, src):
                n = rnd * NG + g
                for t in tiles(g):
                    nc.vector.bn_stats(stats[:, rnd, t, :], src(t)).then_inc(stat_done, 1)
                dve.wait_ge(stat_done, (n + 1) * GT)
                for t in tiles(g):
                    nc.vector.bn_aggr(mv[:, rnd, t, :], stats[:, rnd, t, :]).then_inc(var_done, 1)

            def normalise(rnd, g, src, dst):
                n = rnd * NG + g
                dve.wait_ge(rstd_done, n + 1)
                for t in tiles(g):
                    last = nc.vector.tensor_scalar(dst[:, t, :], src(t), mv[:, rnd, t, 0:1], rstd[:, rnd, t:t + 1],
                                                   ALU.subtract, ALU.mult)
                last.then_inc(n_done, 1)

            for g in range(NG):
                dve.wait_ge(m_done, g + 1)
                dve.wait_ge(xb_done, g + 1)
                nc.vector.tensor_tensor(x_sb[:, grp(g), :], psM[g % 2][:, :].rearrange("p (t d) -> p t d", d=D),
                                        x_sb[:, grp(g), :], ALU.add).then_inc(m_evac, 1)
                dve.wait_ge(m_evac, g + 1)
                statistics(0, g, lambda t: x_sb[:, t, :])
            for g in range(NG):
                normalise(0, g, lambda t: x_sb[:, t, :], xn1)
            for t in range(NT):
                dve.wait_ge(p_done, t + 1)
                nc.vector.tensor_tensor(y[:, t, :], psQ[:, 0:QK], w["b5"][:, 0:QK], ALU.add).then_inc(y_done, 1)
                nc.vector.tensor_tensor(vv[:, t, :], psV[:, 0:VV], w["b5"][:, QK:QK + VV], ALU.add).then_inc(v_done, 1)
            for g in range(NG):
                dve.wait_ge(th_done, g + 1)
                nc.vector.scalar_tensor_tensor(out=y[:, grp(g), :], in0=th[:, grp(g), :], scalar=1.0,
                                               in1=y[:, grp(g), :], op0=ALU.add, op1=ALU.mult).then_inc(w_done, 1)
            for g in range(NG):
                dve.wait_ge(sq_done, g + 1)
                nc.vector.tensor_reduce(ss[:, grp(g), :].rearrange("p t h -> p (t h)"),
                                        sq[:, :, :].rearrange("p t (h d) -> p (t h) d", d=DH), AX.X, ALU.add)\
                    .then_inc(ss_done, 1)
            for g in range(NG):
                dve.wait_ge(nrm_add, g + 1)
                flat = nrm[:, grp(g), :].rearrange("p t h -> p (t h)")
                nc.vector.reciprocal(flat, flat).then_inc(inv_done, 1)
            for g in range(NG):
                dve.wait_ge(inv_done, g + 1)
                heads = y[:, grp(g), :].rearrange("p t (h d) -> p (t h) d", d=DH)
                flat = nrm[:, grp(g), :].rearrange("p t h -> p (t h)")
                nc.vector.scalar_tensor_tensor(
                    out=heads, in0=heads, scalar=1.0, in1=flat.unsqueeze(2).to_broadcast([P, GT * G8, DH]),
                    op0=ALU.add, op1=ALU.mult).then_inc(k_ready, 1)
            for t in range(NT):
                dve.wait_ge(g_done, t + 1)
                gram = [g_of(t, b)[:, 0:2 * D].rearrange("p (k e) -> p k e", k=2) for b in range(2)]
                if t >= 2:
                    dve.wait_ge(state_done, t - 1)
                for b in range(2):
                    last = nc.vector.tensor_tensor(st[:, t % 2, b, :], gram[b][:, 0, :], w["blocks"][:, :], ALU.mult)
                last.then_inc(st1, 1)
                dve.wait_ge(st1, t + 1)
                for b in range(2):
                    last = nc.vector.tensor_tensor(state[:, t, b, :], gram[b][:, 1, :], st[:, t % 2, b, :], ALU.mult)
                last.then_inc(state_done, 1)
            for g in range(NG):
                dve.wait_ge(m_done, NG + g + 1)
                statistics(1, g, lambda t: psM[g % 2][:, cols(t % GT)])
                normalise(1, g, lambda t: psM[g % 2][:, cols(t % GT)], on)
            for g in range(NG):
                dve.wait_ge(m_done, 2 * NG + g + 1)
                dve.wait_ge(x1b_done, g + 1)
                nc.vector.tensor_tensor(x_sb[:, grp(g), :], psM[g % 2][:, :].rearrange("p (t d) -> p t d", d=D),
                                        x_sb[:, grp(g), :], ALU.add).then_inc(m_evac, 1)
                dve.wait_ge(m_evac, NG + g + 1)
                statistics(2, g, lambda t: x_sb[:, t, :])
            dve.wait_ge(t_done, 4 * NG)
            for g in range(NG):
                normalise(2, g, lambda t: x_sb[:, t, :], on)

        @block.tensor
        def _(pe):
            pe.wait_ge(late_in, LATE)

            def into_psT(n, src, g):
                if n >= 2:
                    pe.wait_ge(t_evac, n - 1)
                for t in tiles(g):
                    last = nc.tensor.transpose(psT[n % 2][:, cols(t % GT)], src(t), ident[:, :])
                last.then_inc(t_done, 1)

            def into_psM(read_out, lhsT, rhs, g, ready):
                if g >= 2:
                    pe.wait_ge(m_evac, read_out + g - 1)
                pe.wait_ge(t_evac, ready)
                for t in tiles(g):
                    last = nc.tensor.matmul(psM[g % 2][:, cols(t % GT)], lhsT[:, cols(t)], rhs, start=True, stop=True)
                last.then_inc(m_done, 1)

            for g in range(NG):
                into_psT(g, lambda t: att[:, cols(t)], g)
                if g:
                    into_psM(0, attT, w["x_wo"][:, :], g - 1, g)
            into_psM(0, attT, w["x_wo"][:, :], NG - 1, NG)
            for g in range(NG):
                pe.wait_ge(n_done, g + 1)
                into_psT(NG + g, lambda t: xn1[:, t, :], g)
            pe.wait_ge(wsum_done, 1)
            for t in range(NT):
                pe.wait_ge(t_evac, NG + t // GT + 1)
                if t:
                    pe.wait_ge(y_done, t)
                nc.tensor.matmul(psQ[:, 0:QK], xnT[:, cols(t)], wsum[:, 0:QK], start=True, stop=True)
                if t:
                    pe.wait_ge(v_done, t)
                nc.tensor.matmul(psV[:, 0:VV], xnT[:, cols(t)], wsum[:, QK:QK + VV], start=True, stop=True)\
                    .then_inc(p_done, 1)
            for g in range(NG):
                pe.wait_ge(k_ready, g + 1)
                into_psT(2 * NG + g, lambda t: y[:, t, 0:D], g)
            for t in range(NT):
                if t >= 2:
                    pe.wait_ge(state_done, t - 1)
                for k in range(2):
                    for b in range(2):
                        rows = slice(64 * b, 64 * b + 64)
                        last = nc.tensor.matmul(g_of(t, b)[:, k * D:(k + 1) * D],
                                                y[rows, t, (1 + k) * D:(2 + k) * D], vv[rows, t, k * D:(k + 1) * D],
                                                start=True, stop=True)
                last.then_inc(g_done, 1)
            for g in range(NG):
                pe.wait_ge(t_evac, 2 * NG + g + 1)
                pe.wait_ge(state_done, GT * (g + 1))
                if g < 2:
                    pe.wait_ge(m_evac, NG + g - 1)
                else:
                    pe.wait_ge(n_done, NG + g - 1)
                for t in tiles(g):
                    for b in range(2):
                        last = nc.tensor.matmul(psM[g % 2][64 * b:64 * b + 64, cols(t % GT)],
                                                qT[:, t * P + 64 * b:t * P + 64 * b + 64], state[:, t, b, :],
                                                start=True, stop=True)
                last.then_inc(m_done, 1)
            for g in range(NG):
                pe.wait_ge(n_done, NG + g + 1)
                into_psT(3 * NG + g, lambda t: on[:, t, :], g)
            for g in range(NG):
                into_psM(NG, onT, w["a_wo"][:, :], g, 3 * NG + g + 1)
            for g in range(NG):
                pe.wait_ge(n_done, 2 * NG + g + 1)
                into_psT(4 * NG + g, lambda t: on[:, t, :], g)


def experts(nc, w, keep, w_up_d, w_dn_d, out_d):
    (x_sb, xn3T, wup, wdn) = keep
    TB = TOK // 512
    with ExitStack() as ctx:
        sb = lambda n, s: ctx.enter_context(nc.sbuf_tensor(n, s, F32))
        psb = lambda n: ctx.enter_context(nc.psum_tensor(n, [P, 512], F32))
        sem = lambda n: ctx.enter_context(nc.semaphore(n))
        hT = [sb(f"hT{i}", [P, IC, 512]) for i in range(2)]
        acc = sb("acc", [P, NT, D])
        logit, ex, pr = sb("logit", [P, NT, E]), sb("ex", [P, NT, E]), sb("pr", [P, NT, E])
        top, tot, rtot = sb("top", [P, NT]), sb("tot", [P, NT]), sb("rtot", [P, NT])
        above, ties, rank = sb("above", [P, NT, E, E]), sb("ties", [P, NT, E, E]), sb("rank", [P, NT, E])
        kept, tot2, sw = sb("kept", [P, NT, E]), sb("tot2", [P, NT]), sb("sw", [P, NT * E])
        swe = [sb(f"swe{i}", [P, NT]) for i in range(2)]
        stats, mv = sb("stats3", [P, NT, 6]), sb("mv3", [P, NT, 2])
        rstd, epsv, minus_half = sb("rstd3", [P, NT]), sb("epsv3", [P, 4]), sb("minus_half3", [P, 4])
        ps_up = [psb(f"ps_up{i}") for i in range(4)]
        ps_dn = [psb(f"ps_dn{i}") for i in range(2)]
        ps_gate = psb("ps_gate")
        up_in = [sem("up_in0"), sem("up_in1")]
        gate_done, exp_done, chain, swe_done = sem("gate_done"), sem("gexp_done"), sem("gate_chain"), sem("swe_done")
        up_done, gelu_done, dn_done, acc_done = sem("up_done"), sem("gelu_done"), sem("dn_done"), sem("acc_done")
        sub_done, cst, eps_add, rstd_done = sem("sub_done"), sem("cst3"), sem("eps_add3"), sem("rstd3_done")
        stat_done, var_done, n_done, y_done, stored = sem("stat3"), sem("var3"), sem("n3"), sem("y3"), sem("stored")
        block = ctx.enter_context(nc.Block())

        def pairs(eng, body):
            for p in range(2):
                body(p, 0, p, p)
            with eng.Fori(1, E // 2) as r:
                for p in range(2):
                    body(r * 2 + p, r, p, None)

        @block.sync
        def _(sp):
            def body(e, r, p, known):
                if known is None:
                    sp.wait_ge(dn_done, e * TB - TB)
                sp.dma_start(wup[p][:, :], w_up_d[e]).then_inc(up_in[p], 16)
                sp.dma_start(wdn[p][:, :, :], w_dn_d[e].rearrange("(c p) h -> p c h", p=P)).then_inc(up_in[p], 16)

            pairs(sp, body)
            out_v = out_d.rearrange("(t p) d -> p t d", p=P)
            for g in range(4):
                sp.wait_ge(y_done, g + 1)
                sp.dma_start(out_v[:, 4 * g:4 * g + 4, :], acc[:, 4 * g:4 * g + 4, :]).then_inc(stored, 16)
            sp.wait_ge(stored, 64)

        @block.scalar
        def _(act):
            act.wait_ge(sub_done, 1)
            nc.scalar.activation(ex[:, :, :], logit[:, :, :], ACT.Exp).then_inc(exp_done, 1)

            def body(e, r, p, known):
                for tb in range(TB):
                    for c in range(IC):
                        act.wait_ge(up_done, e * (TB * IC) + (tb * IC + c + 1))
                        if c == 0 and not (known == 0 and tb < 2):
                            act.wait_ge(dn_done, e * TB + (tb - 1))
                        nc.scalar.activation(hT[tb % 2][:, c, :], ps_up[c][:, :], ACT.Gelu).then_inc(gelu_done, 1)

            pairs(act, body)

        @block.gpsimd
        def _(pool):
            pool.memset(acc[:, :, :], 0.0).then_inc(cst, 1)
            pool.memset(epsv[:, :], EPS).then_inc(cst, 1)
            pool.memset(minus_half[:, :], -0.5).then_inc(cst, 1)
            pool.wait_ge(cst, 3)
            for g in range(4):
                pool.wait_ge(var_done, 4 * (g + 1))
                s = slice(4 * g, 4 * g + 4)
                nc.gpsimd.tensor_tensor(rstd[:, s], mv[:, s, 1], epsv[:, :], ALU.add).then_inc(eps_add, 1)
                pool.wait_ge(eps_add, g + 1)
                nc.gpsimd.tensor_tensor(rstd[:, s], rstd[:, s], minus_half[:, :], ALU.pow).then_inc(rstd_done, 1)

        @block.vector
        def _(dve):
            steps = [0]

            def then_wait(ins):
                steps[0] += 1
                ins.then_inc(chain, 1)
                dve.wait_ge(chain, steps[0])

            by_e = lambda a: a[:, :].unsqueeze(2).to_broadcast([P, NT, E])
            dve.wait_ge(gate_done, 1)
            then_wait(nc.vector.tensor_tensor(
                logit[:, :, :], ps_gate[:, 0:NT * E].rearrange("p (t e) -> p t e", e=E),
                w["ebias"][:, :].unsqueeze(1).to_broadcast([P, NT, E]), ALU.add))
            then_wait(nc.vector.tensor_reduce(top[:, :], logit[:, :, :], AX.X, ALU.max))
            nc.vector.tensor_tensor(logit[:, :, :], logit[:, :, :], by_e(top), ALU.subtract).then_inc(sub_done, 1)
            dve.wait_ge(exp_done, 1)
            then_wait(nc.vector.tensor_reduce(tot[:, :], ex[:, :, :], AX.X, ALU.add))
            then_wait(nc.vector.reciprocal(rtot[:, :], tot[:, :]))
            then_wait(nc.vector.tensor_tensor(pr[:, :, :], ex[:, :, :], by_e(rtot), ALU.mult))
            of_j = pr[:, :, :].unsqueeze(2).to_broadcast([P, NT, E, E])
            of_e = pr[:, :, :].unsqueeze(3).to_broadcast([P, NT, E, E])
            nc.vector.tensor_tensor(above[:, :, :, :], of_j, of_e, ALU.is_gt)
            then_wait(nc.vector.tensor_tensor(ties[:, :, :, :], of_j, of_e, ALU.is_equal))
            then_wait(nc.vector.tensor_tensor(ties[:, :, :, :].rearrange("p t e j -> p t (e j)"),
                                              ties[:, :, :, :].rearrange("p t e j -> p t (e j)"),
                                              w["before"][:, :].unsqueeze(1).to_broadcast([P, NT, E * E]), ALU.mult))
            then_wait(nc.vector.tensor_tensor(above[:, :, :, :], above[:, :, :, :], ties[:, :, :, :], ALU.add))
            then_wait(nc.vector.tensor_reduce(rank[:, :, :], above[:, :, :, :], AX.X, ALU.add))
            then_wait(nc.vector.scalar_tensor_tensor(out=kept[:, :, :], in0=rank[:, :, :], scalar=2.0,
                                                     in1=pr[:, :, :], op0=ALU.is_lt, op1=ALU.mult))
            then_wait(nc.vector.tensor_reduce(tot2[:, :], kept[:, :, :], AX.X, ALU.add))
            then_wait(nc.vector.tensor_scalar(tot2[:, :], tot2[:, :], 1e-6, None, ALU.add))
            then_wait(nc.vector.reciprocal(tot2[:, :], tot2[:, :]))
            then_wait(nc.vector.tensor_tensor(sw[:, :].rearrange("p (e t) -> p t e", e=E), kept[:, :, :],
                                              by_e(tot2), ALU.mult))
            dve.wait_ge(cst, 1)

            def body(e, r, p, known):
                if not (known is not None and known < 2):
                    dve.wait_ge(acc_done, e * TB - TB)
                nc.vector.tensor_copy(swe[p][:, :], sw[:, bass.ds(e * NT, NT)]).then_inc(swe_done, 1)
                dve.wait_ge(swe_done, e + 1)
                for tb in range(TB):
                    dve.wait_ge(dn_done, e * TB + (tb + 1))
                    if not (known == 0):
                        dve.wait_ge(acc_done, e * TB + (tb + 1 - TB))
                    for j in range(4):
                        t = 4 * tb + j
                        last = nc.vector.scalar_tensor_tensor(
                            out=acc[:, t, :], in0=ps_dn[tb % 2][:, j * P:(j + 1) * P], scalar=swe[p][:, t:t + 1],
                            in1=acc[:, t, :], op0=ALU.mult, op1=ALU.add)
                    last.then_inc(acc_done, 1)

            pairs(dve, body)
            for g in range(4):
                dve.wait_ge(acc_done, E * TB - 4 + g + 1)
                for t in range(4 * g, 4 * g + 4):
                    nc.vector.bn_stats(stats[:, t, :], acc[:, t, :]).then_inc(stat_done, 1)
                dve.wait_ge(stat_done, 4 * g + 4)
                for t in range(4 * g, 4 * g + 4):
                    nc.vector.bn_aggr(mv[:, t, :], stats[:, t, :]).then_inc(var_done, 1)
            for g in range(4):
                dve.wait_ge(rstd_done, g + 1)
                for t in range(4 * g, 4 * g + 4):
                    last = nc.vector.tensor_scalar(acc[:, t, :], acc[:, t, :], mv[:, t, 0:1], rstd[:, t:t + 1],
                                                   ALU.subtract, ALU.mult)
                last.then_inc(n_done, 1)
                dve.wait_ge(n_done, g + 1)
                s = slice(4 * g, 4 * g + 4)
                nc.vector.tensor_tensor(acc[:, s, :], acc[:, s, :], x_sb[:, s, :], ALU.add).then_inc(y_done, 1)

        @block.tensor
        def _(pe):
            for t in range(NT):
                last = nc.tensor.matmul(ps_gate[:, t * E:(t + 1) * E], xn3T[:, t * P:(t + 1) * P], w["gate"][:, :],
                                        start=True, stop=True)
            last.then_inc(gate_done, 1)

            def down(e, tb, p, first):
                pe.wait_ge(gelu_done, e * (TB * IC) + (tb + 1) * IC)
                if not first:
                    pe.wait_ge(acc_done, e * TB + (tb - 1))
                for j in range(4):
                    for c in range(IC):
                        last = nc.tensor.matmul(ps_dn[tb % 2][:, j * P:(j + 1) * P], hT[tb % 2][:, c, j * P:(j + 1) * P],
                                                wdn[p][:, c, :], start=(c == 0), stop=(c == IC - 1))
                last.then_inc(dn_done, 1)

            def body(e, r, p, known):
                for tb in range(TB):
                    if tb == 0:
                        pe.wait_ge(up_in[p], r * 32 + 32)
                    for c in range(IC):
                        if not (known == 0 and tb == 0):
                            pe.wait_ge(gelu_done, e * (TB * IC) + ((tb - 1) * IC + c + 1))
                        nc.tensor.matmul(ps_up[c][:, :], wup[p][:, c * P:(c + 1) * P], xn3T[:, 512 * tb:512 * tb + 512],
                                         start=True, stop=True).then_inc(up_done, 1)
                    if tb:
                        down(e, tb - 1, p, known == 0 and tb - 1 < 2)
                    elif known != 0:
                        down(e - 1, TB - 1, 1 - p, False)

            pairs(pe, body)
            down(E - 1, TB - 1, 1, False)


def build(nc, a, out_d):
    with ExitStack() as ctx:
        sb = lambda n, s, d: ctx.enter_context(nc.sbuf_tensor(n, s, d))
        x_sb = sb("x_sb", [P, NT, D], F32)
        ident = sb("ident", [P, P], F32)
        ident_b = sb("ident_b", [P, P], BF16)
        ones_f = sb("ones_f", [P, P], F32)
        flag_i = sb("flag_i", [1, 1], I32)
        att = sb("att", [P, NT * D], F32)
        late_in = ctx.enter_context(nc.semaphore("late_in"))
        w = {n: sb("w_" + n, shape, F32) for n, shape, _ in LATE_WEIGHTS}
        q_scr = nc.dram_tensor("q_scr", (2, NSLOT, DH, NPAIR, TOK), BF16, kind="Internal").ap()
        k_scr = nc.dram_tensor("k_scr", (2, 3, DH, NPAIR, SK), BF16, kind="Internal").ap()
        query_phase(nc, (a["x"], a["mask"], a["ident"], a["x_wq"], a["x_bq"]),
                    (x_sb, q_scr, flag_i, ident, ident_b, ones_f))
        cross_attention(nc, (a["ctxT"], a["mask"], a["maskT"], a["x_wk"], a["x_bk"], a["x_wv"]),
                        (q_scr, k_scr, flag_i, ident, ident_b, ones_f, att), a, w, late_in)
        xn3T = sb("xn3T", [P, TOK], F32)
        self_attention(nc, w, (x_sb, att, xn3T, ident, late_in))
        wup = [sb(f"wup{i}", [P, I], F32) for i in range(2)]
        wdn = [sb(f"wdn{i}", [P, IC, D], F32) for i in range(2)]
        experts(nc, w, (x_sb, xn3T, wup, wdn), a["w_up"], a["w_dn"], out_d)


def kernel(**inputs):
    import numpy as np
    import concourse.bacc as bacc
    from concourse.bass_utils import run_bass_kernel_spmd

    n = {k: np.asarray(v) for k, v in inputs.items()}
    mask = n["mask_BxSxS2_bf1"].view(np.uint8)
    by_pair = lambda w: w.reshape(NPAIR, 2, DH, -1).transpose(1, 2, 0, 3).reshape(D, -1)
    row, col = (lambda v: v.reshape(1, -1)), (lambda v: v.reshape(-1, 1))
    wk, bk, wv, bv = (n["L0_attn_" + s] for s in ("Wk", "bk", "Wv", "bv"))
    host = {
        "x": n["x"].reshape(TOK, D),
        "ctxT": n["ctx_1024"].transpose(0, 2, 1),
        "mask": mask,
        "maskT": mask.transpose(0, 2, 1),
        "ident": np.eye(P, dtype=np.float32),
        "x_wq": by_pair(n["L0_xattn_Wq"]).T, "x_bq": by_pair(n["L0_xattn_bq"])[:, 0],
        "x_wk": by_pair(n["L0_xattn_Wk"]).T, "x_bk": by_pair(n["L0_xattn_bk"])[:, 0],
        "x_wv": n["L0_xattn_Wv"].T,
        "x_bv": col(n["L0_xattn_bv"]), "x_wo": n["L0_xattn_Wo"].T, "x_bo": row(n["L0_xattn_bo"]),
        "w5": np.concatenate([n["L0_attn_Wq"].T, wk[0].T, wk[1].T, wv[0].T, wv[1].T], axis=1),
        "b5": row(np.concatenate([n["L0_attn_bq"], bk[0], bk[1], bv[0], bv[1]])),
        "blocks": (np.kron(np.eye(NH), np.ones((DH, DH))) * SQ ** -2.0).astype(np.float32),
        "ln_g": col(n["L0_attn_ln_g"]), "ln_b": col(n["L0_attn_ln_b"]),
        "a_wo": n["L0_attn_Wo"].T, "a_bo": row(n["L0_attn_bo"]),
        "gate": n["L0_ffn_gate_w"].T, "ebias": row(n["L0_ffn_expert_bias"]),
        "before": row(np.tril(np.ones((E, E), np.float32), -1)),
        "w_up": n["L0_ffn_w_up"].transpose(0, 2, 1), "w_dn": n["L0_ffn_w_down"].transpose(0, 2, 1),
    }
    nc = bacc.Bacc("TRN2", target_bir_lowering=False, num_devices=1)
    arrays, aps = {}, {}
    for name, arr in host.items():
        arr = np.ascontiguousarray(arr)
        arrays[f"in_{name}"] = arr
        aps[name] = nc.dram_tensor(f"in_{name}", arr.shape, mybir.dt.from_np(arr.dtype), kind="ExternalInput").ap()
    out = nc.dram_tensor("out", (TOK, D), F32, kind="ExternalOutput").ap()
    build(nc, aps, out)
    r = run_bass_kernel_spmd(nc, [arrays], core_ids=[0])
    return r.results[0]["out"].reshape(NB, SQ, D)
```

```python
from contextlib import ExitStack

import concourse.bass as bass
from concourse import mybir

F32 = mybir.dt.float32
BF16 = mybir.dt.bfloat16
U8 = mybir.dt.uint8
U16 = mybir.dt.uint16
I32 = mybir.dt.int32
ALU = mybir.AluOpType
ACT = mybir.ActivationFunctionType
AX = mybir.AxisListType

P = 128
NB, SQ, SK, D = 32, 64, 1601, 128
NH = 16
DH = D // NH
NPAIR = NH // 2
TOK = NB * SQ
NT = TOK // P
KT = (SK + P - 1) // P
KLAST = SK - (KT - 1) * P
NSLOT = 6
AROWS = NSLOT * DH
ROWS = 2 * AROWS
MROWS = 3
CH = [(0, 401), (401, 801), (801, 1201), (1201, 1601)]
MW = 401
NCH = 4
VG = [(0, 4), (4, 8), (8, 12), (12, 13)]
E, I = 8, 512
IC = I // P
EPS = 1e-5
PV_W = 32
ONE_COL = 2 * DH
TWO_ONES = 1 + 0x3F80 * 2.0 ** -23

LATE_WEIGHTS = [
    ("x_bv", [P, 1], False), ("x_wo", [P, D], False), ("x_bo", [P, D], True),
    ("w5", [P, 5 * D], False), ("b5", [P, 5 * D], True), ("blocks", [P, D], False),
    ("ln_g", [P, 1], False), ("ln_b", [P, 1], False), ("a_wo", [P, D], False), ("a_bo", [P, D], True),
    ("gate", [P, E], False), ("ebias", [P, E], True), ("before", [P, E * E], True)]
LATE = 16 * len(LATE_WEIGHTS)


def keys_of(t):
    return P if t < KT - 1 else KLAST


class QueryPhase:

    def __init__(self, nc, ctx, drams, keep, room):
        self.nc, self.d, self.keep, self.room = nc, drams, keep, room
        sb = lambda n, s, d: ctx.enter_context(nc.sbuf_tensor(n, s, d))
        sem = lambda n: ctx.enter_context(nc.semaphore(n))
        self.wq, self.bq, self.bqs = sb("wq", [P, D], F32), sb("bq", [P, 1], F32), sb("bqs", [P, 1], F32)
        self.stats, self.mv = sb("stats", [P, NT, 6], F32), sb("mv", [P, NT, 2], F32)
        self.eps_t, self.expo, self.rstd = sb("eps_t", [P, NT], F32), sb("expo", [P, NT], F32), sb("rstd", [P, NT], F32)
        self.rest = sb("rest", [P, 512], F32)
        self.q_parts = sb("q_parts", [P, 3, TOK], BF16)
        self.fmin, self.fsum = sb("fmin", [P, 1], F32), sb("fsum", [P, 1], F32)
        self.ok_a, self.ok = sb("ok_a", [P, 1], F32), sb("ok", [P, 1], F32)
        self.x_in = [sem("x_in0"), sem("x_in1")]
        self.w_in, self.mask_in = sem("w_in"), sem("mask_in")
        self.stat_done, self.var_done, self.rstd_done, self.xn_done = (
            sem("stat_done"), sem("var_done"), sem("rstd_done"), sem("xn_done"))
        self.tr_done, self.tr_evac, self.q_done, self.q_evac, self.split = (
            sem("tr_done"), sem("tr_evac"), sem("q_done"), sem("q_evac"), sem("split"))
        self.fmin_done, self.fsum_done, self.ok_done, self.okm_done, self.flag_done, self.cst = (
            sem("fmin_done"), sem("fsum_done"), sem("ok_done"), sem("okm_done"), sem("flag_done"), sem("cst"))
        self.q_stored = [sem("q_stored0"), sem("q_stored1")]
        self.bqs_done, self.identb_done = sem("bqs_done"), sem("identb_done")
        self.n16 = NB * SQ * SK // P // 2
        self.half = self.n16 // 2

    def load_x(self, sp):
        xv = self.d["x"].rearrange("(t p) d -> p t d", p=P)
        x_sb = self.keep["x_sb"]
        sp.dma_start(x_sb[:, 0:4, :], xv[:, 0:4, :]).then_inc(self.x_in[0], 16)
        sp.dma_start(self.keep["ident"][:, :], self.d["ident"]).then_inc(self.w_in, 16)
        sp.dma_start(self.wq[:, :], self.d["x_wq"]).then_inc(self.w_in, 16)
        sp.dma_start(self.bq[:, :], self.d["x_bq"].rearrange("(p a) -> p a", a=1)).then_inc(self.w_in, 16)
        sp.dma_start(x_sb[:, 4:NT, :], xv[:, 4:NT, :]).then_inc(self.x_in[1], 16)

    def load_mask(self, sp):
        sp.dma_start(self.room["mask"].bitcast(U8),
                     self.d["mask"].rearrange("b q k -> (b q k)").rearrange("(p n) -> p n", p=P)).then_inc(self.mask_in, 16)

    def store_q(self, sp, first):
        lo, hi = (0, 512) if first else (512, TOK)
        sp.wait_ge(self.split, 4 if first else 16)
        for s, part in enumerate((0, 0, 0, 1, 1, 2)):
            for a in range(2):
                sp.dma_start(self.room["q_scr"][a, s, :, :, lo:hi].rearrange("r p n -> (r p) n"),
                             self.q_parts[64 * a:64 * a + 64, part, lo:hi]).then_inc(self.q_stored[0 if first else 1], 16)

    def gpsimd(self, pool):
        nc = self.nc
        pool.memset(self.keep["ones_f"][:, :], 1.0).then_inc(self.cst, 1)
        pool.memset(self.eps_t[:, :], EPS).then_inc(self.cst, 1)
        pool.memset(self.expo[:, :], -0.5).then_inc(self.cst, 1)
        pool.wait_ge(self.cst, 3)
        for n, (t0, t1) in enumerate(((0, 4), (4, NT))):
            pool.wait_ge(self.var_done, t1)
            nc.gpsimd.tensor_tensor(self.rstd[:, t0:t1], self.mv[:, t0:t1, 1], self.eps_t[:, t0:t1], ALU.add)\
                .then_inc(self.cst, 1)
            pool.wait_ge(self.cst, 4 + n)
            nc.gpsimd.tensor_tensor(self.rstd[:, t0:t1], self.rstd[:, t0:t1], self.expo[:, t0:t1], ALU.pow)\
                .then_inc(self.rstd_done, 1)

    def vector(self, dve):
        nc, x_sb, xn = self.nc, self.keep["x_sb"], self.room["xn"]
        for n, (t0, t1) in enumerate(((0, 4), (4, NT))):
            dve.wait_ge(self.x_in[n], 16)
            for t in range(t0, t1):
                nc.vector.bn_stats(self.stats[:, t, :], x_sb[:, t, :]).then_inc(self.stat_done, 1)
            for t in range(t0, t1):
                dve.wait_ge(self.stat_done, t + 1)
                nc.vector.bn_aggr(self.mv[:, t, :], self.stats[:, t, :]).then_inc(self.var_done, 1)
        dve.wait_ge(self.w_in, 48)
        nc.vector.tensor_scalar(self.bqs[:, :], self.bq[:, :], DH ** -0.5, None, ALU.mult).then_inc(self.bqs_done, 1)
        nc.vector.tensor_copy(self.keep["ident_b"][:, :], self.keep["ident"][:, :]).then_inc(self.identb_done, 1)
        for n, (t0, t1) in enumerate(((0, 4), (4, NT))):
            dve.wait_ge(self.rstd_done, n + 1)
            for t in range(t0, t1):
                nc.vector.tensor_scalar(xn[:, t * D:(t + 1) * D], x_sb[:, t, :], self.mv[:, t, 0:1],
                                        self.rstd[:, t:t + 1], ALU.subtract, ALU.mult).then_inc(self.xn_done, 1)
        qf, parts, rest = self.room["qf"], self.q_parts, self.rest
        for g in range(4):
            s = slice(512 * g, 512 * g + 512)
            dve.wait_ge(self.q_evac, g + 1)
            nc.vector.tensor_copy(parts[:, 0, s], qf[:, s]).then_inc(self.split, 1)
            dve.wait_ge(self.split, 4 * g + 1)
            nc.vector.tensor_tensor(rest[:, :], qf[:, s], parts[:, 0, s], ALU.subtract).then_inc(self.split, 1)
            dve.wait_ge(self.split, 4 * g + 2)
            nc.vector.tensor_copy(parts[:, 1, s], rest[:, :]).then_inc(self.split, 1)
            dve.wait_ge(self.split, 4 * g + 3)
            nc.vector.tensor_tensor(parts[:, 2, s], rest[:, :], parts[:, 1, s], ALU.subtract).then_inc(self.split, 1)

    def check_mask(self, dve):
        nc = self.nc
        dve.wait_ge(self.mask_in, 16)
        nc.vector.tensor_reduce(self.fmin[:, :], self.room["mask"][:, 0:self.half], AX.X, ALU.min)\
            .then_inc(self.fmin_done, 1)
        dve.wait_ge(self.fmin_done, 1)
        dve.wait_ge(self.fsum_done, 1)
        nc.vector.tensor_scalar(self.ok_a[:, :], self.fmin[:, :], 257.0, None, ALU.is_equal).then_inc(self.ok_done, 1)
        dve.wait_ge(self.ok_done, 1)
        nc.vector.scalar_tensor_tensor(out=self.ok[:, :], in0=self.fsum[:, :], scalar=257.0 * (self.n16 - self.half),
                                       in1=self.ok_a[:, :], op0=ALU.is_equal, op1=ALU.mult).then_inc(self.ok_done, 1)
        dve.wait_ge(self.okm_done, 1)
        nc.vector.tensor_scalar(self.keep["flag_i"][:, :], self.room["ps_f"][0:1, 0:1], float(P), None, ALU.is_equal)\
            .then_inc(self.flag_done, 1)

    def scalar(self, act):
        nc, ps_t, ps_q = self.nc, self.room["ps_t"], self.room["ps_q"]
        act.wait_ge(self.bqs_done, 1)
        for g in range(4):
            act.wait_ge(self.tr_done, g + 1)
            nc.scalar.activation(self.room["xnT"][:, 512 * g:512 * g + 512], ps_t[g % 2], ACT.Copy)\
                .then_inc(self.tr_evac, 1)
            act.wait_ge(self.q_done, g + 1)
            nc.scalar.activation(self.room["qf"][:, 512 * g:512 * g + 512], ps_q[g % 2], ACT.Identity,
                                 bias=self.bqs[:, 0:1], scale=DH ** -0.5).then_inc(self.q_evac, 1)
        act.wait_ge(self.mask_in, 16)
        words = self.room["mask"][:, self.half:self.n16]
        nc.scalar.activation(words.bitcast(BF16), words, ACT.Copy, accum_out=self.fsum[:, :]).then_inc(self.fsum_done, 1)

    def tensor(self, pe):
        nc, ps_t, ps_q, xn = self.nc, self.room["ps_t"], self.room["ps_q"], self.room["xn"]
        pe.wait_ge(self.w_in, 48)
        for g in range(4):
            pe.wait_ge(self.xn_done, 4 * g + 4)
            if g >= 2:
                pe.wait_ge(self.tr_evac, g - 1)
            for t in range(4 * g, 4 * g + 4):
                last = nc.tensor.transpose(ps_t[g % 2][:, (t % 4) * P:(t % 4 + 1) * P], xn[:, t * D:(t + 1) * D],
                                           self.keep["ident"][:, :])
            last.then_inc(self.tr_done, 1)
            pe.wait_ge(self.tr_evac, g + 1)
            if g >= 2:
                pe.wait_ge(self.q_evac, g - 1)
            nc.tensor.matmul(ps_q[g % 2], self.wq[:, :], self.room["xnT"][:, 512 * g:512 * g + 512],
                             start=True, stop=True).then_inc(self.q_done, 1)

    def count_true(self, pe):
        pe.wait_ge(self.ok_done, 2)
        pe.wait_ge(self.cst, 1)
        self.nc.tensor.matmul(self.room["ps_f"][0:1, 0:1], self.ok[:, :], self.keep["ones_f"][:, 0:1],
                              start=True, stop=True).then_inc(self.okm_done, 1)

    def all_true(self, eng):
        eng.wait_ge(self.flag_done, 1)
        return eng.value_load(self.keep["flag_i"][0:1, 0:1]) == 1


def cross_attention(nc, keep, drams, w, late_in):
    ctx_d, mask_d, maskT_d, wk_d, bk_d, wv_d = (drams[n] for n in ("ctxT", "mask", "maskT", "x_wk", "x_bk", "x_wv"))
    q_scr, k_scr, ident, ident_b, att = (keep[n] for n in ("q_scr", "k_scr", "ident", "ident_b", "att"))
    with ExitStack() as ctx:
        sb = lambda n, s, d: ctx.enter_context(nc.sbuf_tensor(n, s, d))
        psb = lambda n: ctx.enter_context(nc.psum_tensor(n, [P, 512], F32))
        sem = lambda n: ctx.enter_context(nc.semaphore(n))
        wk, wv, bk = sb("wk", [P, D], F32), sb("wv", [P, D], F32), sb("bk", [P, 1], F32)
        ctxT = [sb(f"ctxT{i}", [P, SK], F32) for i in range(2)]
        kf = [sb(f"kf{i}", [P, MW], F32) for i in range(2)]
        krest = [sb(f"krest{i}", [P, MW], F32) for i in range(2)]
        kparts = sb("kparts", [P, 3, SK], BF16)
        kst_flat = [sb(f"kst{i}", [P, NPAIR * SK], BF16) for i in range(2)]
        kst = [k[:, :].rearrange("r (a n) -> r a n", a=NPAIR) for k in kst_flat]
        qmax = [sb(f"qmax{i}", [P, NPAIR * P], BF16) for i in range(2)]
        qsc = [sb(f"qsc{i}", [P, NPAIR * P], BF16) for i in range(2)]
        v = [sb(f"v{i}", [P, KT, NPAIR, PV_W], F32) for i in range(2)]
        probs2 = sb("probs", [P, 2 * NPAIR * P], F32)
        probs = [probs2[:, i * NPAIR * P:(i + 1) * NPAIR * P] for i in range(2)]
        mx2 = sb("mx2", [P, 2, NPAIR], F32)
        mx = sb("mx", [P, NPAIR], F32)
        mrest = sb("mrest", [P, NPAIR], F32)
        mparts = sb("mparts", [P, NPAIR, MROWS], BF16)
        oT = sb("oT", [P, 2 * P], F32)
        rec = sb("rec", [P, NPAIR], F32)
        mask_q = sb("mask_q", [P, SK], U8)
        mask_k = sb("mask_k", [P, KT, SQ], U8)
        picked = sb("picked", [P, 2, MW], F32)
        tiny, held = sb("tiny", [P, 1], F32), sb("held", [P, 1], F32)
        args2 = sb("args", [P, 2 * NPAIR * P], F32)
        fill, arg = (args2[:, i * NPAIR * P:(i + 1) * NPAIR * P] for i in range(2))
        score = [psb(f"score{i}") for i in range(2)]
        maxps = [ctx.enter_context(nc.psum_tensor(f"maxps{i}", [P, 2, 512], F32)) for i in range(2)]
        pvps, misc = psb("pvps"), psb("misc")

        query = QueryPhase(nc, ctx, drams, keep, {
            "mask": kst_flat[1][:, :].bitcast(U16), "xn": probs2, "xnT": args2, "qf": att,
            "q_scr": q_scr, "ps_t": [maxps[0][:, i, :] for i in range(2)], "ps_q": [maxps[1][:, i, :] for i in range(2)],
            "ps_f": score[0]})

        w_in = sem("w_in1")
        ctx_in = [sem("ctx_in0"), sem("ctx_in1")]
        cst, ones_in = sem("cst1"), sem("ones_in")
        k_done, k_evac, k_split, k_chain = sem("k_done"), sem("k_evac"), sem("k_split"), sem("k_chain")
        v_done, v_evac = sem("v_done"), sem("v_evac")
        k_scr_in = [sem("k_scr_in0"), sem("k_scr_in1")]
        kst_in = [sem("kst_in0"), sem("kst_in1")]
        qmax_in, qsc_in = sem("qmax_in"), sem("qsc_in")
        max_ready, max_red, m_chain, m_parts = sem("max_ready"), sem("max_red"), sem("m_chain"), sem("m_parts")
        mrow_done, mrow_evac = sem("mrow_done"), sem("mrow_evac")
        score_ready, exp_done, pv_done = sem("score_ready"), sem("exp_done"), sem("pv_done")
        mask_in, mask_kin = sem("mask_in1"), sem("mask_kin")
        pick_fill, pick_done, fill_done, fill_evac, arg_fill, arg_done = (
            sem("pick_fill"), sem("pick_done"), sem("fill_done"), sem("fill_evac"), sem("arg_fill"), sem("arg_done"))
        oT_copied, oT_back, rec_done, att_done = sem("oT_copied"), sem("oT_back"), sem("rec_done"), sem("att_done")

        MAX_STEPS = {0: [4], 1: [5], 2: [6], 3: [7], 4: [8], 5: [9], 6: [10, 11], 7: [12], 8: [13, 14], 9: [15]}
        EARLY_STEPS = {10: [0], 11: [1], 12: [2, 3]}
        SPLIT_SLOT = 10
        MISC = {0: ("k", 2, 0), 1: ("k", 2, 1), 2: ("o", -1, 0), 3: ("v", 1, 2), 4: ("k", 2, 2), 5: ("k", 2, 3),
                6: ("v", 1, 3), 7: ("v", 2, 0), 9: ("v", 2, 1), 11: ("m", 1, 0), 12: ("m", 1, 1)}

        def wanted(kind, stage, i_known):
            return i_known is None or 0 <= i_known + stage < NB

        def evacuated(eng, kind, b, n):
            if kind == "v":
                eng.wait_ge(v_evac, b * 4 + (n + 1))
            elif kind == "k":
                eng.wait_ge(k_evac, b * 4 + (n + 1))
            elif kind == "m":
                eng.wait_ge(mrow_evac, b * 2 + (n + 1))
            else:
                eng.wait_ge(att_done, b * 2 + 2)

        def previous_use(slot, i_known):
            for s in range(slot - 1, -1, -1):
                if s in MISC and wanted(MISC[s][0], MISC[s][1], i_known):
                    return MISC[s]
            return ("v", 1, 1) if i_known == -1 else ("m", 0, 1)

        def iterations(eng, body):
            body(-1, -1, 1, -1)
            body(0, 0, 0, 0)
            body(1, 0, 1, 1)
            with eng.Fori(1, NB // 2 - 2) as r:
                body(r * 2, r, 0, None)
                body(r * 2 + 1, r, 1, None)
            for i in range(NB - 4, NB):
                body(i, i // 2, i % 2, i)

        def batches(eng, body):
            body(0, 0, 0, 0)
            body(1, 0, 1, 1)
            with eng.Fori(1, NB // 2) as r:
                body(r * 2, r, 0, None)
                body(r * 2 + 1, r, 1, None)

        def sync_program(sp):
            def load_ctx(b, p):
                sp.dma_start(ctxT[p][:, :], ctx_d[b, :, :]).then_inc(ctx_in[p], 16)

            def load_q(b, p):
                for a in range(2):
                    dst = qmax[p][a * AROWS:(a + 1) * AROWS, :].rearrange("r (p a n) -> r p a n", a=2, n=SQ)[:, :, a, :]
                    src = q_scr[a].rearrange("s r p n -> (s r) p n")[:, :, bass.ds(b * SQ, SQ)]
                    sp.dma_start(dst, src).then_inc(qmax_in, 16)

            def copy_q(p):
                sp.dma_start(qsc[p][0:ROWS, :], qmax[p][0:ROWS, :]).then_inc(qsc_in, 16)

            def stack_k(half, b, p, tiles_used):
                lo, hi = (0, CH[1][1]) if half == 0 else (CH[2][0], SK)
                sp.wait_ge(k_split, b * 4 + (2 * half + 2))
                for a in range(2):
                    sp.dma_start(k_scr[a, :, :, :, lo:hi].rearrange("s r p n -> (r p) s n"),
                                 kparts[64 * a:64 * a + 64, :, lo:hi]).then_inc(k_scr_in[half], 16)
                sp.wait_ge(k_scr_in[half], b * 32 + 32)
                if tiles_used is not None:
                    sp.wait_ge(score_ready, tiles_used)
                for a in range(2):
                    for row, parts in ((0, 3), (3 * DH, 2), (5 * DH, 1)):
                        src = k_scr[a, 0:parts, :, :, lo:hi].rearrange("s r p n -> (s r) p n")
                        r0 = a * AROWS + row
                        sp.dma_start(kst[p][r0:r0 + parts * DH, :, lo:hi], src).then_inc(kst_in[half], 16)

            query.load_x(sp)
            sp.dma_start(wk[:, :], wk_d).then_inc(w_in, 16)
            sp.dma_start(bk[:, :], bk_d.rearrange("(p a) -> p a", a=1)).then_inc(w_in, 16)
            sp.dma_start(wv[:, :], wv_d).then_inc(w_in, 16)
            load_ctx(0, 0)
            query.load_mask(sp)
            query.store_q(sp, True)
            sp.wait_ge(cst, 1)
            sp.wait_ge(query.q_stored[0], 2 * NSLOT * 16)
            load_q(0, 0)
            stack_k(0, 0, 0, None)
            stack_k(1, 0, 0, None)
            query.store_q(sp, False)
            load_ctx(1, 1)
            for name, shape, to_all in LATE_WEIGHTS:
                src = drams[name].to_broadcast([P, shape[1]]) if to_all else drams[name]
                sp.dma_start(w[name][:, :], src).then_inc(late_in, 16)
            sp.wait_ge(query.q_stored[1], 2 * NSLOT * 16)
            with sp.If(query.all_true(sp)):
                def body(i, r, p, known):
                    if known is None or known + 1 < NB:
                        if known is None or known > 0:
                            sp.wait_ge(score_ready, i * (2 * KT))
                        sp.wait_ge(qmax_in, i * 32 + 64)
                        copy_q(1 - p)
                    if known is None or known + 2 < NB:
                        if known != -1:
                            sp.wait_ge(max_ready, i * 16 + 16)
                            sp.wait_ge(qsc_in, i * 16 + 16)
                        load_q(i + 2, p)
                        stack_k(0, i + 2, p, None if known == -1 else (i * 2 + 1) * KT + 1)
                    if known is None or known + 3 < NB:
                        sp.wait_ge(v_done, (i + 1) * 4 + 4)
                        load_ctx(i + 3, 1 - p)
                    if known is None or known + 2 < NB:
                        stack_k(1, i + 2, p, None if known == -1 else (i * 2 + 2) * KT)

                iterations(sp, body)
            with sp.Else():
                def body(b, r, half, known):
                    if known != 0:
                        sp.wait_ge(v_done, b * 4)
                        load_ctx(b, 0)
                        sp.wait_ge(max_red, b * 16)
                        sp.wait_ge(qsc_in, b * 16)
                        load_q(b, 0)
                    for a in range(2):
                        sp.dma_start(mask_q[64 * a:64 * a + 64, :], mask_d[b, :, :]).then_inc(mask_in, 16)
                    if known != 0:
                        sp.wait_ge(arg_done, b * (2 * KT))
                    sp.dma_start(mask_k[:, 0:KT - 1, :], maskT_d[b, 0:(KT - 1) * P, :].rearrange(
                        "(t p) q -> p t q", p=P)).then_inc(mask_kin, 16)
                    sp.dma_start(mask_k[0:KLAST, KT - 1, :], maskT_d[b, (KT - 1) * P:SK, :]).then_inc(mask_kin, 16)
                    if known != 0:
                        sp.wait_ge(score_ready, b * (2 * KT))
                    sp.wait_ge(qmax_in, b * 32 + 32)
                    copy_q(0)
                    if known != 0:
                        stack_k(0, b, 0, None)
                        stack_k(1, b, 0, None)

                batches(sp, body)
            sp.wait_ge(att_done, 2 * NB)

        def split_k(pool, b, j):
            lo, hi = CH[j]
            w = hi - lo
            pool.wait_ge(k_evac, b * 4 + (j + 1))
            nc.gpsimd.tensor_tensor(krest[j % 2][:, 0:w], kf[j % 2][:, 0:w], kparts[:, 0, lo:hi], ALU.subtract)\
                .then_inc(k_chain, 1)
            nc.gpsimd.tensor_tensor(kparts[:, 1, lo:hi], kf[j % 2][:, 0:w], kparts[:, 0, lo:hi], ALU.subtract)\
                .then_inc(k_chain, 1)
            pool.wait_ge(k_chain, b * 8 + (2 * j + 2))
            nc.gpsimd.tensor_tensor(kparts[:, 2, lo:hi], krest[j % 2][:, 0:w], kparts[:, 1, lo:hi], ALU.subtract)\
                .then_inc(k_split, 1)

        def pool_program(pool):
            query.gpsimd(pool)
            for j in range(NCH):
                split_k(pool, 0, j)
            pool.wait_ge(k_split, NCH)
            pool.memset(kst_flat[0][ROWS:P, :].bitcast(F32), TWO_ONES).then_inc(ones_in, 1)
            pool.wait_ge(ones_in, 1)
            pool.wait_ge(query.fmin_done, 1)
            pool.wait_ge(query.fsum_done, 1)
            pool.memset(kst_flat[1][ROWS:P, :].bitcast(F32), TWO_ONES).then_inc(ones_in, 1)
            with pool.If(query.all_true(pool)):
                def body(i, r, p, known):
                    if known is None or known + 2 < NB:
                        for j in range(NCH):
                            split_k(pool, i + 2, j)

                iterations(pool, body)
            with pool.Else():
                def body(b, r, half, known):
                    for j in range(NCH if known != 0 else 0):
                        split_k(pool, b, j)

                batches(pool, body)

        def scalar_program(act):
            def evac_k(b, j, known, bank=misc):
                lo, hi = CH[j]
                w = hi - lo
                act.wait_ge(k_done, b * 4 + (j + 1))
                if not (known is not None and known == 0 and j < 2):
                    act.wait_ge(k_split, b * 4 + (j - 1))
                if j % 2 == 0 and known != 0:
                    act.wait_ge(kst_in[j // 2], b * 96)
                nc.scalar.activation(kf[j % 2][:, 0:w], bank[:, 0:w], ACT.Identity, bias=bk[:, 0:1])
                nc.scalar.activation(kparts[:, 0, lo:hi], bank[:, 0:w], ACT.Identity, bias=bk[:, 0:1])\
                    .then_inc(k_evac, 1)

            def evac_m(b, h, p, known):
                act.wait_ge(mrow_done, b * 2 + (h + 1))
                nc.scalar.activation(qsc[p][ROWS:ROWS + MROWS, h * 512:h * 512 + 512],
                                     misc[ROWS:ROWS + MROWS, :], ACT.Copy).then_inc(mrow_evac, 1)

            act.wait_ge(w_in, 48)
            for j in range(2):
                evac_k(0, j, 0, (misc, pvps)[j % 2])
            query.scalar(act)
            for j in range(2, NCH):
                evac_k(0, j, 0, (misc, pvps)[j % 2])
            with act.If(query.all_true(act)):
                def body(i, r, p, known):
                    for t in range(KT):
                        n = keys_of(t)
                        for h in range(2 if known != -1 else 0):
                            act.wait_ge(score_ready, i * (2 * KT) + (2 * t + h + 1))
                            if not (known == 0 and t < 2):
                                act.wait_ge(pv_done, i * KT + (t - 1))
                            nc.scalar.activation(probs[(t + p) % 2][0:n, h * 512:h * 512 + 512], score[h][0:n, :],
                                                 ACT.Exp).then_inc(exp_done, 1)
                        if t in MISC and wanted(*MISC[t][0:2], known):
                            kind, stage, num = MISC[t]
                            if kind == "k":
                                evac_k(i + stage, num, None)
                            if kind == "m":
                                evac_m(i + stage, num, 1 - p, None)

                iterations(act, body)
            with act.Else():
                def body(b, r, half, known):
                    for j in range(NCH if known != 0 else 0):
                        evac_k(b, j, known)
                    for h in range(2):
                        evac_m(b, h, 0, known)
                    for h in range(2):
                        act.wait_ge(fill_done, b * 2 + (h + 1))
                        nc.scalar.activation(fill[:, h * 512:h * 512 + 512], misc[:, :], ACT.Identity, bias=tiny[:, 0:1])\
                            .then_inc(fill_evac, 1)
                    for t in range(KT):
                        n = keys_of(t)
                        for h in range(2):
                            act.wait_ge(arg_done, b * (2 * KT) + (2 * t + h + 1))
                            if not (known == 0 and t == 0):
                                act.wait_ge(pv_done, b * KT + t)
                            nc.scalar.activation(probs[t % 2][0:n, h * 512:h * 512 + 512],
                                                 arg[0:n, h * 512:h * 512 + 512], ACT.Exp).then_inc(exp_done, 1)

                batches(act, body)

        def vector_program(dve):
            def reduce_step(b, s):
                dve.wait_ge(max_ready, b * 16 + (s + 1))
                nc.vector.tensor_reduce(mx2[:, s // 8, s % 8:s % 8 + 1], maxps[s % 2][:, :, 0:MW], AX.XY, ALU.max)\
                    .then_inc(max_red, 1)

            def split_m(b, known):
                dve.wait_ge(max_red, b * 16 + 16)
                nc.vector.tensor_tensor(mx[:, :], mx2[:, 0, :], mx2[:, 1, :], ALU.max).then_inc(m_chain, 1)
                if known != 0:
                    dve.wait_ge(mrow_done, b * 2)
                dve.wait_ge(m_chain, b * 4 + 1)
                nc.vector.tensor_scalar(mparts[:, :, 0], mx[:, :], -1.0, None, ALU.mult).then_inc(m_chain, 1)
                dve.wait_ge(m_chain, b * 4 + 2)
                nc.vector.scalar_tensor_tensor(out=mrest[:, :], in0=mx[:, :], scalar=-1.0, in1=mparts[:, :, 0],
                                               op0=ALU.mult, op1=ALU.subtract).then_inc(m_chain, 1)
                dve.wait_ge(m_chain, b * 4 + 3)
                nc.vector.tensor_copy(mparts[:, :, 1], mrest[:, :]).then_inc(m_chain, 1)
                dve.wait_ge(m_chain, b * 4 + 4)
                nc.vector.tensor_tensor(mparts[:, :, 2], mrest[:, :], mparts[:, :, 1], ALU.subtract)\
                    .then_inc(m_parts, 1)

            def evac_v(b, g, p, used):
                t0, t1 = VG[g]
                n = keys_of(t1 - 1)
                dve.wait_ge(v_done, b * 4 + (g + 1))
                if used is not None:
                    dve.wait_ge(pv_done, used)
                nc.vector.tensor_copy(
                    v[p][0:n, t0:t1, :, 0:2 * DH],
                    misc[0:n, 0:(t1 - t0) * P].rearrange("k (t p c) -> k t p c", p=NPAIR, c=2 * DH))\
                    .then_inc(v_evac, 1)

            def copy_o(b):
                dve.wait_ge(pv_done, b * KT + KT)
                nc.vector.tensor_copy(oT[:, :], pvps[:, 0:2 * P]).then_inc(oT_copied, 1)

            def norm_o(b, r, p):
                back = misc[:, 0:2 * P].rearrange("k (p c) -> k p c", c=PV_W)
                dve.wait_ge(oT_back, b + 1)
                nc.vector.reciprocal(rec[:, :], back[:, :, ONE_COL]).then_inc(rec_done, 1)
                dve.wait_ge(rec_done, b + 1)
                for a in range(2):
                    dst = att[64 * p:64 * p + 64, bass.ds(r * D, D)].rearrange("q (p a d) -> q p a d", a=2, d=DH)
                    nc.vector.tensor_tensor(
                        dst[:, :, a, :], back[64 * a:64 * a + 64, :, a * DH:(a + 1) * DH],
                        rec[64 * a:64 * a + 64, :].unsqueeze(2).to_broadcast([64, NPAIR, DH]),
                        ALU.mult).then_inc(att_done, 1)

            for p in range(2):
                last = nc.vector.memset(qmax[p][:, :].bitcast(F32), 0.0)
            last.then_inc(cst, 1)
            for p in range(2):
                nc.vector.memset(v[p][:, :, :, ONE_COL], 1.0)
                last = nc.vector.memset(v[p][:, :, :, ONE_COL + 1:PV_W], 0.0)
            last.then_inc(cst, 1)
            nc.vector.memset(tiny[:, :], 1e-9).then_inc(cst, 1)
            query.vector(dve)
            for g in range(2):
                evac_v(0, g, 0, None)
            query.check_mask(dve)
            with dve.If(query.all_true(dve)):
                for s in sum(EARLY_STEPS.values(), []):
                    reduce_step(0, s)

                def body(i, r, p, known):
                    for t in range(KT):
                        if t == 0 and (known is None or known > 0):
                            copy_o(i - 1)
                        if t == SPLIT_SLOT and (known is None or known + 1 < NB):
                            split_m(i + 1, 0 if known == -1 else None)
                        if t in MISC and wanted(*MISC[t][0:2], known):
                            kind, stage, num = MISC[t]
                            if kind == "v":
                                used = None if known is not None and known + stage < 2 else \
                                    (i + (stage - 2)) * KT + VG[num][1]
                                evac_v(i + stage, num, (p + stage) % 2, used)
                            if kind == "o":
                                norm_o(i - 1, r if p == 1 else r - 1, 1 - p)
                        if known is None or known + 1 < NB:
                            for s in MAX_STEPS.get(t, ()):
                                reduce_step(i + 1, s)
                        if known is None or known + 2 < NB:
                            for s in EARLY_STEPS.get(t, ()):
                                reduce_step(i + 2, s)

                iterations(dve, body)
                copy_o(NB - 1)
                norm_o(NB - 1, NB // 2 - 1, 1)
            with dve.Else():
                def body(b, r, half, known):
                    for g in range(0 if known != 0 else 2, 4):
                        evac_v(b, g, 0, None if known == 0 else b * KT)
                    dve.wait_ge(mask_in, b * 32 + 32)
                    for s in range(16):
                        if not (known == 0 and s == 0):
                            dve.wait_ge(max_red, b * 16 + s)
                        nc.vector.memset(picked[:, :, :], 1e-9).then_inc(pick_fill, 1)
                        dve.wait_ge(pick_fill, b * 16 + (s + 1))
                        dve.wait_ge(max_ready, b * 16 + (s + 1))
                        nc.vector.tensor_copy(held[:, :], tiny[:, :])
                        for c in range(2):
                            lo = 400 * (2 * (s // 8) + c)
                            last = nc.vector.copy_predicated(picked[:, c, :], mask_q[:, lo:lo + MW],
                                                             maxps[s % 2][:, c, 0:MW])
                        last.then_inc(pick_done, 1)
                        dve.wait_ge(pick_done, b * 16 + (s + 1))
                        nc.vector.tensor_reduce(mx2[:, s // 8, s % 8:s % 8 + 1], picked[:, :, :], AX.XY, ALU.max)\
                            .then_inc(max_red, 1)
                    split_m(b, known)
                    dve.wait_ge(mask_kin, b * 32 + 32)
                    for t in range(KT):
                        n = keys_of(t)
                        for h in range(2):
                            at = lambda a: a[0:n, :].rearrange("k (h q) -> k h q", q=SQ)
                            hs = slice(h * 512, h * 512 + 512)
                            k = 2 * t + h
                            if not (known == 0 and t == 0):
                                dve.wait_ge(exp_done, b * (2 * KT) + (k - 1))
                            dve.wait_ge(fill_evac, b * 2 + (h + 1))
                            nc.vector.tensor_copy(arg[0:n, hs], fill[0:n, hs]).then_inc(arg_fill, 1)
                            dve.wait_ge(arg_fill, b * (2 * KT) + (k + 1))
                            dve.wait_ge(score_ready, b * (2 * KT) + (k + 1))
                            nc.vector.tensor_copy(held[:, :], tiny[:, :])
                            nc.vector.copy_predicated(
                                at(arg[:, hs]), mask_k[0:n, t, :].unsqueeze(1).to_broadcast([n, 8, SQ]),
                                at(score[h])).then_inc(arg_done, 1)
                    copy_o(b)
                    norm_o(b, r, half)

                batches(dve, body)

        def tensor_program(pe):
            def k_proj(b, rb, j, p, bank=misc):
                lo, hi = CH[j]
                if j == 0:
                    pe.wait_ge(ctx_in[p], rb * 16 + 16)
                nc.tensor.matmul(bank[:, 0:hi - lo], wk[:, :], ctxT[p][:, lo:hi], start=True, stop=True)\
                    .then_inc(k_done, 1)

            def v_proj(b, g, p):
                t0, t1 = VG[g]
                for t in range(t0, t1):
                    n = keys_of(t)
                    last = nc.tensor.matmul(misc[0:n, (t - t0) * P:(t - t0 + 1) * P],
                                            ctxT[p][:, t * P:t * P + n], wv[:, :], start=True, stop=True)
                last.then_inc(v_done, 1)

            def max_step(b, s, p, known):
                pair, half = s % 8, s // 8
                if s == 0:
                    pe.wait_ge(qmax_in, b * 32 + 32)
                if s % 8 == 0:
                    pe.wait_ge(kst_in[half], b * 96 + 96)
                if not (known == 0 and s < 2):
                    pe.wait_ge(max_red, b * 16 + (s - 1))
                for c in range(2):
                    lo = 400 * (2 * half + c)
                    last = nc.tensor.matmul(maxps[s % 2][:, c, 0:MW], qmax[p][0:ROWS, pair * P:(pair + 1) * P],
                                            kst[p][0:ROWS, pair, lo:lo + MW], start=True, stop=True)
                last.then_inc(max_ready, 1)

            def m_rows(b, h):
                pe.wait_ge(m_parts, b + 1)
                for j in range(4):
                    last = nc.tensor.matmul(misc[ROWS:ROWS + MROWS, j * P:(j + 1) * P], mparts[:, 4 * h + j, :],
                                            ident_b[:, :], start=True, stop=True)
                last.then_inc(mrow_done, 1)

            def scores(i, t, p, known):
                n = keys_of(t)
                for h in range(2):
                    if t == 0:
                        pe.wait_ge(mrow_evac, i * 2 + (h + 1))
                        pe.wait_ge(qsc_in, i * 16 + 16)
                    if not (known == 0 and t == 0):
                        pe.wait_ge(exp_done, i * (2 * KT) + (2 * t + h - 1))
                    for j in range(4):
                        pair = 4 * h + j
                        last = nc.tensor.matmul(score[h][0:n, j * P:(j + 1) * P],
                                                kst[p][0:ROWS + MROWS, pair, t * P:t * P + n],
                                                qsc[p][0:ROWS + MROWS, pair * P:(pair + 1) * P],
                                                start=True, stop=True)
                    last.then_inc(score_ready, 1)

            def p_v(i, t, p, known):
                n = keys_of(t)
                for g, (t0, _) in enumerate(VG):
                    if t == t0:
                        pe.wait_ge(v_evac, i * 4 + (g + 1))
                if t == 0 and known != 0:
                    pe.wait_ge(oT_copied, i)
                for pair in range(NPAIR):
                    g, r = pair % 4, pair // 4
                    if pair % 4 == 0:
                        pe.wait_ge(exp_done, i * (2 * KT) + (2 * t + r + 1))
                    last = nc.tensor.matmul(pvps[32 * g:32 * g + PV_W, r * P:(r + 1) * P], v[p][0:n, t, pair, :],
                                            probs[(t + p) % 2][0:n, pair * P:(pair + 1) * P],
                                            start=(t == 0 and r == 0), stop=(t == KT - 1), skip_group_check=True)
                last.then_inc(pv_done, 1)

            def o_back(b):
                pe.wait_ge(oT_copied, b + 1)
                for r in range(2):
                    last = nc.tensor.transpose(misc[:, r * P:(r + 1) * P], oT[:, r * P:(r + 1) * P], ident[:, :])
                last.then_inc(oT_back, 1)

            pe.wait_ge(w_in, 48)
            for j in range(2):
                k_proj(0, 0, j, 0, (misc, pvps)[j % 2])
            query.tensor(pe)
            for j in range(2, NCH):
                pe.wait_ge(k_evac, j - 1)
                k_proj(0, 0, j, 0, (misc, pvps)[j % 2])
            pe.wait_ge(k_evac, 3)
            v_proj(0, 0, 0)
            evacuated(pe, "v", 0, 0)
            v_proj(0, 1, 0)
            query.count_true(pe)
            with pe.If(query.all_true(pe)):
                pe.wait_ge(ones_in, 2)
                pe.wait_ge(cst, 3)
                for s in sum(EARLY_STEPS.values(), []):
                    max_step(0, s, 0, 0)

                def body(i, r, p, known):
                    for t in range(KT):
                        if known != -1:
                            scores(i, t, p, known)
                        if t > 0 and known != -1:
                            p_v(i, t - 1, p, known)
                        elif t == 0 and (known is None or known > 0):
                            p_v(i - 1, KT - 1, 1 - p, None)
                        if t in MISC and wanted(*MISC[t][0:2], known):
                            kind, stage, num = MISC[t]
                            pk, pst, pn = previous_use(t, known)
                            evacuated(pe, pk, i + pst, pn)
                            if kind == "k":
                                k_proj(i + 2, r + 1, num, p)
                            elif kind == "v":
                                v_proj(i + stage, num, (p + stage) % 2)
                            elif kind == "o":
                                o_back(i - 1)
                            else:
                                m_rows(i + 1, num)
                        if known is None or known + 1 < NB:
                            for s in MAX_STEPS.get(t, ()):
                                max_step(i + 1, s, 1 - p, None)
                        if known is None or known + 2 < NB:
                            for s in EARLY_STEPS.get(t, ()):
                                max_step(i + 2, s, p, None)

                iterations(pe, body)
                p_v(NB - 1, KT - 1, 1, None)
                o_back(NB - 1)
            with pe.Else():
                def body(b, r, half, known):
                    prev = ("v", 0, 1) if known == 0 else ("o", b - 1, 0)
                    work = [("k", j) for j in range(NCH)] + [("v", g) for g in range(4)]
                    for kind, n in work[NCH + 2:] if known == 0 else work:
                        evacuated(pe, *prev)
                        if kind == "k":
                            k_proj(b, b, n, 0)
                        else:
                            v_proj(b, n, 0)
                        prev = (kind, b, n)
                    pe.wait_ge(ones_in, 2)
                    pe.wait_ge(cst, 3)
                    for s in range(16):
                        max_step(b, s, 0, known)
                    evacuated(pe, *prev)
                    m_rows(b, 0)
                    evacuated(pe, "m", b, 0)
                    m_rows(b, 1)
                    evacuated(pe, "m", b, 1)
                    for h in range(2):
                        if h:
                            pe.wait_ge(fill_evac, b * 2 + 1)
                        nc.tensor.matmul(misc[:, :], kst[0][ROWS:ROWS + MROWS, 0, 0:P],
                                         qsc[0][ROWS:ROWS + MROWS, h * 512:h * 512 + 512],
                                         start=True, stop=True).then_inc(fill_done, 1)
                    for t in range(KT):
                        scores(b, t, 0, known)
                        p_v(b, t, 0, known)
                    pe.wait_ge(fill_evac, b * 2 + 2)
                    o_back(b)

                batches(pe, body)

        block = ctx.enter_context(nc.Block())

        @block.sync
        def _(sp):
            sync_program(sp)

        @block.gpsimd
        def _(pool):
            pool_program(pool)

        @block.scalar
        def _(act):
            scalar_program(act)

        @block.vector
        def _(dve):
            vector_program(dve)

        @block.tensor
        def _(pe):
            tensor_program(pe)


def self_attention(nc, w, keep):
    (x_sb, att, xn3T, ident, late_in) = keep
    NG, GT = 4, 4
    QK, VV = 3 * D, 2 * D
    G8 = QK // DH
    with ExitStack() as ctx:
        sb = lambda n, s: ctx.enter_context(nc.sbuf_tensor(n, s, F32))
        psb = lambda n: ctx.enter_context(nc.psum_tensor(n, [P, 512], F32))
        sem = lambda n: ctx.enter_context(nc.semaphore(n))
        attT, xn1, xnT = sb("attT", [P, TOK]), sb("xn1", [P, NT, D]), sb("xnT1", [P, TOK])
        y, vv = sb("y", [P, NT, QK]), sb("vv", [P, NT, VV])
        th, sq = sb("th", [P, NT, QK]), sb("sq", [P, GT, QK])
        ss, nrm = sb("ss", [P, NT, G8]), sb("nrm", [P, NT, G8])
        st = sb("st", [P, 2, 2, D])
        state = sb("state", [P, NT, 2, D])
        qT, on, onT = sb("qT", [P, TOK]), sb("on", [P, NT, D]), sb("onT", [P, TOK])
        stats, mv = sb("stats1", [P, 3, NT, 6]), sb("mv1", [P, 3, NT, 2])
        rstd, epsv, minus_half = sb("rstd1", [P, 3, NT]), sb("epsv", [P, GT]), sb("minus_half", [P, GT])
        wsum = sb("wsum", [P, 5 * D])
        psT = [psb(f"psT{i}") for i in range(2)]
        psM = [psb(f"psM{i}") for i in range(2)]
        psQ, psV = psb("psQ"), psb("psV")
        psG = [psb(f"psG{i}") for i in range(2)]
        t_done, t_evac = sem("t_done"), sem("t_evac")
        m_done, m_evac = sem("m_done"), sem("m_evac")
        p_done, y_done, v_done = sem("p_done"), sem("y_done"), sem("vv_done")
        stat_done, var_done, rstd_done = sem("stat1"), sem("var1"), sem("rstd1_done")
        eps_add = sem("eps_add")
        n_done, cst, xb_done, x1b_done, wsum_done = sem("n_done"), sem("cst2"), sem("xb_done"), sem("x1b_done"), sem("wsum_done")
        th_done, w_done, sq_done, ss_done, root_done, nrm_add, inv_done, k_ready = (
            sem("th_done"), sem("w_done"), sem("sq_done"), sem("ss_done"), sem("root_done"), sem("nrm_add"),
            sem("inv_done"), sem("k_ready"))
        g_done, st1, state_done, res_done = sem("g_done"), sem("st1"), sem("state_done"), sem("res_done")
        block = ctx.enter_context(nc.Block())
        g_of = lambda t, b: (psG if t % 2 == 0 else (psQ, psV))[b]
        cols = lambda t: slice(t * P, (t + 1) * P)
        tiles = lambda g: range(GT * g, GT * g + GT)
        grp = lambda g: slice(GT * g, GT * g + GT)

        @block.gpsimd
        def _(pool):
            pool.memset(epsv[:, :], EPS).then_inc(cst, 1)
            pool.memset(minus_half[:, :], -0.5).then_inc(cst, 1)
            pool.wait_ge(late_in, LATE)
            for t in range(NT):
                last = nc.gpsimd.tensor_tensor(x_sb[:, t, :], x_sb[:, t, :], w["x_bo"][:, :], ALU.add)
                if t % GT == GT - 1:
                    last.then_inc(xb_done, 1)
            pool.wait_ge(cst, 2)

            def rstds(rnd):
                for g in range(NG):
                    n = rnd * NG + g
                    pool.wait_ge(var_done, (n + 1) * GT)
                    nc.gpsimd.tensor_tensor(rstd[:, rnd, grp(g)], mv[:, rnd, grp(g), 1], epsv[:, :], ALU.add)\
                        .then_inc(eps_add, 1)
                    pool.wait_ge(eps_add, n + 1)
                    nc.gpsimd.tensor_tensor(rstd[:, rnd, grp(g)], rstd[:, rnd, grp(g)], minus_half[:, :], ALU.pow)\
                        .then_inc(rstd_done, 1)

            rstds(0)
            for g in range(NG):
                pool.wait_ge(n_done, g + 1)
                for t in tiles(g):
                    last = nc.gpsimd.tensor_tensor(x_sb[:, t, :], x_sb[:, t, :], w["a_bo"][:, :], ALU.add)
                last.then_inc(x1b_done, 1)
            rstds(1)
            rstds(2)
            for g in range(NG):
                pool.wait_ge(n_done, 2 * NG + g + 1)
                nc.gpsimd.tensor_tensor(x_sb[:, grp(g), :], x_sb[:, grp(g), :], on[:, grp(g), :], ALU.add)\
                    .then_inc(res_done, 1)

        @block.scalar
        def _(act):
            act.wait_ge(late_in, LATE)

            def out_of_psT(n, dst, scale=None, bias=None):
                act.wait_ge(t_done, n + 1)
                if bias is None:
                    nc.scalar.activation(dst, psT[n % 2][:, :], ACT.Copy).then_inc(t_evac, 1)
                elif scale is None:
                    nc.scalar.activation(dst, psT[n % 2][:, :], ACT.Identity, bias=bias).then_inc(t_evac, 1)
                else:
                    nc.scalar.activation(dst, psT[n % 2][:, :], ACT.Identity, bias=bias, scale=scale).then_inc(t_evac, 1)

            part = lambda a, g: a[:, 512 * g:512 * g + 512]
            for g in range(NG):
                out_of_psT(g, part(attT, g), bias=w["x_bv"][:, 0:1])
            for g in range(NG):
                out_of_psT(NG + g, part(xnT, g))
            for g in range(NG):
                act.wait_ge(y_done, (g + 1) * GT)
                nc.scalar.activation(th[:, grp(g), :], y[:, grp(g), :], ACT.Tanh, scale=0.5).then_inc(th_done, 1)
            for g in range(NG):
                act.wait_ge(w_done, g + 1)
                if g >= 1:
                    act.wait_ge(ss_done, g)
                nc.scalar.activation(sq[:, :, :], y[:, grp(g), :], ACT.Square, bias=1.0).then_inc(sq_done, 1)
            for g in range(NG):
                act.wait_ge(ss_done, g + 1)
                nc.scalar.activation(nrm[:, grp(g), :], ss[:, grp(g), :], ACT.Sqrt).then_inc(root_done, 1)
            for g in range(NG):
                out_of_psT(2 * NG + g, part(qT, g))
            for g in range(NG):
                out_of_psT(3 * NG + g, part(onT, g), scale=w["ln_g"][:, 0:1], bias=w["ln_b"][:, 0:1])
            for g in range(NG):
                out_of_psT(4 * NG + g, part(xn3T, g))

        @block.vector
        def _(dve):
            dve.wait_ge(late_in, LATE)
            for j in range(5):
                last = nc.vector.tensor_tensor(wsum[:, cols(j)], w["w5"][:, cols(j)], ident[:, :], ALU.add)
            last.then_inc(wsum_done, 1)

            def statistics(rnd, g, src):
                n = rnd * NG + g
                for t in tiles(g):
                    nc.vector.bn_stats(stats[:, rnd, t, :], src(t)).then_inc(stat_done, 1)
                dve.wait_ge(stat_done, (n + 1) * GT)
                for t in tiles(g):
                    nc.vector.bn_aggr(mv[:, rnd, t, :], stats[:, rnd, t, :]).then_inc(var_done, 1)

            def normalise(rnd, g, src, dst):
                n = rnd * NG + g
                dve.wait_ge(rstd_done, n + 1)
                for t in tiles(g):
                    last = nc.vector.tensor_scalar(dst[:, t, :], src(t), mv[:, rnd, t, 0:1], rstd[:, rnd, t:t + 1],
                                                   ALU.subtract, ALU.mult)
                last.then_inc(n_done, 1)

            for g in range(NG):
                dve.wait_ge(m_done, g + 1)
                dve.wait_ge(xb_done, g + 1)
                nc.vector.tensor_tensor(x_sb[:, grp(g), :], psM[g % 2][:, :].rearrange("p (t d) -> p t d", d=D),
                                        x_sb[:, grp(g), :], ALU.add).then_inc(m_evac, 1)
                dve.wait_ge(m_evac, g + 1)
                statistics(0, g, lambda t: x_sb[:, t, :])
            for g in range(NG):
                normalise(0, g, lambda t: x_sb[:, t, :], xn1)
            for t in range(NT):
                dve.wait_ge(p_done, t + 1)
                nc.vector.tensor_tensor(y[:, t, :], psQ[:, 0:QK], w["b5"][:, 0:QK], ALU.add).then_inc(y_done, 1)
                nc.vector.tensor_tensor(vv[:, t, :], psV[:, 0:VV], w["b5"][:, QK:QK + VV], ALU.add).then_inc(v_done, 1)
            for g in range(NG):
                dve.wait_ge(th_done, g + 1)
                nc.vector.scalar_tensor_tensor(out=y[:, grp(g), :], in0=th[:, grp(g), :], scalar=1.0,
                                               in1=y[:, grp(g), :], op0=ALU.add, op1=ALU.mult).then_inc(w_done, 1)
            for g in range(NG):
                dve.wait_ge(sq_done, g + 1)
                nc.vector.tensor_reduce(ss[:, grp(g), :].rearrange("p t h -> p (t h)"),
                                        sq[:, :, :].rearrange("p t (h d) -> p (t h) d", d=DH), AX.X, ALU.add)\
                    .then_inc(ss_done, 1)
            for g in range(NG):
                dve.wait_ge(root_done, g + 1)
                flat = nrm[:, grp(g), :].rearrange("p t h -> p (t h)")
                nc.vector.tensor_scalar(flat, flat, 2e-6, None, ALU.add).then_inc(nrm_add, 1)
            for g in range(NG):
                dve.wait_ge(nrm_add, g + 1)
                flat = nrm[:, grp(g), :].rearrange("p t h -> p (t h)")
                nc.vector.reciprocal(flat, flat).then_inc(inv_done, 1)
            for g in range(NG):
                dve.wait_ge(inv_done, g + 1)
                heads = y[:, grp(g), :].rearrange("p t (h d) -> p (t h) d", d=DH)
                flat = nrm[:, grp(g), :].rearrange("p t h -> p (t h)")
                nc.vector.scalar_tensor_tensor(
                    out=heads, in0=heads, scalar=1.0, in1=flat.unsqueeze(2).to_broadcast([P, GT * G8, DH]),
                    op0=ALU.add, op1=ALU.mult).then_inc(k_ready, 1)
            for t in range(NT):
                dve.wait_ge(g_done, t + 1)
                gram = [g_of(t, b)[:, 0:2 * D].rearrange("p (k e) -> p k e", k=2) for b in range(2)]
                if t >= 2:
                    dve.wait_ge(state_done, t - 1)
                for b in range(2):
                    last = nc.vector.tensor_tensor(st[:, t % 2, b, :], gram[b][:, 0, :], w["blocks"][:, :], ALU.mult)
                last.then_inc(st1, 1)
                dve.wait_ge(st1, t + 1)
                for b in range(2):
                    last = nc.vector.tensor_tensor(state[:, t, b, :], gram[b][:, 1, :], st[:, t % 2, b, :], ALU.mult)
                last.then_inc(state_done, 1)
            for g in range(NG):
                dve.wait_ge(m_done, NG + g + 1)
                statistics(1, g, lambda t: psM[g % 2][:, cols(t % GT)])
                normalise(1, g, lambda t: psM[g % 2][:, cols(t % GT)], on)
            for g in range(NG):
                dve.wait_ge(m_done, 2 * NG + g + 1)
                dve.wait_ge(x1b_done, g + 1)
                nc.vector.tensor_tensor(x_sb[:, grp(g), :], psM[g % 2][:, :].rearrange("p (t d) -> p t d", d=D),
                                        x_sb[:, grp(g), :], ALU.add).then_inc(m_evac, 1)
                dve.wait_ge(m_evac, NG + g + 1)
                statistics(2, g, lambda t: x_sb[:, t, :])
            dve.wait_ge(t_done, 4 * NG)
            for g in range(NG):
                normalise(2, g, lambda t: x_sb[:, t, :], on)

        @block.tensor
        def _(pe):
            pe.wait_ge(late_in, LATE)

            def into_psT(n, src, g):
                if n >= 2:
                    pe.wait_ge(t_evac, n - 1)
                for t in tiles(g):
                    last = nc.tensor.transpose(psT[n % 2][:, cols(t % GT)], src(t), ident[:, :])
                last.then_inc(t_done, 1)

            def into_psM(read_out, lhsT, rhs, g, ready):
                if g >= 2:
                    pe.wait_ge(m_evac, read_out + g - 1)
                pe.wait_ge(t_evac, ready)
                for t in tiles(g):
                    last = nc.tensor.matmul(psM[g % 2][:, cols(t % GT)], lhsT[:, cols(t)], rhs, start=True, stop=True)
                last.then_inc(m_done, 1)

            for g in range(NG):
                into_psT(g, lambda t: att[:, cols(t)], g)
                if g:
                    into_psM(0, attT, w["x_wo"][:, :], g - 1, g)
            into_psM(0, attT, w["x_wo"][:, :], NG - 1, NG)
            for g in range(NG):
                pe.wait_ge(n_done, g + 1)
                into_psT(NG + g, lambda t: xn1[:, t, :], g)
            pe.wait_ge(wsum_done, 1)
            for t in range(NT):
                pe.wait_ge(t_evac, NG + t // GT + 1)
                if t:
                    pe.wait_ge(y_done, t)
                nc.tensor.matmul(psQ[:, 0:QK], xnT[:, cols(t)], wsum[:, 0:QK], start=True, stop=True)
                if t:
                    pe.wait_ge(v_done, t)
                nc.tensor.matmul(psV[:, 0:VV], xnT[:, cols(t)], wsum[:, QK:QK + VV], start=True, stop=True)\
                    .then_inc(p_done, 1)
            for g in range(NG):
                pe.wait_ge(k_ready, g + 1)
                into_psT(2 * NG + g, lambda t: y[:, t, 0:D], g)
            for t in range(NT):
                if t >= 2:
                    pe.wait_ge(state_done, t - 1)
                for k in range(2):
                    for b in range(2):
                        rows = slice(64 * b, 64 * b + 64)
                        last = nc.tensor.matmul(g_of(t, b)[:, k * D:(k + 1) * D],
                                                y[rows, t, (1 + k) * D:(2 + k) * D], vv[rows, t, k * D:(k + 1) * D],
                                                start=True, stop=True)
                last.then_inc(g_done, 1)
            for g in range(NG):
                pe.wait_ge(t_evac, 2 * NG + g + 1)
                pe.wait_ge(state_done, GT * (g + 1))
                if g < 2:
                    pe.wait_ge(m_evac, NG + g - 1)
                else:
                    pe.wait_ge(n_done, NG + g - 1)
                for t in tiles(g):
                    for b in range(2):
                        last = nc.tensor.matmul(psM[g % 2][64 * b:64 * b + 64, cols(t % GT)],
                                                qT[:, t * P + 64 * b:t * P + 64 * b + 64], state[:, t, b, :],
                                                start=True, stop=True)
                last.then_inc(m_done, 1)
            for g in range(NG):
                pe.wait_ge(n_done, NG + g + 1)
                into_psT(3 * NG + g, lambda t: on[:, t, :], g)
            for g in range(NG):
                into_psM(NG, onT, w["a_wo"][:, :], g, 3 * NG + g + 1)
            for g in range(NG):
                pe.wait_ge(n_done, 2 * NG + g + 1)
                into_psT(4 * NG + g, lambda t: on[:, t, :], g)


def experts(nc, w, keep, w_up_d, w_dn_d, out_d):
    (x_sb, xn3T, wup, wdn) = keep
    TB = TOK // 512
    with ExitStack() as ctx:
        sb = lambda n, s: ctx.enter_context(nc.sbuf_tensor(n, s, F32))
        psb = lambda n: ctx.enter_context(nc.psum_tensor(n, [P, 512], F32))
        sem = lambda n: ctx.enter_context(nc.semaphore(n))
        hT = [sb(f"hT{i}", [P, IC, 512]) for i in range(2)]
        acc = sb("acc", [P, NT, D])
        logit, ex, pr = sb("logit", [P, NT, E]), sb("ex", [P, NT, E]), sb("pr", [P, NT, E])
        top, tot, rtot = sb("top", [P, NT]), sb("tot", [P, NT]), sb("rtot", [P, NT])
        above, ties, rank = sb("above", [P, NT, E, E]), sb("ties", [P, NT, E, E]), sb("rank", [P, NT, E])
        kept, tot2, sw = sb("kept", [P, NT, E]), sb("tot2", [P, NT]), sb("sw", [P, NT * E])
        swe = [sb(f"swe{i}", [P, NT]) for i in range(2)]
        stats, mv = sb("stats3", [P, NT, 6]), sb("mv3", [P, NT, 2])
        rstd, epsv, minus_half = sb("rstd3", [P, NT]), sb("epsv3", [P, 4]), sb("minus_half3", [P, 4])
        ps_up = [psb(f"ps_up{i}") for i in range(4)]
        ps_dn = [psb(f"ps_dn{i}") for i in range(2)]
        ps_gate = psb("ps_gate")
        up_in = [sem("up_in0"), sem("up_in1")]
        gate_done, exp_done, chain, swe_done = sem("gate_done"), sem("gexp_done"), sem("gate_chain"), sem("swe_done")
        up_done, gelu_done, dn_done, acc_done = sem("up_done"), sem("gelu_done"), sem("dn_done"), sem("acc_done")
        sub_done, cst, eps_add, rstd_done = sem("sub_done"), sem("cst3"), sem("eps_add3"), sem("rstd3_done")
        stat_done, var_done, n_done, y_done, stored = sem("stat3"), sem("var3"), sem("n3"), sem("y3"), sem("stored")
        block = ctx.enter_context(nc.Block())

        def pairs(eng, body):
            for p in range(2):
                body(p, 0, p, p)
            with eng.Fori(1, E // 2) as r:
                for p in range(2):
                    body(r * 2 + p, r, p, None)

        @block.sync
        def _(sp):
            def body(e, r, p, known):
                if known is None:
                    sp.wait_ge(dn_done, e * TB - TB)
                sp.dma_start(wup[p][:, :], w_up_d[e]).then_inc(up_in[p], 16)
                sp.dma_start(wdn[p][:, :, :], w_dn_d[e].rearrange("(c p) h -> p c h", p=P)).then_inc(up_in[p], 16)

            pairs(sp, body)
            out_v = out_d.rearrange("(t p) d -> p t d", p=P)
            for g in range(4):
                sp.wait_ge(y_done, g + 1)
                sp.dma_start(out_v[:, 4 * g:4 * g + 4, :], acc[:, 4 * g:4 * g + 4, :]).then_inc(stored, 16)
            sp.wait_ge(stored, 64)

        @block.scalar
        def _(act):
            act.wait_ge(sub_done, 1)
            nc.scalar.activation(ex[:, :, :], logit[:, :, :], ACT.Exp).then_inc(exp_done, 1)

            def body(e, r, p, known):
                for tb in range(TB):
                    for c in range(IC):
                        act.wait_ge(up_done, e * (TB * IC) + (tb * IC + c + 1))
                        if c == 0 and not (known == 0 and tb < 2):
                            act.wait_ge(dn_done, e * TB + (tb - 1))
                        nc.scalar.activation(hT[tb % 2][:, c, :], ps_up[c][:, :], ACT.Gelu).then_inc(gelu_done, 1)

            pairs(act, body)

        @block.gpsimd
        def _(pool):
            pool.memset(acc[:, :, :], 0.0).then_inc(cst, 1)
            pool.memset(epsv[:, :], EPS).then_inc(cst, 1)
            pool.memset(minus_half[:, :], -0.5).then_inc(cst, 1)
            pool.wait_ge(cst, 3)
            for g in range(4):
                pool.wait_ge(var_done, 4 * (g + 1))
                s = slice(4 * g, 4 * g + 4)
                nc.gpsimd.tensor_tensor(rstd[:, s], mv[:, s, 1], epsv[:, :], ALU.add).then_inc(eps_add, 1)
                pool.wait_ge(eps_add, g + 1)
                nc.gpsimd.tensor_tensor(rstd[:, s], rstd[:, s], minus_half[:, :], ALU.pow).then_inc(rstd_done, 1)

        @block.vector
        def _(dve):
            steps = [0]

            def then_wait(ins):
                steps[0] += 1
                ins.then_inc(chain, 1)
                dve.wait_ge(chain, steps[0])

            by_e = lambda a: a[:, :].unsqueeze(2).to_broadcast([P, NT, E])
            dve.wait_ge(gate_done, 1)
            then_wait(nc.vector.tensor_tensor(
                logit[:, :, :], ps_gate[:, 0:NT * E].rearrange("p (t e) -> p t e", e=E),
                w["ebias"][:, :].unsqueeze(1).to_broadcast([P, NT, E]), ALU.add))
            then_wait(nc.vector.tensor_reduce(top[:, :], logit[:, :, :], AX.X, ALU.max))
            nc.vector.tensor_tensor(logit[:, :, :], logit[:, :, :], by_e(top), ALU.subtract).then_inc(sub_done, 1)
            dve.wait_ge(exp_done, 1)
            then_wait(nc.vector.tensor_reduce(tot[:, :], ex[:, :, :], AX.X, ALU.add))
            then_wait(nc.vector.reciprocal(rtot[:, :], tot[:, :]))
            then_wait(nc.vector.tensor_tensor(pr[:, :, :], ex[:, :, :], by_e(rtot), ALU.mult))
            of_j = pr[:, :, :].unsqueeze(2).to_broadcast([P, NT, E, E])
            of_e = pr[:, :, :].unsqueeze(3).to_broadcast([P, NT, E, E])
            nc.vector.tensor_tensor(above[:, :, :, :], of_j, of_e, ALU.is_gt)
            then_wait(nc.vector.tensor_tensor(ties[:, :, :, :], of_j, of_e, ALU.is_equal))
            then_wait(nc.vector.tensor_tensor(ties[:, :, :, :].rearrange("p t e j -> p t (e j)"),
                                              ties[:, :, :, :].rearrange("p t e j -> p t (e j)"),
                                              w["before"][:, :].unsqueeze(1).to_broadcast([P, NT, E * E]), ALU.mult))
            then_wait(nc.vector.tensor_tensor(above[:, :, :, :], above[:, :, :, :], ties[:, :, :, :], ALU.add))
            then_wait(nc.vector.tensor_reduce(rank[:, :, :], above[:, :, :, :], AX.X, ALU.add))
            then_wait(nc.vector.scalar_tensor_tensor(out=kept[:, :, :], in0=rank[:, :, :], scalar=2.0,
                                                     in1=pr[:, :, :], op0=ALU.is_lt, op1=ALU.mult))
            then_wait(nc.vector.tensor_reduce(tot2[:, :], kept[:, :, :], AX.X, ALU.add))
            then_wait(nc.vector.tensor_scalar(tot2[:, :], tot2[:, :], 1e-6, None, ALU.add))
            then_wait(nc.vector.reciprocal(tot2[:, :], tot2[:, :]))
            then_wait(nc.vector.tensor_tensor(sw[:, :].rearrange("p (e t) -> p t e", e=E), kept[:, :, :],
                                              by_e(tot2), ALU.mult))
            dve.wait_ge(cst, 1)

            def body(e, r, p, known):
                if not (known is not None and known < 2):
                    dve.wait_ge(acc_done, e * TB - TB)
                nc.vector.tensor_copy(swe[p][:, :], sw[:, bass.ds(e * NT, NT)]).then_inc(swe_done, 1)
                dve.wait_ge(swe_done, e + 1)
                for tb in range(TB):
                    dve.wait_ge(dn_done, e * TB + (tb + 1))
                    if not (known == 0):
                        dve.wait_ge(acc_done, e * TB + (tb + 1 - TB))
                    for j in range(4):
                        t = 4 * tb + j
                        last = nc.vector.scalar_tensor_tensor(
                            out=acc[:, t, :], in0=ps_dn[tb % 2][:, j * P:(j + 1) * P], scalar=swe[p][:, t:t + 1],
                            in1=acc[:, t, :], op0=ALU.mult, op1=ALU.add)
                    last.then_inc(acc_done, 1)

            pairs(dve, body)
            for g in range(4):
                dve.wait_ge(acc_done, E * TB - 4 + g + 1)
                for t in range(4 * g, 4 * g + 4):
                    nc.vector.bn_stats(stats[:, t, :], acc[:, t, :]).then_inc(stat_done, 1)
                dve.wait_ge(stat_done, 4 * g + 4)
                for t in range(4 * g, 4 * g + 4):
                    nc.vector.bn_aggr(mv[:, t, :], stats[:, t, :]).then_inc(var_done, 1)
            for g in range(4):
                dve.wait_ge(rstd_done, g + 1)
                for t in range(4 * g, 4 * g + 4):
                    last = nc.vector.tensor_scalar(acc[:, t, :], acc[:, t, :], mv[:, t, 0:1], rstd[:, t:t + 1],
                                                   ALU.subtract, ALU.mult)
                last.then_inc(n_done, 1)
                dve.wait_ge(n_done, g + 1)
                s = slice(4 * g, 4 * g + 4)
                nc.vector.tensor_tensor(acc[:, s, :], acc[:, s, :], x_sb[:, s, :], ALU.add).then_inc(y_done, 1)

        @block.tensor
        def _(pe):
            for t in range(NT):
                last = nc.tensor.matmul(ps_gate[:, t * E:(t + 1) * E], xn3T[:, t * P:(t + 1) * P], w["gate"][:, :],
                                        start=True, stop=True)
            last.then_inc(gate_done, 1)

            def down(e, tb, p, first):
                pe.wait_ge(gelu_done, e * (TB * IC) + (tb + 1) * IC)
                if not first:
                    pe.wait_ge(acc_done, e * TB + (tb - 1))
                for j in range(4):
                    for c in range(IC):
                        last = nc.tensor.matmul(ps_dn[tb % 2][:, j * P:(j + 1) * P], hT[tb % 2][:, c, j * P:(j + 1) * P],
                                                wdn[p][:, c, :], start=(c == 0), stop=(c == IC - 1))
                last.then_inc(dn_done, 1)

            def body(e, r, p, known):
                for tb in range(TB):
                    if tb == 0:
                        pe.wait_ge(up_in[p], r * 32 + 32)
                    for c in range(IC):
                        if not (known == 0 and tb == 0):
                            pe.wait_ge(gelu_done, e * (TB * IC) + ((tb - 1) * IC + c + 1))
                        nc.tensor.matmul(ps_up[c][:, :], wup[p][:, c * P:(c + 1) * P], xn3T[:, 512 * tb:512 * tb + 512],
                                         start=True, stop=True).then_inc(up_done, 1)
                    if tb:
                        down(e, tb - 1, p, known == 0 and tb - 1 < 2)
                    elif known != 0:
                        down(e - 1, TB - 1, 1 - p, False)

            pairs(pe, body)
            down(E - 1, TB - 1, 1, False)


def build(nc, a, out_d):
    with ExitStack() as ctx:
        sb = lambda n, s, d: ctx.enter_context(nc.sbuf_tensor(n, s, d))
        x_sb = sb("x_sb", [P, NT, D], F32)
        ident = sb("ident", [P, P], F32)
        att = sb("att", [P, NT * D], F32)
        keep = {
            "x_sb": x_sb, "ident": ident, "att": att,
            "ident_b": sb("ident_b", [P, P], BF16), "ones_f": sb("ones_f", [P, P], F32), "flag_i": sb("flag_i", [1, 1], I32),
            "q_scr": nc.dram_tensor("q_scr", (2, NSLOT, DH, NPAIR, TOK), BF16, kind="Internal").ap(),
            "k_scr": nc.dram_tensor("k_scr", (2, 3, DH, NPAIR, SK), BF16, kind="Internal").ap()}
        late_in = ctx.enter_context(nc.semaphore("late_in"))
        w = {n: sb("w_" + n, shape, F32) for n, shape, _ in LATE_WEIGHTS}
        cross_attention(nc, keep, a, w, late_in)
        xn3T = sb("xn3T", [P, TOK], F32)
        self_attention(nc, w, (x_sb, att, xn3T, ident, late_in))
        wup = [sb(f"wup{i}", [P, I], F32) for i in range(2)]
        wdn = [sb(f"wdn{i}", [P, IC, D], F32) for i in range(2)]
        experts(nc, w, (x_sb, xn3T, wup, wdn), a["w_up"], a["w_dn"], out_d)


def kernel(**inputs):
    import numpy as np
    import concourse.bacc as bacc
    from concourse.bass_utils import run_bass_kernel_spmd

    n = {k: np.asarray(v) for k, v in inputs.items()}
    mask = n["mask_BxSxS2_bf1"].view(np.uint8)
    by_pair = lambda w: w.reshape(NPAIR, 2, DH, -1).transpose(1, 2, 0, 3).reshape(D, -1)
    row, col = (lambda v: v.reshape(1, -1)), (lambda v: v.reshape(-1, 1))
    wk, bk, wv, bv = (n["L0_attn_" + s] for s in ("Wk", "bk", "Wv", "bv"))
    host = {
        "x": n["x"].reshape(TOK, D),
        "ctxT": n["ctx_1024"].transpose(0, 2, 1),
        "mask": mask,
        "maskT": mask.transpose(0, 2, 1),
        "ident": np.eye(P, dtype=np.float32),
        "x_wq": by_pair(n["L0_xattn_Wq"]).T, "x_bq": by_pair(n["L0_xattn_bq"])[:, 0],
        "x_wk": by_pair(n["L0_xattn_Wk"]).T, "x_bk": by_pair(n["L0_xattn_bk"])[:, 0],
        "x_wv": n["L0_xattn_Wv"].T,
        "x_bv": col(n["L0_xattn_bv"]), "x_wo": n["L0_xattn_Wo"].T, "x_bo": row(n["L0_xattn_bo"]),
        "w5": np.concatenate([n["L0_attn_Wq"].T, wk[0].T, wk[1].T, wv[0].T, wv[1].T], axis=1),
        "b5": row(np.concatenate([n["L0_attn_bq"], bk[0], bk[1], bv[0], bv[1]])),
        "blocks": (np.kron(np.eye(NH), np.ones((DH, DH))) * SQ ** -2.0).astype(np.float32),
        "ln_g": col(n["L0_attn_ln_g"]), "ln_b": col(n["L0_attn_ln_b"]),
        "a_wo": n["L0_attn_Wo"].T, "a_bo": row(n["L0_attn_bo"]),
        "gate": n["L0_ffn_gate_w"].T, "ebias": row(n["L0_ffn_expert_bias"]),
        "before": row(np.tril(np.ones((E, E), np.float32), -1)),
        "w_up": n["L0_ffn_w_up"].transpose(0, 2, 1), "w_dn": n["L0_ffn_w_down"].transpose(0, 2, 1),
    }
    nc = bacc.Bacc("TRN2", target_bir_lowering=False, num_devices=1)
    arrays, aps = {}, {}
    for name, arr in host.items():
        arr = np.ascontiguousarray(arr)
        arrays[f"in_{name}"] = arr
        aps[name] = nc.dram_tensor(f"in_{name}", arr.shape, mybir.dt.from_np(arr.dtype), kind="ExternalInput").ap()
    out = nc.dram_tensor("out", (TOK, D), F32, kind="ExternalOutput").ap()
    build(nc, aps, out)
    r = run_bass_kernel_spmd(nc, [arrays], core_ids=[0])
    return r.results[0]["out"].reshape(NB, SQ, D)
```

```python
from contextlib import ExitStack

import concourse.bass as bass
from concourse import mybir

F32 = mybir.dt.float32
BF16 = mybir.dt.bfloat16
U8 = mybir.dt.uint8
U16 = mybir.dt.uint16
I32 = mybir.dt.int32
ALU = mybir.AluOpType
ACT = mybir.ActivationFunctionType
AX = mybir.AxisListType

P = 128
NB, SQ, SK, D = 32, 64, 1601, 128
NH = 16
DH = D // NH
NPAIR = NH // 2
TOK = NB * SQ
NT = TOK // P
KT = (SK + P - 1) // P
KLAST = SK - (KT - 1) * P
NSLOT = 6
AROWS = NSLOT * DH
ROWS = 2 * AROWS
MROWS = 3
CH = [(0, 401), (401, 801), (801, 1201), (1201, 1601)]
MW = 401
NCH = 4
VG = [(0, 4), (4, 8), (8, 12), (12, 13)]
E, I = 8, 512
IC = I // P
EPS = 1e-5
PV_W = 32
ONE_COL = 2 * DH
TWO_ONES = 1 + 0x3F80 * 2.0 ** -23

LATE_WEIGHTS = [
    ("x_bv", [P, 1], False), ("x_wo", [P, D], False), ("x_bo", [P, D], True),
    ("w5", [P, 5 * D], False), ("b5", [P, 5 * D], True), ("blocks", [P, D], False),
    ("ln_g", [P, 1], False), ("ln_b", [P, 1], False), ("a_wo", [P, D], False), ("a_bo", [P, D], True),
    ("gate", [P, E], False), ("ebias", [P, E], True), ("before", [P, E * E], True)]
LATE = 16 * len(LATE_WEIGHTS)


def keys_of(t):
    return P if t < KT - 1 else KLAST


class QueryPhase:

    def __init__(self, nc, ctx, drams, keep, room):
        self.nc, self.d, self.keep, self.room = nc, drams, keep, room
        sb = lambda n, s, d: ctx.enter_context(nc.sbuf_tensor(n, s, d))
        sem = lambda n: ctx.enter_context(nc.semaphore(n))
        self.wq, self.bq, self.bqs = sb("wq", [P, D], F32), sb("bq", [P, 1], F32), sb("bqs", [P, 1], F32)
        self.stats, self.mv = sb("stats", [P, NT, 6], F32), sb("mv", [P, NT, 2], F32)
        self.eps_t, self.expo, self.rstd = sb("eps_t", [P, NT], F32), sb("expo", [P, NT], F32), sb("rstd", [P, NT], F32)
        self.rest = sb("rest", [P, 512], F32)
        self.q_parts = sb("q_parts", [P, 3, TOK], BF16)
        self.fmin, self.fsum = sb("fmin", [P, 1], F32), sb("fsum", [P, 1], F32)
        self.ok_a, self.ok = sb("ok_a", [P, 1], F32), sb("ok", [P, 1], F32)
        self.x_in = [sem("x_in0"), sem("x_in1")]
        self.w_in, self.mask_in = sem("w_in"), sem("mask_in")
        self.stat_done, self.var_done, self.rstd_done, self.xn_done = (
            sem("stat_done"), sem("var_done"), sem("rstd_done"), sem("xn_done"))
        self.tr_done, self.tr_evac, self.q_done, self.q_evac, self.split = (
            sem("tr_done"), sem("tr_evac"), sem("q_done"), sem("q_evac"), sem("split"))
        self.fmin_done, self.fsum_done, self.ok_done, self.okm_done, self.flag_done, self.cst = (
            sem("fmin_done"), sem("fsum_done"), sem("ok_done"), sem("okm_done"), sem("flag_done"), sem("cst"))
        self.q_stored = [sem("q_stored0"), sem("q_stored1")]
        self.bqs_done, self.identb_done = sem("bqs_done"), sem("identb_done")
        self.n16 = NB * SQ * SK // P // 2
        self.half = self.n16 // 2

    def load_x(self, sp):
        xv = self.d["x"].rearrange("(t p) d -> p t d", p=P)
        x_sb = self.keep["x_sb"]
        sp.dma_start(x_sb[:, 0:4, :], xv[:, 0:4, :]).then_inc(self.x_in[0], 16)
        sp.dma_start(self.keep["ident"][:, :], self.d["ident"]).then_inc(self.w_in, 16)
        sp.dma_start(self.wq[:, :], self.d["x_wq"]).then_inc(self.w_in, 16)
        sp.dma_start(self.bq[:, :], self.d["x_bq"].rearrange("(p a) -> p a", a=1)).then_inc(self.w_in, 16)
        sp.dma_start(x_sb[:, 4:NT, :], xv[:, 4:NT, :]).then_inc(self.x_in[1], 16)

    def load_mask(self, sp):
        sp.dma_start(self.room["mask"].bitcast(U8),
                     self.d["mask"].rearrange("b q k -> (b q k)").rearrange("(p n) -> p n", p=P)).then_inc(self.mask_in, 16)

    def store_q(self, sp, first):
        lo, hi = (0, 512) if first else (512, TOK)
        sp.wait_ge(self.split, 4 if first else 16)
        for s, part in enumerate((0, 0, 0, 1, 1, 2)):
            for a in range(2):
                sp.dma_start(self.room["q_scr"][a, s, :, :, lo:hi].rearrange("r p n -> (r p) n"),
                             self.q_parts[64 * a:64 * a + 64, part, lo:hi]).then_inc(self.q_stored[0 if first else 1], 16)

    def gpsimd(self, pool):
        nc = self.nc
        pool.memset(self.keep["ones_f"][:, :], 1.0).then_inc(self.cst, 1)
        pool.memset(self.eps_t[:, :], EPS).then_inc(self.cst, 1)
        pool.memset(self.expo[:, :], -0.5).then_inc(self.cst, 1)
        pool.wait_ge(self.cst, 3)
        for n, (t0, t1) in enumerate(((0, 4), (4, NT))):
            pool.wait_ge(self.var_done, t1)
            nc.gpsimd.tensor_tensor(self.rstd[:, t0:t1], self.mv[:, t0:t1, 1], self.eps_t[:, t0:t1], ALU.add)\
                .then_inc(self.cst, 1)
            pool.wait_ge(self.cst, 4 + n)
            nc.gpsimd.tensor_tensor(self.rstd[:, t0:t1], self.rstd[:, t0:t1], self.expo[:, t0:t1], ALU.pow)\
                .then_inc(self.rstd_done, 1)

    def vector(self, dve):
        nc, x_sb, xn = self.nc, self.keep["x_sb"], self.room["xn"]
        for n, (t0, t1) in enumerate(((0, 4), (4, NT))):
            dve.wait_ge(self.x_in[n], 16)
            for t in range(t0, t1):
                nc.vector.bn_stats(self.stats[:, t, :], x_sb[:, t, :]).then_inc(self.stat_done, 1)
            for t in range(t0, t1):
                dve.wait_ge(self.stat_done, t + 1)
                nc.vector.bn_aggr(self.mv[:, t, :], self.stats[:, t, :]).then_inc(self.var_done, 1)
        dve.wait_ge(self.w_in, 48)
        nc.vector.tensor_scalar(self.bqs[:, :], self.bq[:, :], DH ** -0.5, None, ALU.mult).then_inc(self.bqs_done, 1)
        nc.vector.tensor_copy(self.keep["ident_b"][:, :], self.keep["ident"][:, :]).then_inc(self.identb_done, 1)
        for n, (t0, t1) in enumerate(((0, 4), (4, NT))):
            dve.wait_ge(self.rstd_done, n + 1)
            for t in range(t0, t1):
                nc.vector.tensor_scalar(xn[:, t * D:(t + 1) * D], x_sb[:, t, :], self.mv[:, t, 0:1],
                                        self.rstd[:, t:t + 1], ALU.subtract, ALU.mult).then_inc(self.xn_done, 1)
        qf, parts, rest = self.room["qf"], self.q_parts, self.rest
        for g in range(4):
            s = slice(512 * g, 512 * g + 512)
            dve.wait_ge(self.q_evac, g + 1)
            nc.vector.tensor_copy(parts[:, 0, s], qf[:, s]).then_inc(self.split, 1)
            dve.wait_ge(self.split, 4 * g + 1)
            nc.vector.tensor_tensor(rest[:, :], qf[:, s], parts[:, 0, s], ALU.subtract).then_inc(self.split, 1)
            dve.wait_ge(self.split, 4 * g + 2)
            nc.vector.tensor_copy(parts[:, 1, s], rest[:, :]).then_inc(self.split, 1)
            dve.wait_ge(self.split, 4 * g + 3)
            nc.vector.tensor_tensor(parts[:, 2, s], rest[:, :], parts[:, 1, s], ALU.subtract).then_inc(self.split, 1)

    def check_mask(self, dve):
        nc = self.nc
        dve.wait_ge(self.mask_in, 16)
        nc.vector.tensor_reduce(self.fmin[:, :], self.room["mask"][:, 0:self.half], AX.X, ALU.min)\
            .then_inc(self.fmin_done, 1)
        dve.wait_ge(self.fmin_done, 1)
        dve.wait_ge(self.fsum_done, 1)
        nc.vector.tensor_scalar(self.ok_a[:, :], self.fmin[:, :], 257.0, None, ALU.is_equal).then_inc(self.ok_done, 1)
        dve.wait_ge(self.ok_done, 1)
        nc.vector.scalar_tensor_tensor(out=self.ok[:, :], in0=self.fsum[:, :], scalar=257.0 * (self.n16 - self.half),
                                       in1=self.ok_a[:, :], op0=ALU.is_equal, op1=ALU.mult).then_inc(self.ok_done, 1)
        dve.wait_ge(self.okm_done, 1)
        nc.vector.tensor_scalar(self.keep["flag_i"][:, :], self.room["ps_f"][0:1, 0:1], float(P), None, ALU.is_equal)\
            .then_inc(self.flag_done, 1)

    def scalar(self, act):
        nc, ps_t, ps_q = self.nc, self.room["ps_t"], self.room["ps_q"]
        act.wait_ge(self.bqs_done, 1)
        for g in range(4):
            act.wait_ge(self.tr_done, g + 1)
            nc.scalar.activation(self.room["xnT"][:, 512 * g:512 * g + 512], ps_t[g % 2], ACT.Copy)\
                .then_inc(self.tr_evac, 1)
            act.wait_ge(self.q_done, g + 1)
            nc.scalar.activation(self.room["qf"][:, 512 * g:512 * g + 512], ps_q[g % 2], ACT.Identity,
                                 bias=self.bqs[:, 0:1], scale=DH ** -0.5).then_inc(self.q_evac, 1)

    def sum_mask(self, act):
        nc = self.nc
        act.wait_ge(self.mask_in, 16)
        words = self.room["mask"][:, self.half:self.n16]
        nc.scalar.activation(words.bitcast(BF16), words, ACT.Copy, accum_out=self.fsum[:, :]).then_inc(self.fsum_done, 1)

    def tensor(self, pe):
        nc, ps_t, ps_q, xn = self.nc, self.room["ps_t"], self.room["ps_q"], self.room["xn"]
        pe.wait_ge(self.w_in, 48)
        for g in range(4):
            pe.wait_ge(self.xn_done, 4 * g + 4)
            if g >= 2:
                pe.wait_ge(self.tr_evac, g - 1)
            for t in range(4 * g, 4 * g + 4):
                last = nc.tensor.transpose(ps_t[g % 2][:, (t % 4) * P:(t % 4 + 1) * P], xn[:, t * D:(t + 1) * D],
                                           self.keep["ident"][:, :])
            last.then_inc(self.tr_done, 1)
            pe.wait_ge(self.tr_evac, g + 1)
            if g >= 2:
                pe.wait_ge(self.q_evac, g - 1)
            nc.tensor.matmul(ps_q[g % 2], self.wq[:, :], self.room["xnT"][:, 512 * g:512 * g + 512],
                             start=True, stop=True).then_inc(self.q_done, 1)

    def count_true(self, pe):
        pe.wait_ge(self.ok_done, 2)
        pe.wait_ge(self.cst, 1)
        self.nc.tensor.matmul(self.room["ps_f"][0:1, 0:1], self.ok[:, :], self.keep["ones_f"][:, 0:1],
                              start=True, stop=True).then_inc(self.okm_done, 1)

    def all_true(self, eng):
        eng.wait_ge(self.flag_done, 1)
        return eng.value_load(self.keep["flag_i"][0:1, 0:1]) == 1


def cross_attention(nc, keep, drams, w, late_in):
    ctx_d, mask_d, maskT_d, wk_d, bk_d, wv_d = (drams[n] for n in ("ctxT", "mask", "maskT", "x_wk", "x_bk", "x_wv"))
    q_scr, k_scr, ident, ident_b, att = (keep[n] for n in ("q_scr", "k_scr", "ident", "ident_b", "att"))
    with ExitStack() as ctx:
        sb = lambda n, s, d: ctx.enter_context(nc.sbuf_tensor(n, s, d))
        psb = lambda n: ctx.enter_context(nc.psum_tensor(n, [P, 512], F32))
        sem = lambda n: ctx.enter_context(nc.semaphore(n))
        wk, wv, bk = sb("wk", [P, D], F32), sb("wv", [P, D], F32), sb("bk", [P, 1], F32)
        ctxT = [sb(f"ctxT{i}", [P, SK], F32) for i in range(2)]
        kf = [sb(f"kf{i}", [P, MW], F32) for i in range(2)]
        krest = [sb(f"krest{i}", [P, MW], F32) for i in range(2)]
        kparts = sb("kparts", [P, 3, SK], BF16)
        kst_flat = [sb(f"kst{i}", [P, NPAIR * SK], BF16) for i in range(2)]
        kst = [k[:, :].rearrange("r (a n) -> r a n", a=NPAIR) for k in kst_flat]
        qmax = [sb(f"qmax{i}", [P, NPAIR * P], BF16) for i in range(2)]
        qsc = [sb(f"qsc{i}", [P, NPAIR * P], BF16) for i in range(2)]
        v = [sb(f"v{i}", [P, KT, NPAIR, PV_W], F32) for i in range(2)]
        probs2 = sb("probs", [P, 2 * NPAIR * P], F32)
        probs = [probs2[:, i * NPAIR * P:(i + 1) * NPAIR * P] for i in range(2)]
        mx2 = sb("mx2", [P, 2, NPAIR], F32)
        mx = sb("mx", [P, NPAIR], F32)
        mrest = sb("mrest", [P, NPAIR], F32)
        mparts = sb("mparts", [P, NPAIR, MROWS], BF16)
        oT = sb("oT", [P, 2 * P], F32)
        rec = sb("rec", [P, NPAIR], F32)
        mask_q = sb("mask_q", [P, SK], U8)
        mask_k = sb("mask_k", [P, KT, SQ], U8)
        picked = sb("picked", [P, 2, MW], F32)
        tiny, held = sb("tiny", [P, 1], F32), sb("held", [P, 1], F32)
        args2 = sb("args", [P, 2 * NPAIR * P], F32)
        fill, arg = (args2[:, i * NPAIR * P:(i + 1) * NPAIR * P] for i in range(2))
        score = [psb(f"score{i}") for i in range(2)]
        maxps = [ctx.enter_context(nc.psum_tensor(f"maxps{i}", [P, 2, 512], F32)) for i in range(2)]
        pvps, misc = psb("pvps"), psb("misc")

        query = QueryPhase(nc, ctx, drams, keep, {
            "mask": kst_flat[1][:, :].bitcast(U16), "xn": probs2, "xnT": args2, "qf": att,
            "q_scr": q_scr, "ps_t": [maxps[0][:, i, :] for i in range(2)], "ps_q": [maxps[1][:, i, :] for i in range(2)],
            "ps_f": score[0]})

        w_in = sem("w_in1")
        ctx_in = [sem("ctx_in0"), sem("ctx_in1")]
        cst, ones_in, xb_done = sem("cst1"), sem("ones_in"), sem("xb_done")
        k_done, k_evac, k_split, k_chain = sem("k_done"), sem("k_evac"), sem("k_split"), sem("k_chain")
        v_done, v_evac = sem("v_done"), sem("v_evac")
        k_scr_in = [sem("k_scr_in0"), sem("k_scr_in1")]
        kst_in = [sem("kst_in0"), sem("kst_in1")]
        qmax_in, qsc_in = sem("qmax_in"), sem("qsc_in")
        max_ready, max_red, m_chain, m_parts = sem("max_ready"), sem("max_red"), sem("m_chain"), sem("m_parts")
        mrow_done, mrow_evac = sem("mrow_done"), sem("mrow_evac")
        score_ready, exp_done, pv_done = sem("score_ready"), sem("exp_done"), sem("pv_done")
        mask_in, mask_kin = sem("mask_in1"), sem("mask_kin")
        pick_fill, pick_done, fill_done, fill_evac, arg_fill, arg_done = (
            sem("pick_fill"), sem("pick_done"), sem("fill_done"), sem("fill_evac"), sem("arg_fill"), sem("arg_done"))
        oT_copied, oT_back, rec_done, att_done = sem("oT_copied"), sem("oT_back"), sem("rec_done"), sem("att_done")

        MAX_STEPS = {0: [4], 1: [5], 2: [6], 3: [7], 4: [8], 5: [9], 6: [10, 11], 7: [12], 8: [13, 14], 9: [15]}
        EARLY_STEPS = {10: [0], 11: [1], 12: [2, 3]}
        SPLIT_SLOT = 10
        MISC = {0: ("k", 2, 0), 1: ("o", -1, 0), 2: ("k", 2, 1), 3: ("v", 1, 2), 4: ("k", 2, 2), 5: ("v", 1, 3),
                6: ("k", 2, 3), 7: ("v", 2, 0), 9: ("v", 2, 1), 11: ("m", 1, 0), 12: ("m", 1, 1)}

        def wanted(kind, stage, i_known):
            return i_known is None or 0 <= i_known + stage < NB

        def evacuated(eng, kind, b, n):
            if kind == "v":
                eng.wait_ge(v_evac, b * 4 + (n + 1))
            elif kind == "k":
                eng.wait_ge(k_evac, b * 4 + (n + 1))
            elif kind == "m":
                eng.wait_ge(mrow_evac, b * 2 + (n + 1))
            else:
                eng.wait_ge(att_done, b * 2 + 2)

        def previous_use(slot, i_known):
            for s in range(slot - 1, -1, -1):
                if s in MISC and wanted(MISC[s][0], MISC[s][1], i_known):
                    return MISC[s]
            return ("v", 1, 1) if i_known == -1 else ("m", 0, 1)

        def iterations(eng, body):
            body(-1, -1, 1, -1)
            body(0, 0, 0, 0)
            body(1, 0, 1, 1)
            with eng.Fori(1, NB // 2 - 2) as r:
                body(r * 2, r, 0, None)
                body(r * 2 + 1, r, 1, None)
            for i in range(NB - 4, NB):
                body(i, i // 2, i % 2, i)

        def batches(eng, body):
            body(0, 0, 0, 0)
            body(1, 0, 1, 1)
            with eng.Fori(1, NB // 2) as r:
                body(r * 2, r, 0, None)
                body(r * 2 + 1, r, 1, None)

        def sync_program(sp):
            def load_ctx(b, p):
                sp.dma_start(ctxT[p][:, :], ctx_d[b, :, :]).then_inc(ctx_in[p], 16)

            def load_q(b, p):
                for a in range(2):
                    dst = qmax[p][a * AROWS:(a + 1) * AROWS, :].rearrange("r (p a n) -> r p a n", a=2, n=SQ)[:, :, a, :]
                    src = q_scr[a].rearrange("s r p n -> (s r) p n")[:, :, bass.ds(b * SQ, SQ)]
                    sp.dma_start(dst, src).then_inc(qmax_in, 16)

            def copy_q(p):
                sp.dma_start(qsc[p][0:ROWS, :], qmax[p][0:ROWS, :]).then_inc(qsc_in, 16)

            def stack_k(half, b, p, tiles_used):
                lo, hi = (0, CH[1][1]) if half == 0 else (CH[2][0], SK)
                sp.wait_ge(k_split, b * 4 + (2 * half + 2))
                for a in range(2):
                    sp.dma_start(k_scr[a, :, :, :, lo:hi].rearrange("s r p n -> (r p) s n"),
                                 kparts[64 * a:64 * a + 64, :, lo:hi]).then_inc(k_scr_in[half], 16)
                sp.wait_ge(k_scr_in[half], b * 32 + 32)
                if tiles_used is not None:
                    sp.wait_ge(score_ready, tiles_used)
                for a in range(2):
                    for row, parts in ((0, 3), (3 * DH, 2), (5 * DH, 1)):
                        src = k_scr[a, 0:parts, :, :, lo:hi].rearrange("s r p n -> (s r) p n")
                        r0 = a * AROWS + row
                        sp.dma_start(kst[p][r0:r0 + parts * DH, :, lo:hi], src).then_inc(kst_in[half], 16)

            def later():
                query.store_q(sp, False)
                for name, shape, to_all in LATE_WEIGHTS:
                    src = drams[name].to_broadcast([P, shape[1]]) if to_all else drams[name]
                    sp.dma_start(w[name][:, :], src).then_inc(late_in, 16)

            query.load_x(sp)
            sp.dma_start(wk[:, :], wk_d).then_inc(w_in, 16)
            sp.dma_start(bk[:, :], bk_d.rearrange("(p a) -> p a", a=1)).then_inc(w_in, 16)
            sp.dma_start(wv[:, :], wv_d).then_inc(w_in, 16)
            load_ctx(0, 0)
            query.load_mask(sp)
            load_ctx(1, 1)
            query.store_q(sp, True)
            sp.wait_ge(cst, 1)
            sp.wait_ge(query.q_stored[0], 2 * NSLOT * 16)
            load_q(0, 0)
            stack_k(0, 0, 0, None)
            stack_k(1, 0, 0, None)
            with sp.If(query.all_true(sp)):
                def body(i, r, p, known):
                    if known == 0:
                        later()
                        sp.wait_ge(query.q_stored[1], 2 * NSLOT * 16)
                    if known is None or known + 1 < NB:
                        if known is None or known > 0:
                            sp.wait_ge(score_ready, i * (2 * KT))
                        sp.wait_ge(qmax_in, i * 32 + 64)
                        copy_q(1 - p)
                    if known is None or known + 2 < NB:
                        if known != -1:
                            sp.wait_ge(max_ready, i * 16 + 16)
                            sp.wait_ge(qsc_in, i * 16 + 16)
                        load_q(i + 2, p)
                        stack_k(0, i + 2, p, None if known == -1 else (i * 2 + 1) * KT + 1)
                    if known is None or known + 3 < NB:
                        sp.wait_ge(v_done, (i + 1) * 4 + 4)
                        load_ctx(i + 3, 1 - p)
                    if known is None or known + 2 < NB:
                        stack_k(1, i + 2, p, None if known == -1 else (i * 2 + 2) * KT)

                iterations(sp, body)
            with sp.Else():
                def body(b, r, half, known):
                    if known != 0:
                        sp.wait_ge(v_done, b * 4)
                        load_ctx(b, 0)
                        sp.wait_ge(max_red, b * 16)
                        sp.wait_ge(qsc_in, b * 16)
                        load_q(b, 0)
                    for a in range(2):
                        sp.dma_start(mask_q[64 * a:64 * a + 64, :], mask_d[b, :, :]).then_inc(mask_in, 16)
                    if known != 0:
                        sp.wait_ge(arg_done, b * (2 * KT))
                    sp.dma_start(mask_k[:, 0:KT - 1, :], maskT_d[b, 0:(KT - 1) * P, :].rearrange(
                        "(t p) q -> p t q", p=P)).then_inc(mask_kin, 16)
                    sp.dma_start(mask_k[0:KLAST, KT - 1, :], maskT_d[b, (KT - 1) * P:SK, :]).then_inc(mask_kin, 16)
                    if known != 0:
                        sp.wait_ge(score_ready, b * (2 * KT))
                    sp.wait_ge(qmax_in, b * 32 + 32)
                    copy_q(0)
                    if known != 0:
                        stack_k(0, b, 0, None)
                        stack_k(1, b, 0, None)

                later()
                sp.wait_ge(query.q_stored[1], 2 * NSLOT * 16)
                batches(sp, body)
            sp.wait_ge(att_done, 2 * NB)

        def split_k(pool, b, j):
            lo, hi = CH[j]
            w = hi - lo
            pool.wait_ge(k_evac, b * 4 + (j + 1))
            nc.gpsimd.tensor_tensor(krest[j % 2][:, 0:w], kf[j % 2][:, 0:w], kparts[:, 0, lo:hi], ALU.subtract)\
                .then_inc(k_chain, 1)
            nc.gpsimd.tensor_tensor(kparts[:, 1, lo:hi], kf[j % 2][:, 0:w], kparts[:, 0, lo:hi], ALU.subtract)\
                .then_inc(k_chain, 1)
            pool.wait_ge(k_chain, b * 8 + (2 * j + 2))
            nc.gpsimd.tensor_tensor(kparts[:, 2, lo:hi], krest[j % 2][:, 0:w], kparts[:, 1, lo:hi], ALU.subtract)\
                .then_inc(k_split, 1)

        def pool_program(pool):
            query.gpsimd(pool)
            for j in range(2):
                split_k(pool, 0, j)
            pool.wait_ge(k_split, 2)
            pool.memset(kst_flat[0][ROWS:P, :].bitcast(F32), TWO_ONES).then_inc(ones_in, 1)
            pool.wait_ge(ones_in, 1)
            for j in range(2, NCH):
                split_k(pool, 0, j)
            pool.wait_ge(k_split, NCH)
            pool.wait_ge(query.fmin_done, 1)
            pool.wait_ge(query.fsum_done, 1)
            pool.memset(kst_flat[1][ROWS:P, :].bitcast(F32), TWO_ONES).then_inc(ones_in, 1)
            with pool.If(query.all_true(pool)):
                def body(i, r, p, known):
                    if known is None or known + 2 < NB:
                        for j in range(NCH):
                            split_k(pool, i + 2, j)

                iterations(pool, body)
            with pool.Else():
                def body(b, r, half, known):
                    for j in range(NCH if known != 0 else 0):
                        split_k(pool, b, j)

                batches(pool, body)
            pool.wait_ge(k_split, NB * NCH)
            pool.wait_ge(late_in, LATE)
            for t in range(NT):
                last = nc.gpsimd.tensor_tensor(keep["x_sb"][:, t, :], keep["x_sb"][:, t, :], w["x_bo"][:, :], ALU.add)
            last.then_inc(xb_done, 1)
            pool.wait_ge(xb_done, 1)

        def scalar_program(act):
            def evac_k(b, j, known, bank=misc):
                lo, hi = CH[j]
                w = hi - lo
                act.wait_ge(k_done, b * 4 + (j + 1))
                if not (known is not None and known == 0 and j < 2):
                    act.wait_ge(k_split, b * 4 + (j - 1))
                if j % 2 == 0 and known != 0:
                    act.wait_ge(kst_in[j // 2], b * 96)
                nc.scalar.activation(kf[j % 2][:, 0:w], bank[:, 0:w], ACT.Identity, bias=bk[:, 0:1])
                nc.scalar.activation(kparts[:, 0, lo:hi], bank[:, 0:w], ACT.Identity, bias=bk[:, 0:1])\
                    .then_inc(k_evac, 1)

            def evac_m(b, h, p, known):
                act.wait_ge(mrow_done, b * 2 + (h + 1))
                nc.scalar.activation(qsc[p][ROWS:ROWS + MROWS, h * 512:h * 512 + 512],
                                     misc[ROWS:ROWS + MROWS, :], ACT.Copy).then_inc(mrow_evac, 1)

            act.wait_ge(w_in, 48)
            for j in range(2):
                evac_k(0, j, 0, (misc, pvps)[j % 2])
            query.scalar(act)
            for j in range(2, NCH):
                evac_k(0, j, 0, (misc, pvps)[j % 2])
            query.sum_mask(act)
            with act.If(query.all_true(act)):
                def body(i, r, p, known):
                    for t in range(KT):
                        n = keys_of(t)
                        for h in range(2 if known != -1 else 0):
                            act.wait_ge(score_ready, i * (2 * KT) + (2 * t + h + 1))
                            if not (known == 0 and t < 2):
                                act.wait_ge(pv_done, i * KT + (t - 1))
                            nc.scalar.activation(probs[(t + p) % 2][0:n, h * 512:h * 512 + 512], score[h][0:n, :],
                                                 ACT.Exp).then_inc(exp_done, 1)
                        if t in MISC and wanted(*MISC[t][0:2], known):
                            kind, stage, num = MISC[t]
                            if kind == "k":
                                evac_k(i + stage, num, None)
                            if kind == "m":
                                evac_m(i + stage, num, 1 - p, None)

                iterations(act, body)
            with act.Else():
                def body(b, r, half, known):
                    for j in range(NCH if known != 0 else 0):
                        evac_k(b, j, known)
                    for h in range(2):
                        evac_m(b, h, 0, known)
                    for h in range(2):
                        act.wait_ge(fill_done, b * 2 + (h + 1))
                        nc.scalar.activation(fill[:, h * 512:h * 512 + 512], misc[:, :], ACT.Identity, bias=tiny[:, 0:1])\
                            .then_inc(fill_evac, 1)
                    for t in range(KT):
                        n = keys_of(t)
                        for h in range(2):
                            act.wait_ge(arg_done, b * (2 * KT) + (2 * t + h + 1))
                            if not (known == 0 and t == 0):
                                act.wait_ge(pv_done, b * KT + t)
                            nc.scalar.activation(probs[t % 2][0:n, h * 512:h * 512 + 512],
                                                 arg[0:n, h * 512:h * 512 + 512], ACT.Exp).then_inc(exp_done, 1)

                batches(act, body)

        def vector_program(dve):
            def reduce_step(b, s):
                dve.wait_ge(max_ready, b * 16 + (s + 1))
                nc.vector.tensor_reduce(mx2[:, s // 8, s % 8:s % 8 + 1], maxps[s % 2][:, :, 0:MW], AX.XY, ALU.max)\
                    .then_inc(max_red, 1)

            def split_m(b, known):
                dve.wait_ge(max_red, b * 16 + 16)
                nc.vector.tensor_tensor(mx[:, :], mx2[:, 0, :], mx2[:, 1, :], ALU.max).then_inc(m_chain, 1)
                if known != 0:
                    dve.wait_ge(mrow_done, b * 2)
                dve.wait_ge(m_chain, b * 4 + 1)
                nc.vector.tensor_scalar(mparts[:, :, 0], mx[:, :], -1.0, None, ALU.mult).then_inc(m_chain, 1)
                dve.wait_ge(m_chain, b * 4 + 2)
                nc.vector.scalar_tensor_tensor(out=mrest[:, :], in0=mx[:, :], scalar=-1.0, in1=mparts[:, :, 0],
                                               op0=ALU.mult, op1=ALU.subtract).then_inc(m_chain, 1)
                dve.wait_ge(m_chain, b * 4 + 3)
                nc.vector.tensor_copy(mparts[:, :, 1], mrest[:, :]).then_inc(m_chain, 1)
                dve.wait_ge(m_chain, b * 4 + 4)
                nc.vector.tensor_tensor(mparts[:, :, 2], mrest[:, :], mparts[:, :, 1], ALU.subtract)\
                    .then_inc(m_parts, 1)

            def evac_v(b, g, p, used):
                t0, t1 = VG[g]
                n = keys_of(t1 - 1)
                dve.wait_ge(v_done, b * 4 + (g + 1))
                if used is not None:
                    dve.wait_ge(pv_done, used)
                nc.vector.tensor_copy(
                    v[p][0:n, t0:t1, :, 0:2 * DH],
                    misc[0:n, 0:(t1 - t0) * P].rearrange("k (t p c) -> k t p c", p=NPAIR, c=2 * DH))\
                    .then_inc(v_evac, 1)

            def copy_o(b):
                dve.wait_ge(pv_done, b * KT + KT)
                nc.vector.tensor_copy(oT[:, :], pvps[:, 0:2 * P]).then_inc(oT_copied, 1)

            def norm_o(b, r, p):
                back = misc[:, 0:2 * P].rearrange("k (p c) -> k p c", c=PV_W)
                dve.wait_ge(oT_back, b + 1)
                nc.vector.reciprocal(rec[:, :], back[:, :, ONE_COL]).then_inc(rec_done, 1)
                dve.wait_ge(rec_done, b + 1)
                for a in range(2):
                    dst = att[64 * p:64 * p + 64, bass.ds(r * D, D)].rearrange("q (p a d) -> q p a d", a=2, d=DH)
                    nc.vector.tensor_tensor(
                        dst[:, :, a, :], back[64 * a:64 * a + 64, :, a * DH:(a + 1) * DH],
                        rec[64 * a:64 * a + 64, :].unsqueeze(2).to_broadcast([64, NPAIR, DH]),
                        ALU.mult).then_inc(att_done, 1)

            for p in range(2):
                last = nc.vector.memset(qmax[p][:, :].bitcast(F32), 0.0)
            last.then_inc(cst, 1)
            for p in range(2):
                nc.vector.memset(v[p][:, :, :, ONE_COL], 1.0)
                last = nc.vector.memset(v[p][:, :, :, ONE_COL + 1:PV_W], 0.0)
            last.then_inc(cst, 1)
            nc.vector.memset(tiny[:, :], 1e-9).then_inc(cst, 1)
            query.vector(dve)
            for g in range(2):
                evac_v(0, g, 0, None)
            query.check_mask(dve)
            with dve.If(query.all_true(dve)):
                for s in sum(EARLY_STEPS.values(), []):
                    reduce_step(0, s)

                def body(i, r, p, known):
                    for t in range(KT):
                        if t == 0 and (known is None or known > 0):
                            copy_o(i - 1)
                        if t == SPLIT_SLOT and (known is None or known + 1 < NB):
                            split_m(i + 1, 0 if known == -1 else None)
                        if t in MISC and wanted(*MISC[t][0:2], known):
                            kind, stage, num = MISC[t]
                            if kind == "v":
                                used = None if known is not None and known + stage < 2 else \
                                    (i + (stage - 2)) * KT + VG[num][1]
                                evac_v(i + stage, num, (p + stage) % 2, used)
                            if kind == "o":
                                norm_o(i - 1, r if p == 1 else r - 1, 1 - p)
                        if known is None or known + 1 < NB:
                            for s in MAX_STEPS.get(t, ()):
                                reduce_step(i + 1, s)
                        if known is None or known + 2 < NB:
                            for s in EARLY_STEPS.get(t, ()):
                                reduce_step(i + 2, s)

                iterations(dve, body)
                copy_o(NB - 1)
                norm_o(NB - 1, NB // 2 - 1, 1)
            with dve.Else():
                def body(b, r, half, known):
                    for g in range(0 if known != 0 else 2, 4):
                        evac_v(b, g, 0, None if known == 0 else b * KT)
                    dve.wait_ge(mask_in, b * 32 + 32)
                    for s in range(16):
                        if not (known == 0 and s == 0):
                            dve.wait_ge(max_red, b * 16 + s)
                        nc.vector.memset(picked[:, :, :], 1e-9).then_inc(pick_fill, 1)
                        dve.wait_ge(pick_fill, b * 16 + (s + 1))
                        dve.wait_ge(max_ready, b * 16 + (s + 1))
                        nc.vector.tensor_copy(held[:, :], tiny[:, :])
                        for c in range(2):
                            lo = 400 * (2 * (s // 8) + c)
                            last = nc.vector.copy_predicated(picked[:, c, :], mask_q[:, lo:lo + MW],
                                                             maxps[s % 2][:, c, 0:MW])
                        last.then_inc(pick_done, 1)
                        dve.wait_ge(pick_done, b * 16 + (s + 1))
                        nc.vector.tensor_reduce(mx2[:, s // 8, s % 8:s % 8 + 1], picked[:, :, :], AX.XY, ALU.max)\
                            .then_inc(max_red, 1)
                    split_m(b, known)
                    dve.wait_ge(mask_kin, b * 32 + 32)
                    for t in range(KT):
                        n = keys_of(t)
                        for h in range(2):
                            at = lambda a: a[0:n, :].rearrange("k (h q) -> k h q", q=SQ)
                            hs = slice(h * 512, h * 512 + 512)
                            k = 2 * t + h
                            if not (known == 0 and t == 0):
                                dve.wait_ge(exp_done, b * (2 * KT) + (k - 1))
                            dve.wait_ge(fill_evac, b * 2 + (h + 1))
                            nc.vector.tensor_copy(arg[0:n, hs], fill[0:n, hs]).then_inc(arg_fill, 1)
                            dve.wait_ge(arg_fill, b * (2 * KT) + (k + 1))
                            dve.wait_ge(score_ready, b * (2 * KT) + (k + 1))
                            nc.vector.tensor_copy(held[:, :], tiny[:, :])
                            nc.vector.copy_predicated(
                                at(arg[:, hs]), mask_k[0:n, t, :].unsqueeze(1).to_broadcast([n, 8, SQ]),
                                at(score[h])).then_inc(arg_done, 1)
                    copy_o(b)
                    norm_o(b, r, half)

                batches(dve, body)

        def tensor_program(pe):
            def k_proj(b, rb, j, p, bank=misc):
                lo, hi = CH[j]
                if j == 0:
                    pe.wait_ge(ctx_in[p], rb * 16 + 16)
                nc.tensor.matmul(bank[:, 0:hi - lo], wk[:, :], ctxT[p][:, lo:hi], start=True, stop=True)\
                    .then_inc(k_done, 1)

            def v_proj(b, g, p):
                t0, t1 = VG[g]
                for t in range(t0, t1):
                    n = keys_of(t)
                    last = nc.tensor.matmul(misc[0:n, (t - t0) * P:(t - t0 + 1) * P],
                                            ctxT[p][:, t * P:t * P + n], wv[:, :], start=True, stop=True)
                last.then_inc(v_done, 1)

            def max_step(b, s, p, known):
                pair, half = s % 8, s // 8
                if s == 0:
                    pe.wait_ge(qmax_in, b * 32 + 32)
                if s % 8 == 0:
                    pe.wait_ge(kst_in[half], b * 96 + 96)
                if not (known == 0 and s < 2):
                    pe.wait_ge(max_red, b * 16 + (s - 1))
                for c in range(2):
                    lo = 400 * (2 * half + c)
                    last = nc.tensor.matmul(maxps[s % 2][:, c, 0:MW], qmax[p][0:ROWS, pair * P:(pair + 1) * P],
                                            kst[p][0:ROWS, pair, lo:lo + MW], start=True, stop=True)
                last.then_inc(max_ready, 1)

            def m_rows(b, h):
                pe.wait_ge(m_parts, b + 1)
                for j in range(4):
                    last = nc.tensor.matmul(misc[ROWS:ROWS + MROWS, j * P:(j + 1) * P], mparts[:, 4 * h + j, :],
                                            ident_b[:, :], start=True, stop=True)
                last.then_inc(mrow_done, 1)

            def scores(i, t, p, known):
                n = keys_of(t)
                for h in range(2):
                    if t == 0:
                        pe.wait_ge(mrow_evac, i * 2 + (h + 1))
                        pe.wait_ge(qsc_in, i * 16 + 16)
                    if not (known == 0 and t == 0):
                        pe.wait_ge(exp_done, i * (2 * KT) + (2 * t + h - 1))
                    for j in range(4):
                        pair = 4 * h + j
                        last = nc.tensor.matmul(score[h][0:n, j * P:(j + 1) * P],
                                                kst[p][0:ROWS + MROWS, pair, t * P:t * P + n],
                                                qsc[p][0:ROWS + MROWS, pair * P:(pair + 1) * P],
                                                start=True, stop=True)
                    last.then_inc(score_ready, 1)

            def p_v(i, t, p, known):
                n = keys_of(t)
                for g, (t0, _) in enumerate(VG):
                    if t == t0:
                        pe.wait_ge(v_evac, i * 4 + (g + 1))
                if t == 0 and known != 0:
                    pe.wait_ge(oT_copied, i)
                for pair in range(NPAIR):
                    g, r = pair % 4, pair // 4
                    if pair % 4 == 0:
                        pe.wait_ge(exp_done, i * (2 * KT) + (2 * t + r + 1))
                    last = nc.tensor.matmul(pvps[32 * g:32 * g + PV_W, r * P:(r + 1) * P], v[p][0:n, t, pair, :],
                                            probs[(t + p) % 2][0:n, pair * P:(pair + 1) * P],
                                            start=(t == 0 and r == 0), stop=(t == KT - 1), skip_group_check=True)
                last.then_inc(pv_done, 1)

            def o_back(b):
                pe.wait_ge(oT_copied, b + 1)
                for r in range(2):
                    last = nc.tensor.transpose(misc[:, r * P:(r + 1) * P], oT[:, r * P:(r + 1) * P], ident[:, :])
                last.then_inc(oT_back, 1)

            pe.wait_ge(w_in, 48)
            for j in range(2):
                k_proj(0, 0, j, 0, (misc, pvps)[j % 2])
            query.tensor(pe)
            for j in range(2, NCH):
                pe.wait_ge(k_evac, j - 1)
                k_proj(0, 0, j, 0, (misc, pvps)[j % 2])
            pe.wait_ge(k_evac, 3)
            v_proj(0, 0, 0)
            evacuated(pe, "v", 0, 0)
            v_proj(0, 1, 0)
            query.count_true(pe)
            with pe.If(query.all_true(pe)):
                pe.wait_ge(cst, 3)
                for s in sum(EARLY_STEPS.values(), []):
                    max_step(0, s, 0, 0)
                pe.wait_ge(ones_in, 2)

                def body(i, r, p, known):
                    for t in range(KT):
                        if known != -1:
                            scores(i, t, p, known)
                        if t > 0 and known != -1:
                            p_v(i, t - 1, p, known)
                        elif t == 0 and (known is None or known > 0):
                            p_v(i - 1, KT - 1, 1 - p, None)
                        if t in MISC and wanted(*MISC[t][0:2], known):
                            kind, stage, num = MISC[t]
                            pk, pst, pn = previous_use(t, known)
                            evacuated(pe, pk, i + pst, pn)
                            if kind == "k":
                                k_proj(i + 2, r + 1, num, p)
                            elif kind == "v":
                                v_proj(i + stage, num, (p + stage) % 2)
                            elif kind == "o":
                                o_back(i - 1)
                            else:
                                m_rows(i + 1, num)
                        if known is None or known + 1 < NB:
                            for s in MAX_STEPS.get(t, ()):
                                max_step(i + 1, s, 1 - p, None)
                        if known is None or known + 2 < NB:
                            for s in EARLY_STEPS.get(t, ()):
                                max_step(i + 2, s, p, None)

                iterations(pe, body)
                p_v(NB - 1, KT - 1, 1, None)
                o_back(NB - 1)
            with pe.Else():
                def body(b, r, half, known):
                    prev = ("v", 0, 1) if known == 0 else ("o", b - 1, 0)
                    work = [("k", j) for j in range(NCH)] + [("v", g) for g in range(4)]
                    for kind, n in work[NCH + 2:] if known == 0 else work:
                        evacuated(pe, *prev)
                        if kind == "k":
                            k_proj(b, b, n, 0)
                        else:
                            v_proj(b, n, 0)
                        prev = (kind, b, n)
                    pe.wait_ge(ones_in, 2)
                    pe.wait_ge(cst, 3)
                    for s in range(16):
                        max_step(b, s, 0, known)
                    evacuated(pe, *prev)
                    m_rows(b, 0)
                    evacuated(pe, "m", b, 0)
                    m_rows(b, 1)
                    evacuated(pe, "m", b, 1)
                    for h in range(2):
                        if h:
                            pe.wait_ge(fill_evac, b * 2 + 1)
                        nc.tensor.matmul(misc[:, :], kst[0][ROWS:ROWS + MROWS, 0, 0:P],
                                         qsc[0][ROWS:ROWS + MROWS, h * 512:h * 512 + 512],
                                         start=True, stop=True).then_inc(fill_done, 1)
                    for t in range(KT):
                        scores(b, t, 0, known)
                        p_v(b, t, 0, known)
                    pe.wait_ge(fill_evac, b * 2 + 2)
                    o_back(b)

                batches(pe, body)

        block = ctx.enter_context(nc.Block())

        @block.sync
        def _(sp):
            sync_program(sp)

        @block.gpsimd
        def _(pool):
            pool_program(pool)

        @block.scalar
        def _(act):
            scalar_program(act)

        @block.vector
        def _(dve):
            vector_program(dve)

        @block.tensor
        def _(pe):
            tensor_program(pe)


def self_attention(nc, w, keep, load_expert):
    (x_sb, att, xn1, xn3T, logit, ident, late_in) = keep
    NG, GT = 4, 4
    QK, VV = 3 * D, 2 * D
    G8 = QK // DH
    with ExitStack() as ctx:
        sb = lambda n, s: ctx.enter_context(nc.sbuf_tensor(n, s, F32))
        psb = lambda n: ctx.enter_context(nc.psum_tensor(n, [P, 512], F32))
        sem = lambda n: ctx.enter_context(nc.semaphore(n))
        attT, xnT = sb("attT", [P, TOK]), sb("xnT1", [P, TOK])
        y, v_raw = sb("y", [P, NT, QK]), [sb(f"v_raw{i}", [P, VV]) for i in range(4)]
        vv = sb("vv", [P, NT, 2, 2, D])
        th, sq = sb("th", [P, NT, QK]), sb("sq", [P, 2, GT, QK])
        ss, nrm = sb("ss", [P, NT, G8]), sb("nrm", [P, NT, G8])
        st = sb("st", [P, 2, 2 * D])
        state = sb("state", [P, NT, 2 * D])
        qT = sb("qT", [P, TOK])
        on, onT = xn1, attT
        stats, mv = sb("stats1", [P, 3, NT, 6]), sb("mv1", [P, 3, NT, 2])
        rstd, epsv, minus_half = sb("rstd1", [P, 3, NT]), sb("epsv", [P, GT]), sb("minus_half", [P, GT])
        wsum = sb("wsum", [P, 5 * D])
        psT = [psb(f"psT{i}") for i in range(2)]
        psM = [psb(f"psM{i}") for i in range(2)]
        psQ, psV = psb("psQ"), psb("psV")
        psG = [psb(f"psG{i}") for i in range(2)]
        t_done, t_evac = sem("t_done"), sem("t_evac")
        m_done, m_evac = sem("m_done"), sem("m_evac")
        p_done, y_done, v_copied, v_done = sem("p_done"), sem("y_done"), sem("v_copied"), sem("vv_done")
        stat_done, var_done, rstd_done = sem("stat1"), sem("var1"), sem("rstd1_done")
        eps_add = sem("eps_add")
        n_done, cst, x1b_done, wsum_done = sem("n_done"), sem("cst2"), sem("x1b_done"), sem("wsum_done")
        th_done, w_done, sq_done, ss_done, root_done, nrm_add, inv_done, k_ready = (
            sem("th_done"), sem("w_done"), sem("sq_done"), sem("ss_done"), sem("root_done"), sem("nrm_add"),
            sem("inv_done"), sem("k_ready"))
        g_done, st1, state_done = sem("g_done"), sem("st1"), sem("state_done")
        gate_done, logit_done = sem("gate_done"), sem("logit_done")
        block = ctx.enter_context(nc.Block())
        q_of = lambda t: (psQ, psG[0])[t % 2]
        v_of = lambda t: (psV, psG[1])[t % 2]
        g_of = lambda t: (psG[0], psG[1], psQ, psV)[t % 4]
        o_of = lambda g: (psM[0], psM[1], psG[0], psG[1])[g]
        cols = lambda t: slice(t * P, (t + 1) * P)
        tiles = lambda g: range(GT * g, GT * g + GT)
        grp = lambda g: slice(GT * g, GT * g + GT)

        @block.sync
        def _(sp):
            for p in range(2):
                load_expert(sp, p, p)

        @block.gpsimd
        def _(pool):
            pool.memset(epsv[:, :], EPS).then_inc(cst, 1)
            pool.memset(minus_half[:, :], -0.5).then_inc(cst, 1)
            pool.memset(vv[:, :, :, :, :].rearrange("p t k b d -> p (t k b d)"), 0.0).then_inc(cst, 1)
            pool.wait_ge(late_in, LATE)
            pool.wait_ge(cst, 3)

            def rstds(rnd):
                for g in range(NG):
                    n = rnd * NG + g
                    pool.wait_ge(var_done, (n + 1) * GT)
                    nc.gpsimd.tensor_tensor(rstd[:, rnd, grp(g)], mv[:, rnd, grp(g), 1], epsv[:, :], ALU.add)\
                        .then_inc(eps_add, 1)
                    pool.wait_ge(eps_add, n + 1)
                    nc.gpsimd.tensor_tensor(rstd[:, rnd, grp(g)], rstd[:, rnd, grp(g)], minus_half[:, :], ALU.pow)\
                        .then_inc(rstd_done, 1)

            rstds(0)
            pool.wait_ge(rstd_done, NG)
            for t in range(NT):
                pool.wait_ge(v_copied, t + 1)
                for b in range(2):
                    rows = slice(64 * b, 64 * b + 64)
                    nc.gpsimd.tensor_tensor(
                        vv[rows, t, :, b, :], v_raw[t % 4][rows, :].rearrange("p (k d) -> p k d", k=2),
                        w["b5"][rows, QK:QK + VV].rearrange("p (k d) -> p k d", k=2), ALU.add).then_inc(v_done, 1)
            pool.wait_ge(v_done, 2 * NT)
            for g in range(NG):
                pool.wait_ge(n_done, g + 1)
                for t in tiles(g):
                    last = nc.gpsimd.tensor_tensor(x_sb[:, t, :], x_sb[:, t, :], w["a_bo"][:, :], ALU.add)
                last.then_inc(x1b_done, 1)
            rstds(1)
            rstds(2)

        @block.scalar
        def _(act):
            act.wait_ge(late_in, LATE)

            def out_of_psT(n, dst, scale=None, bias=None):
                act.wait_ge(t_done, n + 1)
                if bias is None:
                    nc.scalar.activation(dst, psT[n % 2][:, :], ACT.Copy).then_inc(t_evac, 1)
                elif scale is None:
                    nc.scalar.activation(dst, psT[n % 2][:, :], ACT.Identity, bias=bias).then_inc(t_evac, 1)
                else:
                    nc.scalar.activation(dst, psT[n % 2][:, :], ACT.Identity, bias=bias, scale=scale).then_inc(t_evac, 1)

            part = lambda a, g: a[:, 512 * g:512 * g + 512]
            for g in range(NG):
                out_of_psT(g, part(attT, g), bias=w["x_bv"][:, 0:1])
            for g in range(2):
                out_of_psT(NG + g, part(xnT, g))
            def square(g):
                act.wait_ge(w_done, g + 1)
                if g >= 2:
                    act.wait_ge(ss_done, g - 1)
                nc.scalar.activation(sq[:, g % 2, :, :], y[:, grp(g), :], ACT.Square, bias=1.0).then_inc(sq_done, 1)

            for g in range(NG):
                for t in tiles(g):
                    act.wait_ge(p_done, t + 1)
                    if t >= 4:
                        act.wait_ge(v_done, 2 * t - 6)
                    nc.scalar.activation(v_raw[t % 4][:, :], v_of(t)[:, 0:VV], ACT.Copy).then_inc(v_copied, 1)
                act.wait_ge(y_done, (g + 1) * GT)
                nc.scalar.activation(th[:, grp(g), :], y[:, grp(g), :], ACT.Tanh, scale=0.5).then_inc(th_done, 1)
                if g:
                    square(g - 1)
                if g + 2 < NG:
                    out_of_psT(NG + g + 2, part(xnT, g + 2))
            square(NG - 1)
            for g in range(NG):
                act.wait_ge(ss_done, g + 1)
                nc.scalar.activation(nrm[:, grp(g), :], ss[:, grp(g), :], ACT.Sqrt).then_inc(root_done, 1)
            for g in range(NG):
                out_of_psT(2 * NG + g, part(qT, g))
            for g in range(NG):
                out_of_psT(3 * NG + g, part(onT, g), scale=w["ln_g"][:, 0:1], bias=w["ln_b"][:, 0:1])
            for g in range(NG):
                out_of_psT(4 * NG + g, part(xn3T, g))

        @block.vector
        def _(dve):
            dve.wait_ge(late_in, LATE)
            for j in range(5):
                last = nc.vector.tensor_tensor(wsum[:, cols(j)], w["w5"][:, cols(j)], ident[:, :], ALU.add)
            last.then_inc(wsum_done, 1)

            def statistics(rnd, g, src):
                n = rnd * NG + g
                for t in tiles(g):
                    nc.vector.bn_stats(stats[:, rnd, t, :], src(t)).then_inc(stat_done, 1)
                dve.wait_ge(stat_done, (n + 1) * GT)
                for t in tiles(g):
                    nc.vector.bn_aggr(mv[:, rnd, t, :], stats[:, rnd, t, :]).then_inc(var_done, 1)

            def normalise(rnd, g, src, dst):
                n = rnd * NG + g
                dve.wait_ge(rstd_done, n + 1)
                for t in tiles(g):
                    last = nc.vector.tensor_scalar(dst[:, t, :], src(t), mv[:, rnd, t, 0:1], rstd[:, rnd, t:t + 1],
                                                   ALU.subtract, ALU.mult)
                last.then_inc(n_done, 1)

            for g in range(NG):
                dve.wait_ge(m_done, g + 1)
                nc.vector.tensor_tensor(x_sb[:, grp(g), :], psM[g % 2][:, :].rearrange("p (t d) -> p t d", d=D),
                                        x_sb[:, grp(g), :], ALU.add).then_inc(m_evac, 1)
                dve.wait_ge(m_evac, g + 1)
                statistics(0, g, lambda t: x_sb[:, t, :])
                if g:
                    normalise(0, g - 1, lambda t: x_sb[:, t, :], xn1)
            normalise(0, NG - 1, lambda t: x_sb[:, t, :], xn1)
            def biases(g):
                for t in tiles(g):
                    dve.wait_ge(p_done, t + 1)
                    nc.vector.tensor_tensor(y[:, t, :], q_of(t)[:, 0:QK], w["b5"][:, 0:QK], ALU.add).then_inc(y_done, 1)

            def silu(g):
                dve.wait_ge(th_done, g + 1)
                nc.vector.scalar_tensor_tensor(out=y[:, grp(g), :], in0=th[:, grp(g), :], scalar=1.0,
                                               in1=y[:, grp(g), :], op0=ALU.add, op1=ALU.mult).then_inc(w_done, 1)

            def sum_squares(g):
                dve.wait_ge(sq_done, g + 1)
                nc.vector.tensor_reduce(ss[:, grp(g), :].rearrange("p t h -> p (t h)"),
                                        sq[:, g % 2, :, :].rearrange("p t (h d) -> p (t h) d", d=DH), AX.X, ALU.add)\
                    .then_inc(ss_done, 1)

            for g in range(NG + 2):
                if g < NG:
                    biases(g)
                if 1 <= g < NG + 1:
                    silu(g - 1)
                if g >= 2:
                    sum_squares(g - 2)
            for g in range(NG):
                dve.wait_ge(root_done, g + 1)
                flat = nrm[:, grp(g), :].rearrange("p t h -> p (t h)")
                nc.vector.tensor_scalar(flat, flat, 2e-6, None, ALU.add).then_inc(nrm_add, 1)

            def invert(g):
                dve.wait_ge(nrm_add, g + 1)
                flat = nrm[:, grp(g), :].rearrange("p t h -> p (t h)")
                nc.vector.reciprocal(flat, flat).then_inc(inv_done, 1)

            def by_norms(g):
                dve.wait_ge(inv_done, g + 1)
                heads = y[:, grp(g), :].rearrange("p t (h d) -> p (t h) d", d=DH)
                flat = nrm[:, grp(g), :].rearrange("p t h -> p (t h)")
                nc.vector.scalar_tensor_tensor(
                    out=heads, in0=heads, scalar=1.0, in1=flat.unsqueeze(2).to_broadcast([P, GT * G8, DH]),
                    op0=ALU.add, op1=ALU.mult).then_inc(k_ready, 1)

            def states(g):
                for t in tiles(g):
                    dve.wait_ge(g_done, t + 1)
                    if t >= 2:
                        dve.wait_ge(state_done, t - 1)
                    nc.vector.tensor_tensor(
                        st[:, t % 2, :].rearrange("p (b d) -> p b d", b=2),
                        g_of(t)[:, 0:2 * D].rearrange("p (b d) -> p b d", b=2),
                        w["blocks"][:, :].unsqueeze(1).to_broadcast([P, 2, D]), ALU.mult).then_inc(st1, 1)
                    dve.wait_ge(st1, t + 1)
                    nc.vector.tensor_tensor(state[:, t, :], g_of(t)[:, 2 * D:4 * D], st[:, t % 2, :], ALU.mult)\
                        .then_inc(state_done, 1)

            invert(0)
            for g in range(NG + 1):
                if g + 1 < NG:
                    invert(g + 1)
                if g < NG:
                    by_norms(g)
                if g:
                    states(g - 1)
            for g in range(NG):
                dve.wait_ge(m_done, NG + g + 1)
                statistics(1, g, lambda t: o_of(g)[:, cols(t % GT)])
                if g:
                    normalise(1, g - 1, lambda t: o_of(g - 1)[:, cols(t % GT)], on)
            normalise(1, NG - 1, lambda t: o_of(NG - 1)[:, cols(t % GT)], on)
            dve.wait_ge(t_done, 4 * NG)
            for g in range(NG):
                dve.wait_ge(m_done, 2 * NG + g + 1)
                dve.wait_ge(x1b_done, g + 1)
                nc.vector.tensor_tensor(x_sb[:, grp(g), :], psM[g % 2][:, :].rearrange("p (t d) -> p t d", d=D),
                                        x_sb[:, grp(g), :], ALU.add).then_inc(m_evac, 1)
                dve.wait_ge(m_evac, NG + g + 1)
                statistics(2, g, lambda t: x_sb[:, t, :])
                if g:
                    normalise(2, g - 1, lambda t: x_sb[:, t, :], on)
            normalise(2, NG - 1, lambda t: x_sb[:, t, :], on)
            dve.wait_ge(gate_done, NG)
            nc.vector.tensor_tensor(
                logit[:, :, :], psQ[:, 0:NT * E].rearrange("p (t e) -> p t e", e=E),
                w["ebias"][:, :].unsqueeze(1).to_broadcast([P, NT, E]), ALU.add).then_inc(logit_done, 1)
            dve.wait_ge(logit_done, 1)

        @block.tensor
        def _(pe):
            pe.wait_ge(late_in, LATE)

            def into_psT(n, src, g):
                if n >= 2:
                    pe.wait_ge(t_evac, n - 1)
                for t in tiles(g):
                    last = nc.tensor.transpose(psT[n % 2][:, cols(t % GT)], src(t), ident[:, :])
                last.then_inc(t_done, 1)

            def into_psM(read_out, lhsT, rhs, g, ready):
                if g >= 2:
                    pe.wait_ge(m_evac, read_out + g - 1)
                pe.wait_ge(t_evac, ready)
                for t in tiles(g):
                    last = nc.tensor.matmul(psM[g % 2][:, cols(t % GT)], lhsT[:, cols(t)], rhs, start=True, stop=True)
                last.then_inc(m_done, 1)

            for g in range(NG):
                into_psT(g, lambda t: att[:, cols(t)], g)
                if g:
                    into_psM(0, attT, w["x_wo"][:, :], g - 1, g)
            into_psM(0, attT, w["x_wo"][:, :], NG - 1, NG)
            def project(g):
                for t in tiles(g):
                    pe.wait_ge(t_evac, NG + g + 1)
                    if t >= 2:
                        pe.wait_ge(y_done, t - 1)
                    nc.tensor.matmul(q_of(t)[:, 0:QK], xnT[:, cols(t)], wsum[:, 0:QK], start=True, stop=True)
                    if t >= 2:
                        pe.wait_ge(v_copied, t - 1)
                    nc.tensor.matmul(v_of(t)[:, 0:VV], xnT[:, cols(t)], wsum[:, QK:QK + VV], start=True, stop=True)\
                        .then_inc(p_done, 1)

            pe.wait_ge(wsum_done, 1)
            for g in range(NG):
                pe.wait_ge(n_done, g + 1)
                into_psT(NG + g, lambda t: xn1[:, t, :], g)
                if g:
                    project(g - 1)
            project(NG - 1)
            for g in range(NG):
                pe.wait_ge(k_ready, g + 1)
                into_psT(2 * NG + g, lambda t: y[:, t, 0:D], g)
                for t in tiles(g):
                    pe.wait_ge(v_done, 2 * t + 2)
                    if t >= 4:
                        pe.wait_ge(state_done, t - 3)
                    for k in range(2):
                        last = nc.tensor.matmul(g_of(t)[:, k * 2 * D:(k + 1) * 2 * D], y[:, t, (1 + k) * D:(2 + k) * D],
                                                vv[:, t, k, :, :].rearrange("p b d -> p (b d)"), start=True, stop=True)
                    last.then_inc(g_done, 1)
            for g in range(NG):
                pe.wait_ge(t_evac, 2 * NG + g + 1)
                pe.wait_ge(state_done, min(NT, GT * (g + 1) + 2))
                if g < 2:
                    pe.wait_ge(m_evac, NG + g - 1)
                for t in tiles(g):
                    for b in range(2):
                        last = nc.tensor.matmul(o_of(g)[64 * b:64 * b + 64, cols(t % GT)],
                                                qT[:, t * P + 64 * b:t * P + 64 * b + 64], state[:, t, b * D:(b + 1) * D],
                                                start=True, stop=True)
                last.then_inc(m_done, 1)
            for g in range(NG):
                pe.wait_ge(n_done, NG + g + 1)
                into_psT(3 * NG + g, lambda t: on[:, t, :], g)
            for g in range(NG):
                into_psM(NG, onT, w["a_wo"][:, :], g, 3 * NG + g + 1)
            def gate(g):
                pe.wait_ge(t_evac, 4 * NG + g + 1)
                pe.wait_ge(state_done, NT)
                for t in tiles(g):
                    last = nc.tensor.matmul(psQ[:, t * E:(t + 1) * E], xn3T[:, cols(t)], w["gate"][:, :],
                                            start=True, stop=True)
                last.then_inc(gate_done, 1)

            for g in range(NG):
                pe.wait_ge(n_done, 2 * NG + g + 1)
                into_psT(4 * NG + g, lambda t: on[:, t, :], g)
                if g:
                    gate(g - 1)
            gate(NG - 1)


def experts(nc, keep, load_expert, out_d):
    (x_sb, xn3, xn3T, logit, before, wup, wdn, up_in) = keep
    TB = TOK // 512
    with ExitStack() as ctx:
        sb = lambda n, s: ctx.enter_context(nc.sbuf_tensor(n, s, F32))
        psb = lambda n: ctx.enter_context(nc.psum_tensor(n, [P, 512], F32))
        sem = lambda n: ctx.enter_context(nc.semaphore(n))
        hT = [sb(f"hT{i}", [P, IC, 512]) for i in range(2)]
        acc = sb("acc", [P, NT, D])
        ex, pr = sb("ex", [P, NT, E]), sb("pr", [P, NT, E])
        top, tot, rtot = sb("top", [P, NT]), sb("tot", [P, NT]), sb("rtot", [P, NT])
        above, ties, rank = sb("above", [P, NT, E, E]), sb("ties", [P, NT, E, E]), sb("rank", [P, NT, E])
        kept, tot2, sw = sb("kept", [P, NT, E]), sb("tot2", [P, NT]), sb("sw", [P, NT * E])
        swe = [sb(f"swe{i}", [P, NT]) for i in range(2)]
        stats, mv = sb("stats3", [P, NT, 6]), sb("mv3", [P, NT, 2])
        rstd, epsv, minus_half = sb("rstd3", [P, NT]), sb("epsv3", [P, 4]), sb("minus_half3", [P, 4])
        ps_up = [psb(f"ps_up{i}") for i in range(4)]
        ps_dn = [psb(f"ps_dn{i}") for i in range(2)]
        exp_done, chain, swe_done = sem("gexp_done"), sem("gate_chain"), sem("swe_done")
        up_done, gelu_done, dn_done, acc_done = sem("up_done"), sem("gelu_done"), sem("dn_done"), sem("acc_done")
        acc_zero, res_done = sem("acc_zero"), sem("res_done")
        sub_done, cst, eps_add, rstd_done = sem("sub_done"), sem("cst3"), sem("eps_add3"), sem("rstd3_done")
        stat_done, var_done, n_done, y_done, stored = sem("stat3"), sem("var3"), sem("n3"), sem("y3"), sem("stored")
        block = ctx.enter_context(nc.Block())

        def pairs(eng, body, last_apart=False):
            for p in range(2):
                body(p, 0, p, p)
            with eng.Fori(1, E // 2 - last_apart) as r:
                for p in range(2):
                    body(r * 2 + p, r, p, None)
            if last_apart:
                for p in range(2):
                    body(E - 2 + p, E // 2 - 1, p, E - 2 + p)

        @block.sync
        def _(sp):
            def body(e, r, p, known):
                if known is None:
                    sp.wait_ge(dn_done, e * TB - TB)
                    load_expert(sp, e, p)

            pairs(sp, body)
            out_v = out_d.rearrange("(t p) d -> p t d", p=P)
            for g in range(4):
                sp.wait_ge(y_done, g + 1)
                sp.dma_start(out_v[:, 4 * g:4 * g + 4, :], acc[:, 4 * g:4 * g + 4, :]).then_inc(stored, 16)
            sp.wait_ge(stored, 64)

        @block.scalar
        def _(act):
            act.wait_ge(sub_done, 1)
            nc.scalar.activation(ex[:, :, :], logit[:, :, :], ACT.Exp).then_inc(exp_done, 1)

            def body(e, r, p, known):
                for tb in range(TB):
                    for c in range(IC):
                        act.wait_ge(up_done, e * (TB * IC) + (tb * IC + c + 1))
                        if c == 0 and not (known == 0 and tb < 2):
                            act.wait_ge(dn_done, e * TB + (tb - 1))
                        nc.scalar.activation(hT[tb % 2][:, c, :], ps_up[c][:, :], ACT.Gelu).then_inc(gelu_done, 1)

            pairs(act, body)

        @block.gpsimd
        def _(pool):
            nc.gpsimd.tensor_tensor(x_sb[:, :, :], x_sb[:, :, :], xn3[:, :, :], ALU.add).then_inc(res_done, 1)
            pool.memset(epsv[:, :], EPS).then_inc(cst, 1)
            pool.memset(minus_half[:, :], -0.5).then_inc(cst, 1)
            pool.wait_ge(cst, 2)
            for g in range(4):
                pool.wait_ge(var_done, 4 * (g + 1))
                s = slice(4 * g, 4 * g + 4)
                nc.gpsimd.tensor_tensor(rstd[:, s], mv[:, s, 1], epsv[:, :], ALU.add).then_inc(eps_add, 1)
                pool.wait_ge(eps_add, g + 1)
                nc.gpsimd.tensor_tensor(rstd[:, s], rstd[:, s], minus_half[:, :], ALU.pow).then_inc(rstd_done, 1)

        @block.vector
        def _(dve):
            steps = [0]

            def then_wait(ins):
                steps[0] += 1
                ins.then_inc(chain, 1)
                dve.wait_ge(chain, steps[0])

            by_e = lambda a: a[:, :].unsqueeze(2).to_broadcast([P, NT, E])
            nc.vector.memset(acc[:, :, :], 0.0).then_inc(acc_zero, 1)
            then_wait(nc.vector.tensor_reduce(top[:, :], logit[:, :, :], AX.X, ALU.max))
            nc.vector.tensor_tensor(logit[:, :, :], logit[:, :, :], by_e(top), ALU.subtract).then_inc(sub_done, 1)
            dve.wait_ge(exp_done, 1)
            then_wait(nc.vector.tensor_reduce(tot[:, :], ex[:, :, :], AX.X, ALU.add))
            then_wait(nc.vector.reciprocal(rtot[:, :], tot[:, :]))
            then_wait(nc.vector.tensor_tensor(pr[:, :, :], ex[:, :, :], by_e(rtot), ALU.mult))
            of_j = pr[:, :, :].unsqueeze(2).to_broadcast([P, NT, E, E])
            of_e = pr[:, :, :].unsqueeze(3).to_broadcast([P, NT, E, E])
            nc.vector.tensor_tensor(above[:, :, :, :], of_j, of_e, ALU.is_gt)
            then_wait(nc.vector.tensor_tensor(ties[:, :, :, :], of_j, of_e, ALU.is_equal))
            then_wait(nc.vector.tensor_tensor(ties[:, :, :, :].rearrange("p t e j -> p t (e j)"),
                                              ties[:, :, :, :].rearrange("p t e j -> p t (e j)"),
                                              before[:, :].unsqueeze(1).to_broadcast([P, NT, E * E]), ALU.mult))
            then_wait(nc.vector.tensor_tensor(above[:, :, :, :], above[:, :, :, :], ties[:, :, :, :], ALU.add))
            then_wait(nc.vector.tensor_reduce(rank[:, :, :], above[:, :, :, :], AX.X, ALU.add))
            then_wait(nc.vector.scalar_tensor_tensor(out=kept[:, :, :], in0=rank[:, :, :], scalar=2.0,
                                                     in1=pr[:, :, :], op0=ALU.is_lt, op1=ALU.mult))
            then_wait(nc.vector.tensor_reduce(tot2[:, :], kept[:, :, :], AX.X, ALU.add))
            then_wait(nc.vector.tensor_scalar(tot2[:, :], tot2[:, :], 1e-6, None, ALU.add))
            then_wait(nc.vector.reciprocal(tot2[:, :], tot2[:, :]))
            then_wait(nc.vector.tensor_tensor(sw[:, :].rearrange("p (e t) -> p t e", e=E), kept[:, :, :],
                                              by_e(tot2), ALU.mult))
            dve.wait_ge(acc_zero, 1)

            def body(e, r, p, known):
                if not (known is not None and known < 2):
                    dve.wait_ge(acc_done, e * TB - TB)
                nc.vector.tensor_copy(swe[p][:, :], sw[:, bass.ds(e * NT, NT)]).then_inc(swe_done, 1)
                dve.wait_ge(swe_done, e + 1)
                for tb in range(TB):
                    dve.wait_ge(dn_done, e * TB + (tb + 1))
                    if not (known == 0):
                        dve.wait_ge(acc_done, e * TB + (tb + 1 - TB))
                    for j in range(4):
                        t = 4 * tb + j
                        last = nc.vector.scalar_tensor_tensor(
                            out=acc[:, t, :], in0=ps_dn[tb % 2][:, j * P:(j + 1) * P], scalar=swe[p][:, t:t + 1],
                            in1=acc[:, t, :], op0=ALU.mult, op1=ALU.add)
                    last.then_inc(acc_done, 1)
                    if known == E - 1:
                        dve.wait_ge(acc_done, e * TB + (tb + 1))
                        for t in range(4 * tb, 4 * tb + 4):
                            nc.vector.bn_stats(stats[:, t, :], acc[:, t, :]).then_inc(stat_done, 1)
                        dve.wait_ge(stat_done, 4 * tb + 4)
                        for t in range(4 * tb, 4 * tb + 4):
                            nc.vector.bn_aggr(mv[:, t, :], stats[:, t, :]).then_inc(var_done, 1)
                        if tb:
                            finish(tb - 1)

            def finish(g):
                dve.wait_ge(rstd_done, g + 1)
                for t in range(4 * g, 4 * g + 4):
                    last = nc.vector.tensor_scalar(acc[:, t, :], acc[:, t, :], mv[:, t, 0:1], rstd[:, t:t + 1],
                                                   ALU.subtract, ALU.mult)
                last.then_inc(n_done, 1)
                dve.wait_ge(n_done, g + 1)
                s = slice(4 * g, 4 * g + 4)
                dve.wait_ge(res_done, 1)
                nc.vector.tensor_tensor(acc[:, s, :], acc[:, s, :], x_sb[:, s, :], ALU.add).then_inc(y_done, 1)

            pairs(dve, body, last_apart=True)
            finish(3)

        @block.tensor
        def _(pe):
            def down(e, tb, p, first):
                pe.wait_ge(gelu_done, e * (TB * IC) + (tb + 1) * IC)
                if not first:
                    pe.wait_ge(acc_done, e * TB + (tb - 1))
                for j in range(4):
                    for c in range(IC):
                        last = nc.tensor.matmul(ps_dn[tb % 2][:, j * P:(j + 1) * P], hT[tb % 2][:, c, j * P:(j + 1) * P],
                                                wdn[p][:, c, :], start=(c == 0), stop=(c == IC - 1))
                last.then_inc(dn_done, 1)

            def body(e, r, p, known):
                for tb in range(TB):
                    if tb == 0:
                        pe.wait_ge(up_in[p], r * 32 + 32)
                    for c in range(IC):
                        if not (known == 0 and tb == 0):
                            pe.wait_ge(gelu_done, e * (TB * IC) + ((tb - 1) * IC + c + 1))
                        nc.tensor.matmul(ps_up[c][:, :], wup[p][:, c * P:(c + 1) * P], xn3T[:, 512 * tb:512 * tb + 512],
                                         start=True, stop=True).then_inc(up_done, 1)
                    if tb:
                        down(e, tb - 1, p, known == 0 and tb - 1 < 2)
                    elif known != 0:
                        down(e - 1, TB - 1, 1 - p, False)

            pairs(pe, body)
            down(E - 1, TB - 1, 1, False)


def build(nc, a, out_d):
    with ExitStack() as ctx:
        sb = lambda n, s, d: ctx.enter_context(nc.sbuf_tensor(n, s, d))
        x_sb = sb("x_sb", [P, NT, D], F32)
        ident = sb("ident", [P, P], F32)
        att = sb("att", [P, NT * D], F32)
        keep = {
            "x_sb": x_sb, "ident": ident, "att": att,
            "ident_b": sb("ident_b", [P, P], BF16), "ones_f": sb("ones_f", [P, P], F32), "flag_i": sb("flag_i", [1, 1], I32),
            "q_scr": nc.dram_tensor("q_scr", (2, NSLOT, DH, NPAIR, TOK), BF16, kind="Internal").ap(),
            "k_scr": nc.dram_tensor("k_scr", (2, 3, DH, NPAIR, SK), BF16, kind="Internal").ap()}
        late_in = ctx.enter_context(nc.semaphore("late_in"))
        w = {n: sb("w_" + n, shape, F32) for n, shape, _ in LATE_WEIGHTS}
        cross_attention(nc, keep, a, w, late_in)
        xn3T = sb("xn3T", [P, TOK], F32)
        xn1 = sb("xn1", [P, NT, D], F32)
        logit = sb("logit", [P, NT, E], F32)
        wup = [sb(f"wup{i}", [P, I], F32) for i in range(2)]
        wdn = [sb(f"wdn{i}", [P, IC, D], F32) for i in range(2)]
        up_in = [ctx.enter_context(nc.semaphore(f"up_in{i}")) for i in range(2)]

        def load_expert(sp, e, p):
            sp.dma_start(wup[p][:, :], a["w_up"][e]).then_inc(up_in[p], 16)
            sp.dma_start(wdn[p][:, :, :], a["w_dn"][e].rearrange("(c p) h -> p c h", p=P)).then_inc(up_in[p], 16)

        self_attention(nc, w, (x_sb, att, xn1, xn3T, logit, ident, late_in), load_expert)
        experts(nc, (x_sb, xn1, xn3T, logit, w["before"], wup, wdn, up_in), load_expert, out_d)


def kernel(**inputs):
    import numpy as np
    import concourse.bacc as bacc
    from concourse.bass_utils import run_bass_kernel_spmd

    n = {k: np.asarray(v) for k, v in inputs.items()}
    mask = n["mask_BxSxS2_bf1"].view(np.uint8)
    by_pair = lambda w: w.reshape(NPAIR, 2, DH, -1).transpose(1, 2, 0, 3).reshape(D, -1)
    row, col = (lambda v: v.reshape(1, -1)), (lambda v: v.reshape(-1, 1))
    wk, bk, wv, bv = (n["L0_attn_" + s] for s in ("Wk", "bk", "Wv", "bv"))
    host = {
        "x": n["x"].reshape(TOK, D),
        "ctxT": n["ctx_1024"].transpose(0, 2, 1),
        "mask": mask,
        "maskT": mask.transpose(0, 2, 1),
        "ident": np.eye(P, dtype=np.float32),
        "x_wq": by_pair(n["L0_xattn_Wq"]).T, "x_bq": by_pair(n["L0_xattn_bq"])[:, 0],
        "x_wk": by_pair(n["L0_xattn_Wk"]).T, "x_bk": by_pair(n["L0_xattn_bk"])[:, 0],
        "x_wv": n["L0_xattn_Wv"].T,
        "x_bv": col(n["L0_xattn_bv"]), "x_wo": n["L0_xattn_Wo"].T, "x_bo": row(n["L0_xattn_bo"]),
        "w5": np.concatenate([n["L0_attn_Wq"].T, wk[0].T, wk[1].T, wv[0].T, wv[1].T], axis=1),
        "b5": row(np.concatenate([n["L0_attn_bq"], bk[0], bk[1], bv[0], bv[1]])),
        "blocks": (np.kron(np.eye(NH), np.ones((DH, DH))) * SQ ** -2.0).astype(np.float32),
        "ln_g": col(n["L0_attn_ln_g"]), "ln_b": col(n["L0_attn_ln_b"]),
        "a_wo": n["L0_attn_Wo"].T, "a_bo": row(n["L0_attn_bo"]),
        "gate": n["L0_ffn_gate_w"].T, "ebias": row(n["L0_ffn_expert_bias"]),
        "before": row(np.tril(np.ones((E, E), np.float32), -1)),
        "w_up": n["L0_ffn_w_up"].transpose(0, 2, 1), "w_dn": n["L0_ffn_w_down"].transpose(0, 2, 1),
    }
    nc = bacc.Bacc("TRN2", target_bir_lowering=False, num_devices=1)
    arrays, aps = {}, {}
    for name, arr in host.items():
        arr = np.ascontiguousarray(arr)
        arrays[f"in_{name}"] = arr
        aps[name] = nc.dram_tensor(f"in_{name}", arr.shape, mybir.dt.from_np(arr.dtype), kind="ExternalInput").ap()
    out = nc.dram_tensor("out", (TOK, D), F32, kind="ExternalOutput").ap()
    build(nc, aps, out)
    r = run_bass_kernel_spmd(nc, [arrays], core_ids=[0])
    return r.results[0]["out"].reshape(NB, SQ, D)
```
